# Optimizing a Trainium2 kernel written in Bass

```python
import numpy as np
import jax
import jax.numpy as jnp

def _softmax(x, axis=-1):
    return jax.nn.softmax(x, axis=axis)

def _gelu(x):
    return jax.nn.gelu(x, approximate=True)

def _silu(x):
    return jax.nn.silu(x)

def _sigmoid(x):
    return jax.nn.sigmoid(x)

def _layernorm(x, axis=-1, eps=1e-05):
    m = jnp.mean(x, axis=axis, keepdims=True)
    v = jnp.var(x, axis=axis, keepdims=True)
    return (x - m) / jnp.sqrt(v + eps)

def _scatter_add(tgt, idx, src, axis=0):
    return tgt.at[idx].add(src)

def _segment_sum(src, seg, n):
    return jax.ops.segment_sum(src, seg, n)
kernel_name = 'mk_flamingo_gated_d1_seqx_r8_7cd998'

def setup_inputs(seed: int=0):
    np.random.seed(seed)
    _w = jnp.asarray

    def _rec_inputs():
        import jax
        import jax.numpy as jnp
        _rk = jax.random.key(seed)
        x = 7.22e-05 + 1 * jax.random.normal(jax.random.fold_in(_rk, 1), (32, 56, 128), jnp.float32)
        _lenS = 56 - jax.random.randint(jax.random.fold_in(_rk, 7), (32,), 0, max(1, 56 // 4) + 1, jnp.int32)
        _lenS2 = 1500 - jax.random.randint(jax.random.fold_in(_rk, 8), (32,), 0, max(1, 1500 // 4) + 1, jnp.int32)
        _ctx_1024P = jax.random.normal(jax.random.fold_in(_rk, 11), (32, 16, 128), jnp.float32)
        _ctx_1024c = jax.random.dirichlet(jax.random.fold_in(_rk, 511), 0.3 * jnp.ones((16,), jnp.float32), (32, 1500))
        _ctx_1024t = jnp.einsum('bsk,bkd->bsd', _ctx_1024c, _ctx_1024P)
        _ctx_1024t = _ctx_1024t * jax.lax.rsqrt(jnp.mean(jnp.square(_ctx_1024t)) + 1e-12) * 0.953939
        ctx_1024 = 2.81802e-05 + 1.00001 * (_ctx_1024t + 0.3 * jax.random.normal(jax.random.fold_in(_rk, 611), (32, 1500, 128), jnp.float32))
        _g = jax.random.normal(jax.random.fold_in(_rk, 9001), (2, 1), jnp.float32)
        _g = jnp.sign(_g) * jnp.maximum(jnp.abs(_g), 1.0) + (_g == 0) * 1.0
        g_xattn = _g[0]
        g_ffn = _g[1]
        return (x, ctx_1024, g_xattn, g_ffn)
    x, ctx_1024, g_xattn, g_ffn = _rec_inputs()

    def _L0_xattn_setup():
        import jax, jax.numpy as jnp
        import numpy as np
        B, NT, NM, C, H, FF = (8, 128, 256, 128, 8, 512)

        def _ln(x, g, b):
            m = x.mean(-1, keepdims=True)
            v = jnp.mean((x - m) ** 2, axis=-1, keepdims=True)
            return (x - m) / jnp.sqrt(v + 1e-05) * g + b
        key = jax.random.key(seed)
        ks = jax.random.split(key, 8)
        w = lambda k, shape, s=0.02: jax.random.normal(k, shape, dtype=jnp.float32) * s
        return {'tgt': jax.random.normal(ks[0], (B, NT, C), dtype=jnp.float32), 'memory': jax.random.normal(ks[1], (B, NM, C), dtype=jnp.float32), 'qkv_w': w(ks[2], (3 * C, C)), 'qkv_b': jnp.zeros((3 * C,), jnp.float32), 'sa_out_w': w(ks[3], (C, C)), 'sa_out_b': jnp.zeros((C,), jnp.float32), 'in_proj_w': w(ks[4], (3 * C, C)), 'in_proj_b': jnp.zeros((3 * C,), jnp.float32), 'mha_out_w': w(ks[5], (C, C)), 'mha_out_b': jnp.zeros((C,), jnp.float32), 'lin1_w': w(ks[6], (FF, C)), 'lin1_b': jnp.zeros((FF,), jnp.float32), 'lin2_w': w(ks[7], (C, FF)), 'lin2_b': jnp.zeros((C,), jnp.float32), 'ln1_g': jnp.ones((C,), jnp.float32), 'ln1_b': jnp.zeros((C,), jnp.float32), 'ln2_g': jnp.ones((C,), jnp.float32), 'ln2_b': jnp.zeros((C,), jnp.float32), 'ln3_g': jnp.ones((C,), jnp.float32), 'ln3_b': jnp.zeros((C,), jnp.float32)}
    _L0_xattn_all = _L0_xattn_setup()
    _L0_xattn_in = {k: v for k, v in _L0_xattn_all.items() if k in ('qkv_w', 'qkv_b', 'sa_out_w', 'sa_out_b', 'in_proj_w', 'in_proj_b', 'mha_out_w', 'mha_out_b', 'lin1_w', 'lin1_b', 'lin2_w', 'lin2_b', 'ln1_g', 'ln1_b', 'ln2_g', 'ln2_b', 'ln3_g', 'ln3_b')}
    del _L0_xattn_all

    def _L0_ffn_setup():
        import jax, jax.numpy as jnp
        import numpy as np
        L, E, H, F, K = (4, 4, 128, 512, 2)
        B, S = (4, 256)
        EPS = 1e-05

        def _moe_layer(x, rw, rb, g, b, w1, b1, w2, b2):
            logits = jnp.einsum('bsh,he->bse', x, rw) + rb
            probs = jax.nn.softmax(logits, axis=-1)
            vals, idx = jax.lax.top_k(probs, K)
            vals = vals / vals.sum(axis=-1, keepdims=True)
            mu = x.mean(axis=-1, keepdims=True)
            xc = x - mu
            xhat = xc * jax.lax.rsqrt((xc * xc).mean(axis=-1, keepdims=True) + EPS)
            xe = xhat[None] * g[:, None, None, :] + b[:, None, None, :]
            h = jax.nn.gelu(jnp.einsum('ebsh,ehf->ebsf', xe, w1) + b1[:, None, None, :], approximate=False)
            y = jnp.einsum('ebsf,efh->ebsh', h, w2) + b2[:, None, None, :]
            expert_out = x[None] + y
            comb = jnp.einsum('bsk,bske->bse', vals, jax.nn.one_hot(idx, E, dtype=x.dtype))
            return jnp.einsum('bse,ebsh->bsh', comb, expert_out)
        key = jax.random.key(seed)
        ks = jax.random.split(key, 4)
        return {'hidden_states': jax.random.normal(ks[0], (B, S, H), jnp.float32), 'router_w': 0.02 * jax.random.normal(ks[1], (L, H, E), jnp.float32), 'router_b': jnp.zeros((L, E), jnp.float32), 'ln_g': jnp.ones((L, E, H), jnp.float32), 'ln_b': jnp.zeros((L, E, H), jnp.float32), 'w1': 0.02 * jax.random.normal(ks[2], (L, E, H, F), jnp.float32), 'b1': jnp.zeros((L, E, F), jnp.float32), 'w2': 0.02 * jax.random.normal(ks[3], (L, E, F, H), jnp.float32), 'b2': jnp.zeros((L, E, H), jnp.float32)}
    _L0_ffn_all = _L0_ffn_setup()
    _L0_ffn_in = {k: v for k, v in _L0_ffn_all.items() if k in ('router_w', 'router_b', 'ln_g', 'ln_b', 'w1', 'b1', 'w2', 'b2')}
    del _L0_ffn_all
    return {'x': x, 'ctx_1024': ctx_1024, 'g_xattn': g_xattn, 'g_ffn': g_ffn, 'L0_xattn_qkv_w': _L0_xattn_in['qkv_w'], 'L0_xattn_qkv_b': _L0_xattn_in['qkv_b'], 'L0_xattn_sa_out_w': _L0_xattn_in['sa_out_w'], 'L0_xattn_sa_out_b': _L0_xattn_in['sa_out_b'], 'L0_xattn_in_proj_w': _L0_xattn_in['in_proj_w'], 'L0_xattn_in_proj_b': _L0_xattn_in['in_proj_b'], 'L0_xattn_mha_out_w': _L0_xattn_in['mha_out_w'], 'L0_xattn_mha_out_b': _L0_xattn_in['mha_out_b'], 'L0_xattn_lin1_w': _L0_xattn_in['lin1_w'], 'L0_xattn_lin1_b': _L0_xattn_in['lin1_b'], 'L0_xattn_lin2_w': _L0_xattn_in['lin2_w'], 'L0_xattn_lin2_b': _L0_xattn_in['lin2_b'], 'L0_xattn_ln1_g': _L0_xattn_in['ln1_g'], 'L0_xattn_ln1_b': _L0_xattn_in['ln1_b'], 'L0_xattn_ln2_g': _L0_xattn_in['ln2_g'], 'L0_xattn_ln2_b': _L0_xattn_in['ln2_b'], 'L0_xattn_ln3_g': _L0_xattn_in['ln3_g'], 'L0_xattn_ln3_b': _L0_xattn_in['ln3_b'], 'L0_ffn_router_w': _L0_ffn_in['router_w'], 'L0_ffn_router_b': _L0_ffn_in['router_b'], 'L0_ffn_ln_g': _L0_ffn_in['ln_g'], 'L0_ffn_ln_b': _L0_ffn_in['ln_b'], 'L0_ffn_w1': _L0_ffn_in['w1'], 'L0_ffn_b1': _L0_ffn_in['b1'], 'L0_ffn_w2': _L0_ffn_in['w2'], 'L0_ffn_b2': _L0_ffn_in['b2']}

def reference(x, ctx_1024, g_xattn, g_ffn, L0_xattn_qkv_w, L0_xattn_qkv_b, L0_xattn_sa_out_w, L0_xattn_sa_out_b, L0_xattn_in_proj_w, L0_xattn_in_proj_b, L0_xattn_mha_out_w, L0_xattn_mha_out_b, L0_xattn_lin1_w, L0_xattn_lin1_b, L0_xattn_lin2_w, L0_xattn_lin2_b, L0_xattn_ln1_g, L0_xattn_ln1_b, L0_xattn_ln2_g, L0_xattn_ln2_b, L0_xattn_ln3_g, L0_xattn_ln3_b, L0_ffn_router_w, L0_ffn_router_b, L0_ffn_ln_g, L0_ffn_ln_b, L0_ffn_w1, L0_ffn_b1, L0_ffn_w2, L0_ffn_b2):
    import jax
    import jax.numpy as jnp

    def _L0_xattn_ref(tgt, memory, qkv_w, qkv_b, sa_out_w, sa_out_b, in_proj_w, in_proj_b, mha_out_w, mha_out_b, lin1_w, lin1_b, lin2_w, lin2_b, ln1_g, ln1_b, ln2_g, ln2_b, ln3_g, ln3_b):
        import jax, jax.numpy as jnp
        import numpy as np
        B, NT, NM, C, H, FF = (8, 128, 256, 128, 8, 512)

        def _ln(x, g, b):
            m = x.mean(-1, keepdims=True)
            v = jnp.mean((x - m) ** 2, axis=-1, keepdims=True)
            return (x - m) / jnp.sqrt(v + 1e-05) * g + b
        Bx, N, Cx = tgt.shape
        qkv = tgt @ qkv_w.T + qkv_b
        q, k, v = jnp.split(qkv, 3, axis=-1)
        scores = jnp.einsum('bnc,bmc->bnm', q, k) * jnp.sqrt(jnp.float32(Cx))
        diag = jnp.eye(N, dtype=bool)
        scores = jnp.where(diag[None, :, :], scores, -jnp.inf)
        attn = jax.nn.softmax(scores, axis=-1)
        sa = jnp.einsum('bnm,bmc->bnc', attn, v) @ sa_out_w.T + sa_out_b
        x = _ln(tgt + sa, ln1_g, ln1_b)
        d = Cx // H
        wq, wk, wv = jnp.split(in_proj_w, 3, axis=0)
        bq, bk, bv = jnp.split(in_proj_b, 3, axis=0)
        qh = (x @ wq.T + bq).reshape(Bx, N, H, d).transpose(0, 2, 1, 3)
        kh = (memory @ wk.T + bk).reshape(Bx, -1, H, d).transpose(0, 2, 1, 3)
        vh = (memory @ wv.T + bv).reshape(Bx, -1, H, d).transpose(0, 2, 1, 3)
        a = jax.nn.softmax(jnp.einsum('bhnd,bhmd->bhnm', qh, kh) / jnp.sqrt(jnp.float32(d)), axis=-1)
        ca = jnp.einsum('bhnm,bhmd->bhnd', a, vh).transpose(0, 2, 1, 3).reshape(Bx, N, Cx)
        ca = ca @ mha_out_w.T + mha_out_b
        x = _ln(x + ca, ln2_g, ln2_b)
        ff = jax.nn.relu(x @ lin1_w.T + lin1_b) @ lin2_w.T + lin2_b
        return _ln(x + ff, ln3_g, ln3_b)

    def _L0_ffn_ref(hidden_states, router_w, router_b, ln_g, ln_b, w1, b1, w2, b2):
        import jax, jax.numpy as jnp
        import numpy as np
        L, E, H, F, K = (4, 4, 128, 512, 2)
        B, S = (4, 256)
        EPS = 1e-05

        def _moe_layer(x, rw, rb, g, b, w1, b1, w2, b2):
            logits = jnp.einsum('bsh,he->bse', x, rw) + rb
            probs = jax.nn.softmax(logits, axis=-1)
            vals, idx = jax.lax.top_k(probs, K)
            vals = vals / vals.sum(axis=-1, keepdims=True)
            mu = x.mean(axis=-1, keepdims=True)
            xc = x - mu
            xhat = xc * jax.lax.rsqrt((xc * xc).mean(axis=-1, keepdims=True) + EPS)
            xe = xhat[None] * g[:, None, None, :] + b[:, None, None, :]
            h = jax.nn.gelu(jnp.einsum('ebsh,ehf->ebsf', xe, w1) + b1[:, None, None, :], approximate=False)
            y = jnp.einsum('ebsf,efh->ebsh', h, w2) + b2[:, None, None, :]
            expert_out = x[None] + y
            comb = jnp.einsum('bsk,bske->bse', vals, jax.nn.one_hot(idx, E, dtype=x.dtype))
            return jnp.einsum('bse,ebsh->bsh', comb, expert_out)
        x = hidden_states
        for l in range(L):
            x = _moe_layer(x, router_w[l], router_b[l], ln_g[l], ln_b[l], w1[l], b1[l], w2[l], b2[l])
        return x
    x = x + jnp.tanh(g_xattn[0]) * _L0_xattn_ref(_layernorm(x, axis=-1), ctx_1024, L0_xattn_qkv_w, L0_xattn_qkv_b, L0_xattn_sa_out_w, L0_xattn_sa_out_b, L0_xattn_in_proj_w, L0_xattn_in_proj_b, L0_xattn_mha_out_w, L0_xattn_mha_out_b, L0_xattn_lin1_w, L0_xattn_lin1_b, L0_xattn_lin2_w, L0_xattn_lin2_b, L0_xattn_ln1_g, L0_xattn_ln1_b, L0_xattn_ln2_g, L0_xattn_ln2_b, L0_xattn_ln3_g, L0_xattn_ln3_b)
    x = x + jnp.tanh(g_ffn[0]) * _L0_ffn_ref(_layernorm(x, axis=-1), L0_ffn_router_w, L0_ffn_router_b, L0_ffn_ln_g, L0_ffn_ln_b, L0_ffn_w1, L0_ffn_b1, L0_ffn_w2, L0_ffn_b2)
    return x

_drawn_inputs = setup_inputs


def setup_inputs(seed=0):
    import zlib

    import numpy as np

    out = dict(_drawn_inputs(seed))
    spreads = {'L0_xattn_qkv_b': (0.0, 0.499),
     'L0_xattn_sa_out_b': (0.0, 0.1),
     'L0_xattn_in_proj_b': (0.0, 0.551),
     'L0_xattn_mha_out_b': (0.0, 0.1),
     'L0_xattn_lin1_b': (0.0, 0.35),
     'L0_xattn_lin2_b': (0.0, 0.1),
     'L0_xattn_ln1_g': (1.0, 0.2),
     'L0_xattn_ln1_b': (0.0, 0.1),
     'L0_xattn_ln2_g': (1.0, 0.2),
     'L0_xattn_ln2_b': (0.0, 0.1),
     'L0_xattn_ln3_g': (1.0, 0.2),
     'L0_xattn_ln3_b': (0.0, 0.1),
     'L0_ffn_router_b': (0.0, 0.1),
     'L0_ffn_ln_g': (1.0, 0.6),
     'L0_ffn_ln_b': (0.0, 0.587),
     'L0_ffn_b1': (0.0, 0.1),
     'L0_ffn_b2': (0.0, 0.1)}
    factors = {'ctx_1024': 3.645, 'L0_xattn_in_proj_w': 3.502, 'L0_xattn_mha_out_w': 2.997}
    for name, (base, spread) in spreads.items():
        noise = np.random.default_rng([zlib.crc32(name.encode()), seed]).standard_normal(out[name].shape)
        drawn = base * np.exp(spread * noise) if base else spread * noise
        out[name] = jnp.asarray(drawn.astype(out[name].dtype))
    for name, factor in factors.items():
        out[name] = (out[name] * factor).astype(out[name].dtype)
    return out
```

```python
import concourse.bass as bass
from concourse import mybir
from contextlib import ExitStack

B, NQ, NKEY, C = 32, 56, 1500, 128
HEADS, HD = 8, 16
FF = 512
LAYERS, EXPERTS = 4, 4
TOK = B * NQ
P = 128
TILES = TOK // P
GROUPS = TILES // 2
GW = 2 * P
KT, KP = 12, 125
QW = HEADS * NQ
PAIR = 2 * NQ
NCH = 4
TPS = KT // NCH
SW = TPS * KP
RW = NKEY // TPS
CB = 8
CW = CB * NQ
CHUNKS = TOK // CW
FT = FF // P
EPS = 1e-5
WS = 64.0


def flamingo_block(nc, x, ctx_n, ctx_t, g_xattn, g_ffn, sa_wv, sa_bv, sa_wot, sa_bo, wq, wk, wv, bq, bv,
                   wot, wot_h, bo, l1t, l1b, l2t, l2b, ln1, ln2, ln3_g, ln3_b, rw, rb, moe_g, moe_b,
                   w1, b1, w2, b2, out):
    f32, f16, bf16 = mybir.dt.float32, mybir.dt.float16, mybir.dt.bfloat16
    ALU, ACT, AX = mybir.AluOpType, mybir.ActivationFunctionType, mybir.AxisListType
    add, sub, mul = ALU.add, ALU.subtract, ALU.mult
    es = ExitStack()
    with es:
        def sb(name, shape, dt=f32):
            return es.enter_context(nc.sbuf_tensor(name, shape, dt))

        def sem(name):
            return es.enter_context(nc.semaphore(name))

        ident = sb("ident", [P, P])
        ident_b = sb("ident_b", [P, P], bf16)
        ones32 = sb("ones32", [P, P])
        ones_b = sb("ones_b", [P, P], bf16)
        neghalf = sb("neghalf", [P, TILES])
        sa_wv_s = sb("sa_wv_s", [P, P])
        sa_bv_s = sb("sa_bv_s", [P, 1])
        sa_wot_s = sb("sa_wot_s", [P, P])
        sa_bias = sb("sa_bias", [P, P])
        wq_s = sb("wq_s", [HD, HEADS, P])
        wk_s = sb("wk_s", [HD, HEADS, P])
        wv_s = sb("wv_s", [HD, HEADS, P])
        wo_s = sb("wo_s", [HD, HEADS, P])
        bq_s = sb("bq_s", [HD, HEADS])
        bv_s = sb("bv_s", [P, 1])
        wot_s = sb("wot_s", [P, P])
        ca_bias = sb("ca_bias", [P, 1])
        l1_s = sb("l1_s", [P, FF])
        l1b_s = sb("l1b_s", [P, FT])
        l2_s = sb("l2_s", [P, FT, P])
        l2b_s = sb("l2b_s", [P, 1])
        ln1_s = sb("ln1_s", [P, 2])
        ln2_s = sb("ln2_s", [P, 2])
        g3_row = sb("g3_row", [P, P])
        b3_row = sb("b3_row", [P, P])
        gates = sb("gates", [P, 2])
        rw_s = sb("rw_s", [P, LAYERS * EXPERTS])
        rb_s = sb("rb_s", [P, LAYERS, EXPERTS])
        rw_hi = sb("rw_hi", [P, LAYERS * EXPERTS], f16)
        rw_lo = sb("rw_lo", [P, LAYERS * EXPERTS], f16)
        rw_sum = sb("rw_sum", [P, LAYERS, EXPERTS])
        moe_g_s = sb("moe_g_s", [P, LAYERS * EXPERTS])
        moe_b_s = sb("moe_b_s", [P, LAYERS * EXPERTS])
        b1_s = sb("b1_s", [P, LAYERS, EXPERTS * FT])
        b2_s = sb("b2_s", [EXPERTS, LAYERS, P])
        m_sa = sb("m_sa", [P, P])
        a_qk = sb("a_qk", [P, HEADS, P])
        a_vo = sb("a_vo", [P, HEADS, P])
        q_bias = sb("q_bias", [P, HEADS])

        x_tm = sb("x_tm", [P, TILES, P])
        y_tm = sb("y_tm", [P, TILES, P])
        z_tm = sb("z_tm", [P, TILES, P])
        f_t = sb("f_t", [P, TOK])
        stats = sb("stats", [P, TILES, 6])
        mv = sb("mv", [P, TILES, 2])
        mean = sb("mean", [P, TILES])
        y_grp = sb("y_grp", [P, 2, P])
        grp = sb("grp", [P, 5, 2])
        ve = sb("ve", [P, TILES])
        rstd = sb("rstd", [P, TILES])
        shift = sb("shift", [P, TILES])

        q_region = sb("q_region", [P, B * QW])
        q_parts = q_region[:, :].bitcast(f16).rearrange("p (b s w) -> p b s w", b=B, s=2)
        ctx_sum = q_region[:, :].rearrange("p (b h n) -> p b h n", b=B, h=HEADS)

        n32 = [v[:].rearrange("p t c -> p (t c)")[:, 0:KT * P] for v in (y_tm, z_tm)]
        t32 = [sb(f"t32_{i}", [P, NKEY]) for i in range(2)]
        n_hi = [sb(f"n_hi{i}", [P, KT, P], f16) for i in range(2)]
        n_lo = [sb(f"n_lo{i}", [P, KT, P], f16) for i in range(2)]
        TPAD = NKEY + 4
        t_hi = [sb(f"t_hi{i}", [P, TPAD], f16) for i in range(2)]
        t_lo = [sb(f"t_lo{i}", [P, TPAD], f16) for i in range(2)]
        p32 = [sb(f"p32_{i}", [P, TPS, QW]) for i in range(2)]
        p_hi = [sb(f"p_hi{i}", [P, TPS, QW], f16) for i in range(2)]
        p_lo = [sb(f"p_lo{i}", [P, TPS, QW], f16) for i in range(2)]
        nmax = sb("nmax", [P, NCH])
        shift_d = [sb(f"shift_d{i}", [P, QW], bf16) for i in range(2)]
        p_sum = [sb(f"p_sum{i}", [P, QW]) for i in range(2)]
        inv_sum = sb("inv_sum", [P, NCH])
        inv_diag = sb("inv_diag", [P, QW])

        w1_raw = sb("w1_raw", [P, EXPERTS, FF])
        w2_raw = sb("w2_raw", [P, EXPERTS * FT, P])
        at = [0]

        def carve(words, dt=f32):
            v = q_region[:, at[0]:at[0] + words]
            at[0] += words
            return v if dt is f32 else v.bitcast(dt)

        w1_hi, w1_lo, w2_hi, w2_lo = ([carve(EXPERTS * FF // 2, f16) for _ in range(2)] for _ in range(4))
        ff_at = at[0]
        h32 = [carve(FT * GW).rearrange("p (q n) -> p q n", q=FT) for _ in range(2)]
        h_hi = [carve(FT * GW // 2, f16).rearrange("p (q n) -> p q n", q=FT) for _ in range(2)]
        h_lo = [carve(FT * GW // 2, f16).rearrange("p (q n) -> p q n", q=FT) for _ in range(2)]
        xt_hi = carve(TOK // 2, f16)
        xt_lo = carve(TOK // 2, f16)
        assert at[0] <= B * QW
        ffh = [q_region[:, ff_at + i * FT * CW:ff_at + (i + 1) * FT * CW].rearrange("p (q n) -> p q n", q=FT) for i in range(2)]
        b1_fold = [sb(f"b1_fold{i}", [P, EXPERTS * FT]) for i in range(2)]
        lg = sb("lg", [P, TILES, EXPERTS])
        lg_t = sb("lg_t", [P, TILES, EXPERTS])
        rank = sb("rank", [P, TILES, EXPERTS])
        best = sb("best", [P, TILES, EXPERTS])
        second = sb("second", [P, TILES, EXPERTS])
        top = sb("top", [P, 3, TILES])
        gap = sb("gap", [P, TILES])
        std = sb("std", [P, TILES])
        comb = sb("comb", [P, TILES, EXPERTS])
        comb_s = sb("comb_s", [P, TILES, EXPERTS])
        comb_t = f_t[0:EXPERTS, :]

        psum = es.enter_context(nc.psum_tensor("psum", [P, 8, 512], f32))
        bank = [psum[:, i, :] for i in range(8)]
        max_scores = psum[0:PAIR, 0:TPS, 0:RW]

        x_loaded, w_loaded, moe_small_loaded = sem("x_loaded"), sem("w_loaded"), sem("moe_small_loaded")
        t_loaded = [sem(f"t_loaded{i}") for i in range(2)]
        n_loaded = [sem(f"n_loaded{i}") for i in range(2)]
        w1_loaded, w2_loaded = sem("w1_loaded"), sem("w2_loaded")
        consts_made, pool_step = sem("consts_made"), sem("pool_step")
        vec_step = sem("vec_step")
        folds_mm, folds_done, gates_done, rows_gated = (sem(n) for n in ("folds_mm", "folds_done", "gates_done", "rows_gated"))
        ln_var, ln_rstd, ln_out = sem("ln_var"), sem("ln_rstd"), sem("ln_out")
        tr_done, tr_evac = sem("tr_done"), sem("tr_evac")
        sa_mm = sem("sa_mm")
        q_mm, q_hi_done, q_lo_done = sem("q_mm"), sem("q_hi_done"), sem("q_lo_done")
        max_mm, max_read, shift_ready = sem("max_mm"), sem("max_read"), sem("shift_ready")
        score_mm, phi_done, plo_done, p_added = sem("score_mm"), sem("phi_done"), sem("plo_done"), sem("p_added")
        pv_mm, ctx_copied, p_sum_mm, inv_ready, inv_diag_ready = (sem(n) for n in ("pv_mm", "ctx_copied", "p_sum_mm", "inv_ready", "inv_diag_ready"))
        inv_mm, sum_done = sem("inv_mm"), sem("sum_done")
        thi_done, tlo_done, nhi_done, nlo_done = sem("thi_done"), sem("tlo_done"), sem("nhi_done"), sem("nlo_done")
        x_biased = sem("x_biased")
        ca_mm, ca_added = sem("ca_mm"), sem("ca_added")
        back_done = sem("back_done")
        ff1_mm, ff1_act, ff2_mm, ff2_added = sem("ff1_mm"), sem("ff1_act"), sem("ff2_mm"), sem("ff2_added")
        w_split, b1_mm, b1_done, b2_mm = sem("w_split"), sem("b1_mm"), sem("b1_done"), sem("b2_mm")
        hid_mm, gelu_done, hhi_done, hlo_done = sem("hid_mm"), sem("gelu_done"), sem("hhi_done"), sem("hlo_done")
        y_mm, acc_done, b2_added = sem("y_mm"), sem("acc_done"), sem("b2_added")
        xh_ready, xt_mm, xthi_done, xtlo_done, logit_mm = (sem(n) for n in ("xh_ready", "xt_mm", "xthi_done", "xtlo_done", "logit_mm"))
        g_var, g_rstd, g_step = sem("g_var"), sem("g_rstd"), sem("g_step")
        y_copied = sem("y_copied")
        gap_ready, gate_tanh, comb_ready = sem("gap_ready"), sem("gate_tanh"), sem("comb_ready")
        ct_mm, ct_done = sem("ct_mm"), sem("ct_done")
        out_ready, out_stored = sem("out_ready"), sem("out_stored")

        small_loads = [
            (sa_wv_s[:], sa_wv), (sa_bv_s[:], sa_bv), (sa_wot_s[:], sa_wot), (sa_bias[:], sa_bo.to_broadcast([P, P])),
            (wq_s[:], wq), (wk_s[:], wk), (wv_s[:], wv), (wo_s[:], wot_h), (bq_s[:], bq), (bv_s[:], bv), (wot_s[:], wot),
            (ca_bias[:], bo), (l1_s[:], l1t), (l1b_s[:], l1b), (l2_s[:], l2t.rearrange("(q p) o -> p q o", p=P)), (l2b_s[:], l2b),
            (ln1_s[:], ln1), (ln2_s[:], ln2), (g3_row[:], ln3_g.to_broadcast([P, P])), (b3_row[:], ln3_b.to_broadcast([P, P])),
            (gates[:, 0:1], g_xattn.to_broadcast([P, 1])), (gates[:, 1:2], g_ffn.to_broadcast([P, 1])),
            (rw_s[:], rw), (rb_s[:], rb.to_broadcast([P, LAYERS * EXPERTS]).rearrange("p (l e) -> p l e", l=LAYERS)),
        ]
        moe_small = [(moe_g_s[:], moe_g), (moe_b_s[:], moe_b), (b1_s[:], b1), (b2_s[:], b2)]
        W_ALL = 16 * len(small_loads)
        LN_SEQ = {"in": 1, "one": 2, "two": 3, "three": 4, "outer": 5}
        TR_CH = [(0, 4), (4, 8), (8, 12), (12, 14)]

        block = es.enter_context(nc.Block())

        def seq_pairs(engine, step):
            step(0, 0)
            step(1, 1)
            with engine.Fori(1, B // 2 - 1) as i:
                for par in range(2):
                    step(i * 2 + par, par)
            step(B - 2, 0)
            step(B - 1, 1)

        def is_int(b, v=None):
            return type(b) is int and (v is None or b == v)

        def before(b, par, j):
            return (b, par, j - 1) if j else (b - 1, 1 - par, NCH - 1)

        ADDS = KT - 1

        def adds(b, j):
            return b * ADDS + (TPS * (j + 1) - 1)

        def context_sums(b):
            return ctx_sum[:, b, :, :] if is_int(b) else ctx_sum[:, bass.ds(b, 1), :, :].rearrange("p o h n -> p (o h) n")

        @block.sync
        def _(sp):
            sp.dma_start(x_tm[:], x.rearrange("(t p) c -> p t c", p=P)).then_inc(x_loaded, 16)
            for dst, src in small_loads:
                sp.dma_start(dst, src).then_inc(w_loaded, 16)
            for dst, src in moe_small:
                sp.dma_start(dst, src).then_inc(moe_small_loaded, 16)

            def load(b, par):
                if not is_int(b) or b >= 2:
                    sp.wait_ge(tlo_done, (b - 1) * NCH)
                sp.dma_start(t32[par][:], ctx_t[b] if is_int(b) else ctx_t[bass.ds(b, 1), :, :].rearrange("o p n -> (o p) n")).then_inc(t_loaded[par], 16)
                if not is_int(b) or b >= 2:
                    sp.wait_ge(nlo_done, b - 1)
                else:
                    sp.wait_ge(tr_done, 8)
                sp.dma_start(n32[par][0:KP, :], ctx_n[b] if is_int(b) else ctx_n[bass.ds(b, 1), :, :].rearrange("o p n -> (o p) n")).then_inc(n_loaded[par], 16)
            sp.dma_start(w1_raw[:], w1[0]).then_inc(w1_loaded, 16)
            sp.dma_start(w2_raw[:], w2[0]).then_inc(w2_loaded, 16)
            load(0, 0)
            load(1, 1)
            with sp.Fori(1, B // 2) as i:
                for par in range(2):
                    load(i * 2 + par, par)
            for l in range(1, LAYERS):
                sp.wait_ge(w_split, 2 * EXPERTS * l)
                sp.dma_start(w1_raw[:], w1[l]).then_inc(w1_loaded, 16)
                sp.dma_start(w2_raw[:], w2[l]).then_inc(w2_loaded, 16)
            out_v = out.rearrange("(t p) c -> p t c", p=P)
            for g in range(GROUPS):
                sp.wait_ge(out_ready, g + 1)
                sp.dma_start(out_v[:, 2 * g:2 * g + 2, :], x_tm[:, 2 * g:2 * g + 2, :]).then_inc(out_stored, 16)
            sp.wait_ge(out_stored, 16 * GROUPS)

        @block.gpsimd
        def _(pool):
            steps = [0]

            def step(ins):
                steps[0] += 1
                ins.then_inc(pool_step, 1)
                pool.wait_ge(pool_step, steps[0])

            step(nc.gpsimd.memset(ident[:], 0.0))
            step(nc.gpsimd.affine_select(out=ident[:], in_=ident[:], compare_op=ALU.not_equal, fill=1.0, base=0,
                                         pattern=[[-1, P]], channel_multiplier=1))
            nc.gpsimd.tensor_copy(ident_b[:], ident[:]).then_inc(consts_made, 1)
            nc.gpsimd.memset(ones32[:], 1.0).then_inc(consts_made, 1)
            nc.gpsimd.memset(ones_b[:], 1.0).then_inc(consts_made, 1)
            step(nc.gpsimd.memset(neghalf[:], -0.5))
            for i in range(2):
                nc.gpsimd.memset(t_hi[i][:, NKEY:TPAD], 0.0).then_inc(consts_made, 1)
                nc.gpsimd.memset(t_lo[i][:, NKEY:TPAD], 0.0).then_inc(consts_made, 1)

            def rsqrt_all(n):
                pool.wait_ge(ln_var, n)
                nc.gpsimd.tensor_tensor(rstd[:], ve[:], neghalf[:], ALU.pow).then_inc(ln_rstd, 1)

            rsqrt_all(LN_SEQ["in"])
            rsqrt_all(LN_SEQ["one"])
            pool.wait_ge(rows_gated, 1)
            pool.wait_ge(ln_out, 1)
            nc.gpsimd.tensor_tensor(x_tm[:], x_tm[:], b3_row[:, None, :].to_broadcast([P, TILES, P]), add).then_inc(x_biased, 1)

            def split_piece(l, k):
                s, e = l % 2, k % EXPERTS
                first = k < EXPERTS
                raw = w1_raw[:, e, :] if first else w2_raw[:, e * FT:(e + 1) * FT, :].rearrange("p q c -> p (q c)")
                hi, lo = (w1_hi[s], w1_lo[s]) if first else (w2_hi[s], w2_lo[s])
                cols = slice(e * FF, (e + 1) * FF)
                gain = moe_g_s[:, EXPERTS * l + e:EXPERTS * l + e + 1] if first else 1.0
                step(nc.gpsimd.tensor_scalar(raw, raw, gain, WS, mul, mul))
                step(nc.gpsimd.tensor_copy(hi[:, cols], raw))
                last = nc.gpsimd.tensor_tensor(lo[:, cols], raw, hi[:, cols], sub)
                last.then_inc(w_split, 1)

            def split_ready(l):
                pool.wait_ge(w1_loaded, 16 * (l + 1))
                pool.wait_ge(w2_loaded, 16 * (l + 1))
                pool.wait_ge(b1_mm, l + 1)
                if l >= 2:
                    pool.wait_ge(y_mm, GROUPS * EXPERTS * (l - 1))

            def split_n(b, par):
                pool.wait_ge(nhi_done, b + 1)
                nc.gpsimd.tensor_tensor(n_lo[par][0:KP, :, :].rearrange("p t c -> p (t c)"), n32[par][0:KP, :],
                                        n_hi[par][0:KP, :, :].rearrange("p t c -> p (t c)"), sub).then_inc(nlo_done, 1)

            def sequence(b, par):
                total = p_sum[par][0:KP, :]
                for j in range(NCH):
                    for i in range(TPS):
                        t = TPS * j + i
                        if t == 0:
                            continue
                        pool.wait_ge(phi_done, b * KT + (t + 1))
                        tile = p32[j % 2][0:KP, i, :]
                        if t == 1:
                            if not (is_int(b) and b < 2):
                                pool.wait_ge(p_sum_mm, b - 1)
                            nc.gpsimd.tensor_tensor(total, p32[0][0:KP, 0, :], tile, add).then_inc(p_added, 1)
                        else:
                            pool.wait_ge(p_added, b * ADDS + (t - 1))
                            nc.gpsimd.tensor_tensor(total, total, tile, add).then_inc(p_added, 1)
                    if j == 1 and not is_int(b, B - 1):
                        split_n(b + 1, 1 - par)

            split_n(0, 0)
            seq_pairs(pool, sequence)

            pool.wait_ge(moe_small_loaded, 16 * len(moe_small))
            rsqrt_all(LN_SEQ["two"])
            split_ready(0)
            pool.wait_ge(ca_mm, CHUNKS)
            for k in range(0, 3):
                split_piece(0, k)
            rsqrt_all(LN_SEQ["three"])
            for k in range(3, 5):
                split_piece(0, k)
            rsqrt_all(LN_SEQ["outer"])
            for k in range(5, 2 * EXPERTS):
                split_piece(0, k)

            def rsqrt_group(n, g):
                pool.wait_ge(g_var, n)
                nc.gpsimd.tensor_tensor(rstd[:, bass.ds(2 * g, 2)], ve[:, bass.ds(2 * g, 2)], neghalf[:, 0:2], ALU.pow).then_inc(g_rstd, 1)

            with pool.Fori(0, GROUPS) as g:
                rsqrt_group(g + 1, g)
            PIECES = [(0,), (1,), (2,), (3,), (4,), (5,), (6, 7)]
            for l in range(1, LAYERS):
                for g in range(GROUPS):
                    rsqrt_group(GROUPS * l + g + 1, g)
                    if g == 0:
                        split_ready(l)
                    for k in PIECES[g]:
                        split_piece(l, k)

        @block.scalar
        def _(act):
            act.wait_ge(w_loaded, W_ALL)
            nc.scalar.activation(gates[:], gates[:], ACT.Tanh).then_inc(gates_done, 1)

            def evac(n, src, affine=None):
                for c, (t0, t1) in enumerate(TR_CH):
                    act.wait_ge(tr_done, 4 * n + c + 1)
                    w = (t1 - t0) * P
                    a = {} if affine is None else {"scale": affine[:, 0:1], "bias": affine[:, 1:2]}
                    nc.scalar.activation(f_t[:, t0 * P:t1 * P], src[c][:, 0:w], ACT.Identity, **a).then_inc(tr_evac, 1)

            evac(0, bank[4:8])
            evac(1, bank[4:8], ln1_s)
            act.wait_ge(folds_done, 1)
            for k in range(CHUNKS * HEADS):
                c, h = divmod(k, HEADS)
                act.wait_ge(q_mm, k + 1)
                nc.scalar.activation(q_parts[:, c * CB:(c + 1) * CB, 0, h * NQ:(h + 1) * NQ],
                                     bank[k % 4][:, 0:CW].rearrange("p (b n) -> p b n", b=CB), ACT.Identity,
                                     bias=q_bias[:, h:h + 1]).then_inc(q_hi_done, 1)

            def split_t(b, par, j):
                if j == 0:
                    act.wait_ge(t_loaded[par], 16 * (b // 2 + 1) if is_int(b) else (b - par) * 8 + 16)
                nc.scalar.copy(t_hi[par][:, j * SW:(j + 1) * SW], t32[par][:, j * SW:(j + 1) * SW]).then_inc(thi_done, 1)

            def copy_sums(b):
                act.wait_ge(pv_mm, b * NCH + NCH)
                nc.scalar.copy(context_sums(b), bank[6][:, 0:QW].rearrange("p (h n) -> p h n", h=HEADS)).then_inc(ctx_copied, 1)

            def split_n(b, par):
                act.wait_ge(n_loaded[par], 16 * (b // 2 + 1) if is_int(b) else (b - par) * 8 + 16)
                nc.scalar.copy(n_hi[par][0:KP, :, :].rearrange("p t c -> p (t c)"), n32[par][0:KP, :]).then_inc(nhi_done, 1)

            for b in range(2):
                for j in range(NCH):
                    split_t(b, b, j)
            split_n(0, 0)

            def sequence(b, par):
                for j in range(NCH):
                    ring = j % 2
                    if j == 1 and not is_int(b, 0):
                        copy_sums(b - 1)
                    if not (is_int(b, 0) and j < 2):
                        act.wait_ge(pv_mm, b * NCH + (j - 1))
                        act.wait_ge(p_added, adds(b, j - 2) if j >= 2 else adds(b - 1, j + 2))
                    for i in range(TPS):
                        t = TPS * j + i
                        act.wait_ge(score_mm, b * KT + (t + 1))
                        nc.scalar.activation(p32[ring][0:KP, i, :], bank[3 + i][0:KP, 0:QW], ACT.Exp)
                        nc.scalar.activation(p_hi[ring][0:KP, i, :], bank[3 + i][0:KP, 0:QW], ACT.Exp).then_inc(phi_done, 1)
                    if not (is_int(b) and b >= B - 2):
                        split_t(b + 2, par, j)
                    if j == 1 and not is_int(b, B - 1):
                        split_n(b + 1, 1 - par)

            seq_pairs(act, sequence)
            copy_sums(B - 1)

            evac(2, bank[0:4], ln2_s)
            for c in range(CHUNKS):
                for q in range(FT):
                    act.wait_ge(ff1_mm, c * FT + q + 1)
                    if q == 0 and c >= 2:
                        act.wait_ge(ff2_mm, c - 1)
                    nc.scalar.activation(ffh[c % 2][:, q, :], bank[q][:, 0:CW], ACT.Relu, bias=l1b_s[:, q:q + 1]).then_inc(ff1_act, 1)

            def split_xt(n, g):
                act.wait_ge(xt_mm, n)
                nc.scalar.copy(xt_hi[:, bass.ds(g * GW, GW)], bank[6][:, 0:GW]).then_inc(xthi_done, 1)

            with act.Fori(0, GROUPS) as g:
                split_xt(g + 1, g)

            def hidden(u, l, e):
                par = e % 2
                act.wait_ge(hid_mm, u + 1)
                if not (l == 0 and is_int(u) and u < 2):
                    act.wait_ge(hlo_done, u - 1)
                for q in range(FT):
                    k = e * FT + q
                    last = nc.scalar.activation(h32[par][:, q, :], bank[2 * par + q // 2][:, (q % 2) * GW:(q % 2 + 1) * GW],
                                                ACT.Gelu, scale=1.0 / WS, bias=b1_fold[l % 2][:, k:k + 1])
                last.then_inc(gelu_done, 1)
                act.wait_ge(gelu_done, u + 1)
                if not (l == 0 and is_int(u) and u < 2):
                    act.wait_ge(y_mm, u - 1)
                nc.scalar.copy(h_hi[par], h32[par]).then_inc(hhi_done, 1)

            def route(l):
                act.wait_ge(gap_ready, l + 1)
                nc.scalar.activation(gap[:], gap[:], ACT.Tanh, scale=0.5).then_inc(gate_tanh, 1)

            def combs_t(l, c):
                t0, t1 = TR_CH[c]
                act.wait_ge(ct_mm, 4 * l + c + 1)
                nc.scalar.copy(comb_t[:, t0 * P:t1 * P], bank[6][0:EXPERTS, 0:(t1 - t0) * P]).then_inc(ct_done, 1)

            for l in range(LAYERS):
                base = GROUPS * EXPERTS * l
                act.wait_ge(b1_done, l + 1)
                route(l)
                for e in range(EXPERTS):
                    hidden(base + e, l, e)
                    if e:
                        combs_t(l, e - 1)
                combs_t(l, 3)
                with act.Fori(1, GROUPS) as g:
                    for e in range(EXPERTS):
                        hidden(g * EXPERTS + (base + e), l, e)
                        if e == 2 and l < LAYERS - 1:
                            split_xt(g + GROUPS * (l + 1), g - 1)
                if l < LAYERS - 1:
                    split_xt(GROUPS * (l + 2), GROUPS - 1)

        @block.vector
        def _(dve):
            steps = [0]

            def step(ins):
                steps[0] += 1
                ins.then_inc(vec_step, 1)
                dve.wait_ge(vec_step, steps[0])

            V = nc.vector

            def layer_norm(n, src, dst):
                for t in range(TILES):
                    last = V.bn_stats(stats[:, t, :], src(t))
                step(last)
                for t in range(TILES):
                    last = V.bn_aggr(mv[:, t, :], stats[:, t, :])
                step(last)
                V.tensor_scalar(ve[:], mv[:, :, 1], EPS, None, add).then_inc(ln_var, 1)
                dve.wait_ge(ln_rstd, n)
                step(V.scalar_tensor_tensor(out=shift[:], in0=mv[:, :, 0], scalar=-1.0, in1=rstd[:], op0=mul, op1=mul))
                for t in range(TILES):
                    last = V.tensor_scalar(dst(t), src(t), rstd[:, t:t + 1], shift[:, t:t + 1], mul, add)
                last.then_inc(ln_out, 1)
                dve.wait_ge(ln_out, n)

            dve.wait_ge(w_loaded, W_ALL)
            dve.wait_ge(folds_mm, 1)
            V.tensor_copy(m_sa[:], bank[0][:, 0:128])
            V.tensor_tensor(sa_bias[:], bank[0][:, 128:256], sa_bias[:], add)
            V.tensor_tensor(ca_bias[:], bank[0][:, 256:257], ca_bias[:], add)
            V.tensor_copy(rw_sum[:].rearrange("p l e -> p (l e)"), bank[0][:, 260:276])
            V.tensor_scalar(q_bias[:], bank[0][:, 280:288], HD ** -0.5, None, mul)
            for i in range(2):
                V.tensor_scalar(a_qk[:, 4 * i:4 * i + 4, :], bank[1 + i][:, :].rearrange("p (h c) -> p h c", h=4), HD ** -0.5, None, mul)
                V.tensor_copy(a_vo[:, 4 * i:4 * i + 4, :], bank[3 + i][:, :].rearrange("p (h c) -> p h c", h=4))
            dve.wait_ge(gates_done, 1)
            V.tensor_scalar(g3_row[:], g3_row[:], gates[:, 0:1], None, mul)
            V.tensor_scalar(b3_row[:], b3_row[:], gates[:, 0:1], None, mul).then_inc(rows_gated, 1)
            step(V.tensor_scalar(rw_s[:], rw_s[:], WS, None, mul))
            step(V.tensor_copy(rw_hi[:], rw_s[:]))
            V.tensor_tensor(rw_lo[:], rw_s[:], rw_hi[:], sub).then_inc(folds_done, 1)
            dve.wait_ge(folds_done, 1)

            dve.wait_ge(x_loaded, 16)
            layer_norm(LN_SEQ["in"], lambda t: x_tm[:, t, :], lambda t: y_tm[:, t, :])
            step(V.tensor_tensor(z_tm[:], y_tm[:], sa_bias[:, None, :].to_broadcast([P, TILES, P]), add))
            for c, (t0, t1) in enumerate(TR_CH):
                dve.wait_ge(sa_mm, c + 1)
                last = V.tensor_tensor(z_tm[:, t0:t1, :], bank[c][:, 0:(t1 - t0) * P].rearrange("p (t c) -> p t c", c=P),
                                       z_tm[:, t0:t1, :], add)
            step(last)
            layer_norm(LN_SEQ["one"], lambda t: z_tm[:, t, :], lambda t: z_tm[:, t, :])
            for k in range(CHUNKS * HEADS):
                c, h = divmod(k, HEADS)
                dve.wait_ge(q_hi_done, k + 1)
                V.scalar_tensor_tensor(out=q_parts[:, c * CB:(c + 1) * CB, 1, h * NQ:(h + 1) * NQ],
                                       in0=bank[k % 4][:, 0:CW].rearrange("p (b n) -> p b n", b=CB), scalar=q_bias[:, h:h + 1],
                                       in1=q_parts[:, c * CB:(c + 1) * CB, 0, h * NQ:(h + 1) * NQ],
                                       op0=add, op1=sub).then_inc(q_lo_done, 1)

            def fold_b1(l):
                dve.wait_ge(b1_mm, l + 1)
                V.tensor_tensor(b1_fold[l % 2][:], bank[7][:, 256:256 + EXPERTS * FT], b1_s[:, l, :], add).then_inc(b1_done, 1)

            fold_b1(0)

            def split_t(b, par, j):
                dve.wait_ge(thi_done, b * NCH + (j + 1))
                V.tensor_tensor(t_lo[par][:, j * SW:(j + 1) * SW], t32[par][:, j * SW:(j + 1) * SW],
                                t_hi[par][:, j * SW:(j + 1) * SW], sub).then_inc(tlo_done, 1)

            def maximum(b, par, j):
                dve.wait_ge(max_mm, b * NCH + (j + 1))
                V.tensor_reduce(out=nmax[0:PAIR, j:j + 1],
                                in_=max_scores, axis=AX.XY, op=ALU.max).then_inc(max_read, 1)
                dve.wait_ge(max_read, b * NCH + (j + 1))
                if j == 0 and not (is_int(b) and b < 2):
                    dve.wait_ge(score_mm, (b - 1) * KT)
                V.tensor_scalar(shift_d[par][0:PAIR, j * PAIR:(j + 1) * PAIR], ident_b[0:PAIR, 0:PAIR],
                                nmax[0:PAIR, j:j + 1], -1.0, mul, mul).then_inc(shift_ready, 1)

            def low_probs(b, j):
                ring = j % 2
                dve.wait_ge(phi_done, b * KT + TPS * (j + 1))
                V.tensor_tensor(p_lo[ring][0:KP, :, :].rearrange("p t w -> p (t w)"),
                                p32[ring][0:KP, :, :].rearrange("p t w -> p (t w)"),
                                p_hi[ring][0:KP, :, :].rearrange("p t w -> p (t w)"), sub).then_inc(plo_done, 1)

            def invert(b):
                dve.wait_ge(p_sum_mm, b + 1)
                V.reciprocal(inv_sum[0:PAIR, :], bank[7][0:PAIR, QW:QW + NCH]).then_inc(inv_ready, 1)
                dve.wait_ge(inv_ready, b + 1)
                blocks = [PAIR, NCH, PAIR]
                V.tensor_tensor(inv_diag[0:PAIR, :].rearrange("p (j w) -> p j w", j=NCH), ident[0:PAIR, None, 0:PAIR].to_broadcast(blocks),
                                inv_sum[0:PAIR, :, None].to_broadcast(blocks), mul).then_inc(inv_diag_ready, 1)

            def divide(b):
                dve.wait_ge(inv_mm, b + 1)
                dve.wait_ge(ctx_copied, b + 1)
                o = context_sums(b)
                V.tensor_tensor(o, bank[7][:, 0:QW].rearrange("p (h n) -> p h n", h=HEADS), o, mul).then_inc(sum_done, 1)

            for b in range(2):
                for j in range(NCH):
                    split_t(b, b, j)
            for j in range(NCH):
                maximum(0, 0, j)

            def sequence(b, par):
                for j in range(NCH):
                    first = is_int(b, 0) and j == 0
                    pb, ppar, pj = before(b, par, j)
                    if not first:
                        low_probs(pb, pj)
                    if not is_int(b, B - 1):
                        maximum(b + 1, 1 - par, j)
                    if not first and not (is_int(pb) and pb >= B - 2):
                        split_t(pb + 2, ppar, pj)
                    if not is_int(b, 0):
                        if j == 1:
                            invert(b - 1)
                        if j == 3:
                            divide(b - 1)

            seq_pairs(dve, sequence)
            low_probs(B - 1, NCH - 1)
            invert(B - 1)
            divide(B - 1)

            for c in range(CHUNKS):
                dve.wait_ge(ca_mm, c + 1)
                V.scalar_tensor_tensor(out=f_t[:, c * CW:(c + 1) * CW], in0=bank[c][:, 0:CW], scalar=ca_bias[:, 0:1],
                                       in1=f_t[:, c * CW:(c + 1) * CW], op0=add, op1=add).then_inc(ca_added, 1)

            def tm_psum(banks):
                return lambda t: banks[t // 4][:, (t % 4) * P:(t % 4 + 1) * P]

            dve.wait_ge(back_done, 1)
            layer_norm(LN_SEQ["two"], tm_psum(bank[4:8]), lambda t: z_tm[:, t, :])
            dve.wait_ge(tr_evac, 12)
            for c in range(CHUNKS):
                dve.wait_ge(ff2_mm, c + 1)
                V.scalar_tensor_tensor(out=f_t[:, c * CW:(c + 1) * CW], in0=bank[4 + c][:, 0:CW], scalar=l2b_s[:, 0:1],
                                       in1=f_t[:, c * CW:(c + 1) * CW], op0=add, op1=add).then_inc(ff2_added, 1)
            dve.wait_ge(back_done, 2)
            layer_norm(LN_SEQ["three"], tm_psum(bank[0:4]), lambda t: z_tm[:, t, :])
            step(V.tensor_tensor(z_tm[:], z_tm[:], g3_row[:, None, :].to_broadcast([P, TILES, P]), mul))
            dve.wait_ge(x_biased, 1)
            step(V.tensor_tensor(x_tm[:], x_tm[:], z_tm[:], add))
            layer_norm(LN_SEQ["outer"], lambda t: x_tm[:, t, :], lambda t: y_tm[:, t, :])

            G_STEPS = 4

            def normalise(n, g):
                tiles = bass.ds(2 * g, 2)
                for i in range(2):
                    last = V.bn_stats(stats[:, i, :], y_grp[:, i, :])
                last.then_inc(g_step, 1)
                dve.wait_ge(g_step, n * G_STEPS + 1)
                V.tensor_tensor(grp[:, 0, :], stats[:, 0:2, 1], stats[:, 0:2, 4], add)
                V.tensor_tensor(grp[:, 1, :], stats[:, 0:2, 1], stats[:, 0:2, 4], sub)
                V.tensor_tensor(grp[:, 2, :], stats[:, 0:2, 2], stats[:, 0:2, 5], add).then_inc(g_step, 1)
                dve.wait_ge(g_step, n * G_STEPS + 2)
                V.scalar_tensor_tensor(out=grp[:, 3, :], in0=grp[:, 1, :], scalar=0.25, in1=grp[:, 1, :], op0=mul, op1=mul)
                V.tensor_scalar(mean[:, tiles], grp[:, 0, :], 0.5, None, mul)
                V.tensor_scalar(grp[:, 4, :], grp[:, 2, :], 1.0 / P, EPS, mul, add).then_inc(g_step, 1)
                dve.wait_ge(g_step, n * G_STEPS + 3)
                V.tensor_tensor(ve[:, tiles], grp[:, 3, :], grp[:, 4, :], add).then_inc(g_var, 1)
                dve.wait_ge(g_rstd, n + 1)
                V.scalar_tensor_tensor(out=shift[:, 0:2], in0=grp[:, 0, :], scalar=-0.5, in1=rstd[:, tiles],
                                       op0=mul, op1=mul).then_inc(g_step, 1)
                dve.wait_ge(g_step, n * G_STEPS + 4)
                if not is_int(n, 0):
                    dve.wait_ge(xt_mm, n)
                for i in range(2):
                    last = V.tensor_scalar(z_tm[:, i, :], y_grp[:, i, :], rstd[:, bass.ds(2 * g + i, 1)], shift[:, i:i + 1], mul, add)
                last.then_inc(xh_ready, 1)

            def split_xt(n, g):
                dve.wait_ge(xthi_done, n)
                V.tensor_tensor(xt_lo[:, bass.ds(g * GW, GW)], bank[6][:, 0:GW], xt_hi[:, bass.ds(g * GW, GW)], sub).then_inc(xtlo_done, 1)

            with dve.Fori(0, GROUPS) as g:
                V.tensor_scalar(y_grp[:], y_tm[:, bass.ds(2 * g, 2), :], 1.0, None, mul).then_inc(y_copied, 1)
                dve.wait_ge(y_copied, g + 1)
                normalise(g, g)
                split_xt(g + 1, g)

            def route(l):
                te = [P, TILES, EXPERTS]
                dve.wait_ge(logit_mm, GROUPS * (l + 1))
                step(V.tensor_tensor(std[:], ve[:], rstd[:], mul))
                step(V.scalar_tensor_tensor(out=lg[:], in0=bank[7][:, 0:TILES * EXPERTS].rearrange("p (t e) -> p t e", t=TILES),
                                            scalar=1.0 / WS, in1=std[:, :, None].to_broadcast(te), op0=mul, op1=mul))
                step(V.tensor_tensor(lg_t[:], mean[:, :, None].to_broadcast(te), rw_sum[:, l:l + 1, :].to_broadcast(te), mul))
                step(V.tensor_tensor(lg[:], lg[:], lg_t[:], add))
                step(V.tensor_tensor(lg[:], lg[:], rb_s[:, l:l + 1, :].to_broadcast(te), add))
                step(V.tensor_tensor(rank[:], lg[:, :, 0:1].to_broadcast(te), lg[:], ALU.is_gt))
                for j in range(1, EXPERTS):
                    step(V.tensor_tensor(lg_t[:], lg[:, :, j:j + 1].to_broadcast(te), lg[:], ALU.is_gt))
                    step(V.tensor_tensor(rank[:], rank[:], lg_t[:], add))
                for j in range(EXPERTS - 1):
                    r = [P, TILES, EXPERTS - 1 - j]
                    step(V.tensor_tensor(lg_t[:, :, j + 1:], lg[:, :, j:j + 1].to_broadcast(r), lg[:, :, j + 1:], ALU.is_equal))
                    step(V.tensor_tensor(rank[:, :, j + 1:], rank[:, :, j + 1:], lg_t[:, :, j + 1:], add))
                V.tensor_scalar(best[:], rank[:], 0.0, None, ALU.is_equal)
                step(V.tensor_scalar(second[:], rank[:], 1.0, None, ALU.is_equal))
                for i, m in enumerate((best, second)):
                    step(V.tensor_tensor(lg_t[:], m[:], lg[:], mul))
                    step(V.tensor_reduce(out=top[:, i, :], in_=lg_t[:], axis=AX.X, op=add))
                V.tensor_tensor(gap[:], top[:, 0, :], top[:, 1, :], sub).then_inc(gap_ready, 1)
                dve.wait_ge(gate_tanh, l + 1)
                V.tensor_scalar(top[:, 0, :], gap[:], 0.5, 0.5, mul, add)
                step(V.tensor_scalar(top[:, 1, :], gap[:], -0.5, 0.5, mul, add))
                V.tensor_tensor(best[:], best[:], top[:, 0, :, None].to_broadcast(te), mul)
                step(V.tensor_tensor(second[:], second[:], top[:, 1, :, None].to_broadcast(te), mul))
                step(V.tensor_tensor(comb[:], best[:], second[:], add))
                V.tensor_scalar(comb_s[:], comb[:], 1.0 / WS, None, mul).then_inc(comb_ready, 1)
                dve.wait_ge(comb_ready, l + 1)

            def low_parts(u, l, e):
                par = e % 2
                dve.wait_ge(hhi_done, u + 1)
                V.tensor_tensor(h_lo[par], h32[par], h_hi[par], sub).then_inc(hlo_done, 1)

            def accumulate(u, l, g, e):
                dve.wait_ge(y_mm, u + 1)
                for i in range(2):
                    yt = y_tm[:, bass.ds(2 * g + i, 1), :].rearrange("p o c -> p (o c)")
                    cs = comb_s[:, bass.ds(2 * g + i, 1), e:e + 1].rearrange("p o c -> p (o c)")
                    last = V.scalar_tensor_tensor(out=yt if e < EXPERTS - 1 else y_grp[:, i, :], in0=bank[4 + e % 2][:, i * P:(i + 1) * P], scalar=cs, in1=yt,
                                                  op0=mul, op1=add)
                last.then_inc(acc_done, 1)
                dve.wait_ge(acc_done, u + 1)

            def add_b2(l, c):
                t0, t1 = TR_CH[c]
                dve.wait_ge(b2_mm, 4 * l + c + 1)
                V.tensor_tensor(y_tm[:, t0:t1, :], bank[7][:, 0:(t1 - t0) * P].rearrange("p (t c) -> p t c", c=P),
                                y_tm[:, t0:t1, :], add).then_inc(b2_added, 1)
                dve.wait_ge(b2_added, 4 * l + c + 1)

            def finish(l, n, g):
                if l < LAYERS - 1:
                    V.tensor_scalar(y_tm[:, bass.ds(2 * g, 2), :], y_grp[:], 1.0, None, mul)
                    normalise(n, g)
                else:
                    V.scalar_tensor_tensor(out=x_tm[:, bass.ds(2 * g, 2), :], in0=y_grp[:],
                                           scalar=gates[:, 1:2], in1=x_tm[:, bass.ds(2 * g, 2), :], op0=mul, op1=add).then_inc(out_ready, 1)

            for l in range(LAYERS):
                base = GROUPS * EXPERTS * l
                route(l)
                for e in range(EXPERTS):
                    low_parts(base + e, l, e)
                    if e:
                        accumulate(base + e - 1, l, 0, e - 1)
                    if e >= 2:
                        add_b2(l, e - 2)
                add_b2(l, 2)
                add_b2(l, 3)
                if l < LAYERS - 1:
                    fold_b1(l + 1)
                with dve.Fori(1, GROUPS) as g:
                    for e in range(EXPERTS):
                        u = g * EXPERTS + (base + e)
                        low_parts(u, l, e)
                        accumulate(u - 1, l, g - 1 if e == 0 else g, (e - 1) % EXPERTS)
                        if e == 0:
                            finish(l, g + (GROUPS * (l + 1) - 1), g - 1)
                        if e == 3 and l < LAYERS - 1:
                            split_xt(g + GROUPS * (l + 1), g - 1)
                accumulate(base + GROUPS * EXPERTS - 1, l, GROUPS - 1, EXPERTS - 1)
                finish(l, GROUPS * (l + 2) - 1, GROUPS - 1)
                if l < LAYERS - 1:
                    split_xt(GROUPS * (l + 2), GROUPS - 1)

        @block.tensor
        def _(pe):
            def mm(dst, lhs, rhs, start=True, stop=True):
                return nc.tensor.matmul(dst, lhs, rhs, start=start, stop=stop)

            pe.wait_ge(w_loaded, W_ALL)
            pe.wait_ge(consts_made, 7)
            mm(bank[0][:, 0:128], sa_wv_s[:], sa_wot_s[:])
            mm(bank[0][:, 128:256], sa_bv_s[:, 0:1].to_broadcast([P, P]), sa_wot_s[:])
            mm(bank[0][:, 256:257], wot_s[:], bv_s[:])
            mm(bank[0][:, 260:276], ones32[:], rw_s[:])
            for h in range(HEADS):
                mm(bank[0][:, 280 + h:281 + h], wk_s[:, h, :], bq_s[:, h:h + 1])
                mm(bank[1 + h // 4][:, (h % 4) * P:(h % 4 + 1) * P], wq_s[:, h, :], wk_s[:, h, :])
                last = mm(bank[3 + h // 4][:, (h % 4) * P:(h % 4 + 1) * P], wv_s[:, h, :], wo_s[:, h, :])
            last.then_inc(folds_mm, 1)

            def transposes(src, banks, done, each):
                for c, (t0, t1) in enumerate(TR_CH):
                    for t in range(t0, t1):
                        last = nc.tensor.transpose(banks[c][:, (t - t0) * P:(t - t0 + 1) * P], src(t), ident[:])
                    if each:
                        last.then_inc(done, 1)
                if not each:
                    last.then_inc(done, 1)

            pe.wait_ge(folds_done, 1)
            pe.wait_ge(ln_out, 1)
            transposes(lambda t: y_tm[:, t, :], bank[4:8], tr_done, True)
            for c, (t0, t1) in enumerate(TR_CH):
                pe.wait_ge(tr_evac, c + 1)
                for t in range(t0, t1):
                    last = mm(bank[c][:, (t - t0) * P:(t - t0 + 1) * P], f_t[:, t * P:(t + 1) * P], m_sa[:])
                last.then_inc(sa_mm, 1)
            pe.wait_ge(ln_out, 2)
            transposes(lambda t: z_tm[:, t, :], bank[4:8], tr_done, True)
            pe.wait_ge(tr_evac, 8)
            for k in range(CHUNKS * HEADS):
                c, h = divmod(k, HEADS)
                if k >= 4:
                    pe.wait_ge(q_lo_done, k - 3)
                mm(bank[k % 4][:, 0:CW], a_qk[:, h, :], f_t[:, c * CW:(c + 1) * CW]).then_inc(q_mm, 1)
            def fold_b1(l):
                pe.wait_ge(w1_loaded, 16 * (l + 1))
                if l == 0:
                    pe.wait_ge(moe_small_loaded, 16 * len(moe_small))
                for k in range(EXPERTS * FT):
                    e, q = divmod(k, FT)
                    last = mm(bank[7][:, 256 + k:257 + k], w1_raw[:, e, q * P:(q + 1) * P],
                              moe_b_s[:, EXPERTS * l + e:EXPERTS * l + e + 1])
                last.then_inc(b1_mm, 1)

            fold_b1(0)
            pe.wait_ge(q_lo_done, CHUNKS * HEADS)
            pe.wait_ge(b1_done, 1)

            def queries(b, s, w0, w):
                if is_int(b):
                    return q_parts[:, b, s, w0:w0 + w]
                return q_parts[:, bass.ds(b, 1), s, w0:w0 + w].rearrange("p o w -> p (o w)")

            def maximum(b, par, j):
                if j == 0:
                    pe.wait_ge(thi_done, (b + 1) * NCH)
                if not (is_int(b, 0) and j == 0):
                    pe.wait_ge(max_read, b * NCH + j)
                for r in range(TPS):
                    last = mm(psum[0:PAIR, r, 0:RW], queries(b, 0, j * PAIR, PAIR), t_hi[par][:, r * RW:(r + 1) * RW])
                last.then_inc(max_mm, 1)

            def scores(b, par, j):
                if j == 0:
                    pe.wait_ge(tlo_done, (b + 1) * NCH)
                    pe.wait_ge(shift_ready, (b + 1) * NCH)
                for i in range(TPS):
                    t = TPS * j + i
                    dst = bank[3 + i][:, 0:QW]
                    keys = slice(t * KP, t * KP + P)
                    if not (is_int(b, 0) and j == 0):
                        pe.wait_ge(phi_done, b * KT + (t - TPS + 1))
                    mm(dst, t_hi[par][:, keys], queries(b, 0, 0, QW), True, False)
                    mm(dst, t_hi[par][:, keys], queries(b, 1, 0, QW), False, False)
                    mm(dst, t_lo[par][:, keys], queries(b, 0, 0, QW), False, False)
                    mm(dst, ones_b[0:PAIR, :], shift_d[par][0:PAIR, :], False, True).then_inc(score_mm, 1)

            def weighted(b, par, j):
                ring = j % 2
                pe.wait_ge(plo_done, b * NCH + (j + 1))
                if j == 0:
                    pe.wait_ge(nlo_done, b + 1)
                    if not is_int(b, 0):
                        pe.wait_ge(ctx_copied, b)
                for i in range(TPS):
                    t = TPS * j + i
                    hi, lo = p_hi[ring][0:KP, i, :], p_lo[ring][0:KP, i, :]
                    first, end = t == 0, t == KT - 1
                    mm(bank[6][:, 0:QW], n_hi[par][0:KP, t, :], hi, first, False)
                    mm(bank[6][:, 0:QW], n_hi[par][0:KP, t, :], lo, False, False)
                    last = mm(bank[6][:, 0:QW], n_lo[par][0:KP, t, :], hi, False, end)
                last.then_inc(pv_mm, 1)

            def probability_sums(b, par):
                pe.wait_ge(p_added, b * ADDS + ADDS)
                if not (is_int(b) and b < 1):
                    pe.wait_ge(sum_done, b)
                for j in range(NCH):
                    last = mm(bank[7][0:PAIR, QW + j:QW + j + 1], p_sum[par][0:KP, j * PAIR:(j + 1) * PAIR], ones32[0:KP, 0:1])
                last.then_inc(p_sum_mm, 1)

            def spread_inverses(b):
                pe.wait_ge(inv_diag_ready, b + 1)
                mm(bank[7][:, 0:QW], ones32[0:PAIR, :], inv_diag[0:PAIR, :]).then_inc(inv_mm, 1)

            for j in range(NCH):
                maximum(0, 0, j)

            def sequence(b, par):
                for j in range(NCH):
                    if not is_int(b, B - 1):
                        maximum(b + 1, 1 - par, j)
                    if j == 2 and not is_int(b, 0):
                        spread_inverses(b - 1)
                    scores(b, par, j)
                    if not (is_int(b, 0) and j == 0):
                        weighted(*before(b, par, j))
                    if j == 0 and not is_int(b, 0):
                        probability_sums(b - 1, 1 - par)

            seq_pairs(pe, sequence)
            weighted(B - 1, 1, NCH - 1)
            probability_sums(B - 1, 1)
            spread_inverses(B - 1)

            pe.wait_ge(sum_done, B)
            for c in range(CHUNKS):
                for h in range(HEADS):
                    last = mm(bank[c][:, 0:CW], a_vo[:, h, :], ctx_sum[:, c * CB:(c + 1) * CB, h, :], h == 0, h == HEADS - 1)
                last.then_inc(ca_mm, 1)
            pe.wait_ge(ca_added, CHUNKS)
            transposes(lambda t: f_t[:, t * P:(t + 1) * P], bank[4:8], back_done, False)
            pe.wait_ge(ln_out, LN_SEQ["two"])
            transposes(lambda t: z_tm[:, t, :], bank[0:4], tr_done, True)
            pe.wait_ge(tr_evac, 12)
            for c in range(CHUNKS + 1):
                if c < CHUNKS:
                    for q in range(FT):
                        if c:
                            pe.wait_ge(ff1_act, (c - 1) * FT + q + 1)
                        mm(bank[q][:, 0:CW], l1_s[:, q * P:(q + 1) * P], f_t[:, c * CW:(c + 1) * CW]).then_inc(ff1_mm, 1)
                if c:
                    pe.wait_ge(ff1_act, c * FT)
                    for q in range(FT):
                        last = mm(bank[3 + c][:, 0:CW], l2_s[:, q, :], ffh[(c - 1) % 2][:, q, :], q == 0, q == FT - 1)
                    last.then_inc(ff2_mm, 1)
            pe.wait_ge(ff2_added, CHUNKS)
            transposes(lambda t: f_t[:, t * P:(t + 1) * P], bank[0:4], back_done, False)

            def group_transposes(n, g):
                pe.wait_ge(xh_ready, n + 1)
                if not is_int(n, 0):
                    pe.wait_ge(xtlo_done, n)
                for i in range(2):
                    last = nc.tensor.transpose(bank[6][:, i * P:(i + 1) * P],
                                               z_tm[:, i, :], ident[:])
                last.then_inc(xt_mm, 1)

            def group_logits(l, n, g):
                pe.wait_ge(xtlo_done, n + 1)
                cols = slice(EXPERTS * l, EXPERTS * (l + 1))
                for i in range(2):
                    dst = bank[7][:, bass.ds((2 * g + i) * EXPERTS, EXPERTS)]
                    hi, lo = (v[:, bass.ds(g * GW + i * P, P)] for v in (xt_hi, xt_lo))
                    mm(dst, hi, rw_hi[:, cols], True, False)
                    mm(dst, hi, rw_lo[:, cols], False, False)
                    last = mm(dst, lo, rw_hi[:, cols], False, True)
                last.then_inc(logit_mm, 1)

            def hidden(u, l, g, e):
                s, par = l % 2, e % 2
                if not (l == 0 and is_int(u) and u < 2):
                    pe.wait_ge(gelu_done, u - 1)
                toks = bass.ds(g * GW, GW)
                for q in range(FT):
                    dst = bank[2 * par + q // 2][:, (q % 2) * GW:(q % 2 + 1) * GW]
                    w = slice(e * FF + q * P, e * FF + (q + 1) * P)
                    mm(dst, w1_hi[s][:, w], xt_hi[:, toks], True, False)
                    mm(dst, w1_hi[s][:, w], xt_lo[:, toks], False, False)
                    last = mm(dst, w1_lo[s][:, w], xt_hi[:, toks], False, True)
                last.then_inc(hid_mm, 1)

            def output(u, l, g, e):
                s, par = l % 2, e % 2
                pe.wait_ge(hlo_done, u + 1)
                if not (l == 0 and is_int(u) and u < 2):
                    pe.wait_ge(acc_done, u - 1)
                for i in range(2):
                    dst = bank[4 + par][:, i * P:(i + 1) * P]
                    for q in range(FT):
                        w = slice((e * FT + q) * P, (e * FT + q + 1) * P)
                        toks = slice(i * P, (i + 1) * P)
                        mm(dst, h_hi[par][:, q, toks], w2_hi[s][:, w], q == 0, False)
                        mm(dst, h_hi[par][:, q, toks], w2_lo[s][:, w], False, False)
                        last = mm(dst, h_lo[par][:, q, toks], w2_hi[s][:, w], False, q == FT - 1)
                last.then_inc(y_mm, 1)

            def weights_transposed(l, c):
                t0, t1 = TR_CH[c]
                pe.wait_ge(comb_ready, l + 1)
                if l or c:
                    pe.wait_ge(ct_done, 4 * l + c)
                    pe.wait_ge(xtlo_done, GROUPS * (l + 1))
                for t in range(t0, t1):
                    last = nc.tensor.transpose(bank[6][0:EXPERTS, (t - t0) * P:(t - t0 + 1) * P], comb[:, t, :], ident[:])
                last.then_inc(ct_mm, 1)

            def output_biases(l, c):
                t0, t1 = TR_CH[c]
                pe.wait_ge(ct_done, 4 * l + c + 1)
                if l or c:
                    pe.wait_ge(b2_added, 4 * l + c)
                for t in range(t0, t1):
                    last = mm(bank[7][:, (t - t0) * P:(t - t0 + 1) * P], comb_t[:, t * P:(t + 1) * P], b2_s[:, l, :])
                last.then_inc(b2_mm, 1)

            pe.wait_ge(ln_out, LN_SEQ["three"])
            with pe.Fori(0, GROUPS) as g:
                group_transposes(g, g)
                group_logits(0, g, g)
            for l in range(LAYERS):
                base = GROUPS * EXPERTS * l
                pe.wait_ge(w_split, 2 * EXPERTS * (l + 1))
                for e in range(EXPERTS):
                    hidden(base + e, l, 0, e)
                    if e:
                        output(base + e - 1, l, 0, e - 1)
                        weights_transposed(l, e - 1)
                    if e >= 2:
                        output_biases(l, e - 2)
                weights_transposed(l, 3)
                output_biases(l, 2)
                output_biases(l, 3)
                if l < LAYERS - 1:
                    pe.wait_ge(b2_added, 4 * (l + 1))
                    fold_b1(l + 1)
                with pe.Fori(1, GROUPS) as g:
                    for e in range(EXPERTS):
                        u = g * EXPERTS + (base + e)
                        hidden(u, l, g, e)
                        output(u - 1, l, g - 1 if e == 0 else g, (e - 1) % EXPERTS)
                        if l < LAYERS - 1:
                            n = g + (GROUPS * (l + 1) - 1)
                            if e == 2:
                                group_transposes(n, g - 1)
                            if e == 3:
                                pe.wait_ge(b1_done, l + 2)
                                group_logits(l + 1, n, g - 1)
                output(base + GROUPS * EXPERTS - 1, l, GROUPS - 1, EXPERTS - 1)
                if l < LAYERS - 1:
                    n = GROUPS * (l + 2) - 1
                    group_transposes(n, GROUPS - 1)
                    group_logits(l + 1, n, GROUPS - 1)


_OUT = (B, NQ, C)


def kernel(**inputs):
    import numpy as _np
    import concourse.bacc as _bacc
    from concourse import mybir as _mybir
    from concourse.bass_utils import run_bass_kernel_spmd as _run

    a = {k: _np.asarray(v) for k, v in inputs.items()}
    qkv_w, qkv_b = a["L0_xattn_qkv_w"], a["L0_xattn_qkv_b"]
    in_w, in_b = a["L0_xattn_in_proj_w"], a["L0_xattn_in_proj_b"]
    ctx, out_w = a["ctx_1024"], a["L0_xattn_mha_out_w"]

    def heads_first(w):
        return w.reshape(HEADS, HD, P).transpose(1, 0, 2)

    layout = {
        "x": a["x"].reshape(TOK, C),
        "ctx_n": ctx.reshape(B, KP, KT * C),
        "ctx_t": ctx.reshape(B, KP, KT, C).transpose(0, 3, 2, 1).reshape(B, C, NKEY),
        "g_xattn": a["g_xattn"].reshape(1, 1),
        "g_ffn": a["g_ffn"].reshape(1, 1),
        "sa_wv": qkv_w[2 * C:3 * C],
        "sa_bv": qkv_b[2 * C:3 * C].reshape(C, 1),
        "sa_wot": a["L0_xattn_sa_out_w"].T,
        "sa_bo": a["L0_xattn_sa_out_b"].reshape(1, C),
        "wq": heads_first(in_w[0:C]),
        "wk": heads_first(in_w[C:2 * C]),
        "wv": heads_first(in_w[2 * C:3 * C]),
        "bq": in_b[0:C].reshape(HEADS, HD).T,
        "bv": in_b[2 * C:3 * C].reshape(C, 1),
        "wot": out_w.T,
        "wot_h": heads_first(out_w.T),
        "bo": a["L0_xattn_mha_out_b"].reshape(C, 1),
        "l1t": a["L0_xattn_lin1_w"].T,
        "l1b": a["L0_xattn_lin1_b"].reshape(FT, P).T,
        "l2t": a["L0_xattn_lin2_w"].T,
        "l2b": a["L0_xattn_lin2_b"].reshape(C, 1),
        "ln1": _np.stack([a["L0_xattn_ln1_g"], a["L0_xattn_ln1_b"]], 1),
        "ln2": _np.stack([a["L0_xattn_ln2_g"], a["L0_xattn_ln2_b"]], 1),
        "ln3_g": a["L0_xattn_ln3_g"].reshape(1, C),
        "ln3_b": a["L0_xattn_ln3_b"].reshape(1, C),
        "rw": a["L0_ffn_router_w"].transpose(1, 0, 2).reshape(C, LAYERS * EXPERTS),
        "rb": a["L0_ffn_router_b"].reshape(1, LAYERS * EXPERTS),
        "moe_g": a["L0_ffn_ln_g"].reshape(LAYERS * EXPERTS, C).T,
        "moe_b": a["L0_ffn_ln_b"].reshape(LAYERS * EXPERTS, C).T,
        "w1": a["L0_ffn_w1"].transpose(0, 2, 1, 3),
        "b1": a["L0_ffn_b1"].reshape(LAYERS, EXPERTS * FT, P).transpose(2, 0, 1),
        "w2": a["L0_ffn_w2"].reshape(LAYERS, EXPERTS * FT, P, C).transpose(0, 2, 1, 3),
        "b2": a["L0_ffn_b2"].transpose(1, 0, 2),
    }
    nc = _bacc.Bacc("TRN2", target_bir_lowering=False, num_devices=1)
    arrays, args = {}, []
    for name, v in layout.items():
        v = _np.ascontiguousarray(v)
        arrays[f"in_{name}"] = v
        args.append(nc.dram_tensor(f"in_{name}", v.shape, _mybir.dt.from_np(v.dtype), kind="ExternalInput").ap())
    args.append(nc.dram_tensor("out", (TOK, C), _mybir.dt.float32, kind="ExternalOutput").ap())
    flamingo_block(nc, *args)
    r = _run(nc, [arrays], core_ids=[0])
    return _np.asarray(r.results[0]["out"]).reshape(_OUT)
```

```python
import concourse.bass as bass
from concourse import mybir
from contextlib import ExitStack

B, NQ, NKEY, C = 32, 56, 1500, 128
HEADS, HD = 8, 16
FF = 512
LAYERS, EXPERTS = 4, 4
TOK = B * NQ
P = 128
TP = PAIR = 2 * NQ
TILES = TOK // TP
KT, KP = 12, 125
QW = HEADS * NQ
NCH = 4
TPS = KT // NCH
SW = TPS * KP
RW = NKEY // TPS
CB = 8
CW = CB * NQ
CHUNKS = TOK // CW
CT = CW // TP
FT = FF // P
EPS = 1e-5
WS = 64.0


def flamingo_block(nc, x, ctx_n, ctx_t, g_xattn, g_ffn, sa_wv, sa_bv, sa_wot, sa_bo, wq, wk, wv, bq, bv,
                   wot, wot_h, bo, l1t, l1b, l2t, l2b, ln1, ln2, ln3_g, ln3_b, rw, rb, moe_g, moe_b,
                   w1, b1, w2, b2, out):
    f32, f16, bf16 = mybir.dt.float32, mybir.dt.float16, mybir.dt.bfloat16
    ALU, ACT, AX = mybir.AluOpType, mybir.ActivationFunctionType, mybir.AxisListType
    add, sub, mul = ALU.add, ALU.subtract, ALU.mult
    es = ExitStack()
    with es:
        def sb(name, shape, dt=f32):
            return es.enter_context(nc.sbuf_tensor(name, shape, dt))

        def sem(name):
            return es.enter_context(nc.semaphore(name))

        ident = sb("ident", [P, P])
        ident_b = sb("ident_b", [P, P], bf16)
        ones32 = sb("ones32", [P, P])
        ones_b = sb("ones_b", [P, P], bf16)
        ones_h = sb("ones_h", [P, TP], f16)
        neghalf = sb("neghalf", [P, CT])
        sa_wv_s = sb("sa_wv_s", [P, P])
        sa_bv_s = sb("sa_bv_s", [P, 1])
        sa_wot_s = sb("sa_wot_s", [P, P])
        sa_bias = sb("sa_bias", [P, P])
        wq_s = sb("wq_s", [HD, HEADS, P])
        wk_s = sb("wk_s", [HD, HEADS, P])
        wv_s = sb("wv_s", [HD, HEADS, P])
        wo_s = sb("wo_s", [HD, HEADS, P])
        bq_s = sb("bq_s", [HD, HEADS])
        bv_s = sb("bv_s", [P, 1])
        wot_s = sb("wot_s", [P, P])
        ca_bias = sb("ca_bias", [P, 1])
        l1_s = sb("l1_s", [P, FF])
        l1b_s = sb("l1b_s", [P, FT])
        l2_s = sb("l2_s", [P, FT, P])
        l2b_s = sb("l2b_s", [P, 1])
        ln1_s = sb("ln1_s", [P, 2])
        ln2_s = sb("ln2_s", [P, 2])
        g3_row = sb("g3_row", [P, P])
        b3_row = sb("b3_row", [P, P])
        gates = sb("gates", [P, 2])
        rw_s = sb("rw_s", [P, LAYERS * EXPERTS])
        rb_s = sb("rb_s", [P, LAYERS, EXPERTS])
        rw_hi = sb("rw_hi", [P, LAYERS * EXPERTS], f16)
        rw_lo = sb("rw_lo", [P, LAYERS * EXPERTS], f16)
        rw_sum = sb("rw_sum", [P, LAYERS, EXPERTS])
        moe_g_s = sb("moe_g_s", [P, LAYERS * EXPERTS])
        moe_b_s = sb("moe_b_s", [P, LAYERS * EXPERTS])
        b1_s = sb("b1_s", [P, LAYERS, EXPERTS * FT])
        m_sa = sb("m_sa", [P, P])
        a_qk = sb("a_qk", [P, HEADS, P])
        a_vo = sb("a_vo", [P, HEADS, P])
        q_bias = sb("q_bias", [P, HEADS])

        x_tm = sb("x_tm", [P, TILES, P])
        y_tm = sb("y_tm", [P, TILES, P])
        z_tm = sb("z_tm", [P, TILES, P])
        f_t = sb("f_t", [P, TOK])
        stats = sb("stats", [P, CT, 6])
        mv = sb("mv", [P, CT, 2])
        ln_var, ln_neg, ln_scale, ln_shift = (sb(n, [P, 3, TILES]) for n in ("ln_var", "ln_neg", "ln_scale", "ln_shift"))

        q_region = sb("q_region", [P, B * QW])
        q_parts = q_region[:, :].bitcast(f16).rearrange("p (b s w) -> p b s w", b=B, s=2)
        ctx_sum = q_region[:, :].rearrange("p (b h n) -> p b h n", b=B, h=HEADS)

        n32 = [v[:].rearrange("p t c -> p (t c)")[:, 0:KT * P] for v in (y_tm, z_tm)]
        t32 = [sb(f"t32_{i}", [P, NKEY]) for i in range(2)]
        n_hi = [sb(f"n_hi{i}", [P, KT, P], f16) for i in range(2)]
        n_lo = [sb(f"n_lo{i}", [P, KT, P], f16) for i in range(2)]
        TPAD = NKEY + 4
        t_hi = [sb(f"t_hi{i}", [P, TPAD], f16) for i in range(2)]
        t_lo = [sb(f"t_lo{i}", [P, TPAD], f16) for i in range(2)]
        p32 = [sb(f"p32_{i}", [P, TPS, QW]) for i in range(2)]
        p_hi = [sb(f"p_hi{i}", [P, TPS, QW], f16) for i in range(2)]
        p_lo = [sb(f"p_lo{i}", [P, TPS, QW], f16) for i in range(2)]
        nmax = sb("nmax", [P, NCH])
        shift_d = [sb(f"shift_d{i}", [P, QW], bf16) for i in range(2)]
        p_sum = [sb(f"p_sum{i}", [P, QW]) for i in range(2)]
        inv_sum = sb("inv_sum", [P, NCH])
        inv_diag = sb("inv_diag", [P, QW])

        w1_raw = sb("w1_raw", [P, EXPERTS, FF])
        w2_raw = sb("w2_raw", [P, EXPERTS * FT, P])

        def part(buf, words, dt=f32):
            v = buf[:].rearrange("p a b -> p (a b)") if len(buf.shape) == 3 else buf[:]
            v = v[:, 0:words] if v.dtype is f32 else v[:, 0:2 * words].bitcast(f32)
            return v if dt is f32 else v.bitcast(dt)

        def region(chunk, words, dt=f32, at=0):
            v = q_region[:, chunk * CB * QW + at:chunk * CB * QW + at + words]
            return v if dt is f32 else v.bitcast(dt)

        EW, HW = EXPERTS * FF // 2, FT * CW
        ffh = [region(c, HW).rearrange("p (q n) -> p q n", q=FT) for c in range(CHUNKS)]
        xt_hi, xt_lo = region(0, TOK // 2, f16, HW), region(0, TOK // 2, f16, HW + TOK // 2)
        h32 = [region(1 + i, HW, at=HW).rearrange("p (q n) -> p q n", q=FT) for i in range(2)]
        h_hi = [region(0, HW // 2, f16, i * HW // 2).rearrange("p (q n) -> p q n", q=FT) for i in range(2)]
        h_lo = [region(1, HW // 2, f16, i * HW // 2).rearrange("p (q n) -> p q n", q=FT) for i in range(2)]
        w1_hi = [part(p32[0], EW, f16), region(2, EW, f16)]
        w1_lo = [part(p32[1], EW, f16), region(3, EW, f16)]
        w2_hi = [part(t32[0], EW, f16), region(3, EW, f16, EW)]
        w2_lo = [part(t32[1], EW, f16), region(3, EW, f16, 2 * EW)]
        y_grp, z_grp = (part(p_hi[i], CT * P).rearrange("p (t c) -> p t c", t=CT) for i in (1, 0))
        b2_raw = [part(v, EXPERTS * P) for v in (n_lo[0], n_lo[1], t_lo[0], t_lo[1])]
        b2_parts = [part(v, EXPERTS * P, f16)[:, k * EXPERTS * P:(k + 1) * EXPERTS * P] for v in n_hi for k in range(2)]
        b1_fold = [sb(f"b1_fold{i}", [P, EXPERTS * FT]) for i in range(2)]
        te = [TP, CT, EXPERTS]
        pairs = [TP, CT, EXPERTS, EXPERTS]
        e_stats_s = sb("e_stats_s", [P, CT, 6])
        (m_sum, m_diff, v_sum, e_neg, e_mean, e_var, e_scale, e_shift, e_std, gap) = (
            sb(n, [P, CT]) for n in ("m_sum", "m_diff", "v_sum", "e_neg", "e_mean", "e_var", "e_scale", "e_shift", "e_std", "gap"))
        lg, lg_bias, rank, best, second, picked, halves = (
            sb(n, [P, CT, EXPERTS]) for n in ("lg", "lg_bias", "rank", "best", "second", "picked", "halves"))
        larger, equal = sb("larger", [P, CT, EXPERTS, EXPERTS]), sb("equal", [P, CT, EXPERTS, EXPERTS])
        lower = sb("lower", [P, EXPERTS, EXPERTS])
        comb_s = sb("comb_s", [P, CHUNKS, CT, EXPERTS])

        psum = es.enter_context(nc.psum_tensor("psum", [P, 8, 512], f32))
        bank = [psum[:, i, :] for i in range(8)]
        max_scores = psum[0:PAIR, 0:TPS, 0:RW]

        x_loaded = [sem(f"x_loaded{c}") for c in range(CHUNKS)]
        fold_loaded, w_loaded, moe_small_loaded = (sem(n) for n in ("fold_loaded", "w_loaded", "moe_small_loaded"))
        t_loaded = [sem(f"t_loaded{i}") for i in range(2)]
        n_loaded = [sem(f"n_loaded{i}") for i in range(2)]
        w1_loaded, w2_loaded = sem("w1_loaded"), sem("w2_loaded")
        consts_made, pool_step = sem("consts_made"), sem("pool_step")
        vec_step = sem("vec_step")
        folds_mm, folds_done, gates_done, rows_gated = (sem(n) for n in ("folds_mm", "folds_done", "gates_done", "rows_gated"))
        var_ready, scale_ready, normed = ([sem(f"{n}{k}") for k in range(5)] for n in ("var_ready", "scale_ready", "normed"))
        y_tr, y_tr_evac, sa_mm, sa_added, z_tr, z_tr_evac = (sem(n) for n in ("y_tr", "y_tr_evac", "sa_mm", "sa_added", "z_tr", "z_tr_evac"))
        q_mm, q_hi_done, q_lo_done = sem("q_mm"), sem("q_hi_done"), sem("q_lo_done")
        max_mm, max_read, shift_ready = sem("max_mm"), sem("max_read"), sem("shift_ready")
        score_mm, phi_done, plo_done, p_added = sem("score_mm"), sem("phi_done"), sem("plo_done"), sem("p_added")
        pv_mm, ctx_copied, p_sum_mm, inv_ready, inv_diag_ready = (sem(n) for n in ("pv_mm", "ctx_copied", "p_sum_mm", "inv_ready", "inv_diag_ready"))
        inv_mm, sum_done = sem("inv_mm"), sem("sum_done")
        thi_done, tlo_done, nhi_done, nlo_done = sem("thi_done"), sem("tlo_done"), sem("nhi_done"), sem("nlo_done")
        x_biased = sem("x_biased")
        ca_mm, ca_added, ca_back, x2_tr, x2_tr_evac = (sem(n) for n in ("ca_mm", "ca_added", "ca_back", "x2_tr", "x2_tr_evac"))
        ff_back = sem("ff_back")
        ff1_mm, ff1_act, ff2_mm, ff2_added = sem("ff1_mm"), sem("ff1_act"), sem("ff2_mm"), sem("ff2_added")
        w_split, b1_mm, b1_done = sem("w_split"), sem("b1_mm"), sem("b1_done")
        b2_cleared, b2_loaded, b2_ready = sem("b2_cleared"), sem("b2_loaded"), sem("b2_ready")
        hid_mm, gelu_done, hhi_done, hlo_done = sem("hid_mm"), sem("gelu_done"), sem("hhi_done"), sem("hlo_done")
        y_mm, acc_done, y_saved = sem("y_mm"), sem("acc_done"), sem("y_saved")
        e_stats, e_normable, e_normed, e_step, route_step = (sem(n) for n in ("e_stats", "e_normable", "e_normed", "e_step", "route_step"))
        xt_mm, xthi_done, xtlo_done, logit_mm = (sem(n) for n in ("xt_mm", "xthi_done", "xtlo_done", "logit_mm"))
        lg_ready, gap_ready, gate_tanh, comb_ready = (sem(n) for n in ("lg_ready", "gap_ready", "gate_tanh", "comb_ready"))
        out_ready, out_stored = sem("out_ready"), sem("out_stored")

        fold_loads = [
            (sa_wv_s[:], sa_wv), (sa_wot_s[:], sa_wot), (sa_bv_s[:], sa_bv), (sa_bias[:], sa_bo.to_broadcast([P, P])),
            (wq_s[:], wq), (wk_s[:], wk), (wv_s[:], wv), (wo_s[:], wot_h), (bq_s[:], bq), (bv_s[:], bv), (wot_s[:], wot),
            (ca_bias[:], bo), (rw_s[:], rw), (gates[:, 0:1], g_xattn.to_broadcast([P, 1])), (gates[:, 1:2], g_ffn.to_broadcast([P, 1])),
            (g3_row[:], ln3_g.to_broadcast([P, P])), (b3_row[:], ln3_b.to_broadcast([P, P])),
        ]
        small_loads = [
            (ln1_s[:], ln1), (l1_s[:], l1t), (l1b_s[:], l1b), (l2_s[:], l2t.rearrange("(q p) o -> p q o", p=P)), (l2b_s[:], l2b),
            (ln2_s[:], ln2), (rb_s[:], rb.to_broadcast([P, LAYERS * EXPERTS]).rearrange("p (l e) -> p l e", l=LAYERS)),
        ]
        moe_small = [(moe_g_s[:], moe_g), (moe_b_s[:], moe_b), (b1_s[:], b1)]
        LN_IN, LN_ONE, LN_TWO, LN_THREE, LN_OUTER = range(5)
        LN_SLOT = (0, 1, 0, 1, 2)
        BR = 32

        def chunk(c):
            return slice(CT * c, CT * (c + 1)) if is_int(c) else bass.ds(c * CT, CT)

        def tiles_of(bank_i):
            return bank[bank_i][0:TP, :].rearrange("p (t c) -> p t c", t=CT)

        def last_count(l, g, e):
            return g * EXPERTS + (CHUNKS * EXPERTS * l + e)

        def expert_groups(engine, body):
            for l in range(LAYERS):
                peeled = 2 if l == LAYERS - 1 else 1
                for g in range(peeled):
                    body(l, g)
                with engine.Fori(peeled, CHUNKS) as g:
                    body(l, g)

        def chained(engine, s, base):
            done = [0]

            def link(ins):
                done[0] += 1
                ins.then_inc(s, 1)
                engine.wait_ge(s, base + done[0])
            return link

        def follower(l, g):
            if is_int(g, 0):
                return CHUNKS * l + CHUNKS - 1, l, CHUNKS - 1
            if l == LAYERS - 1:
                return None
            return g + (CHUNKS * (l + 1) - 1), l + 1, g - 1

        block = es.enter_context(nc.Block())

        def seq_pairs(engine, step):
            step(0, 0)
            step(1, 1)
            with engine.Fori(1, B // 2 - 1) as i:
                for par in range(2):
                    step(i * 2 + par, par)
            step(B - 2, 0)
            step(B - 1, 1)

        def is_int(b, v=None):
            return type(b) is int and (v is None or b == v)

        def before(b, par, j):
            return (b, par, j - 1) if j else (b - 1, 1 - par, NCH - 1)

        ADDS = KT - 1

        def adds(b, j):
            return b * ADDS + (TPS * (j + 1) - 1)

        def context_sums(b):
            return ctx_sum[:, b, :, :] if is_int(b) else ctx_sum[:, bass.ds(b, 1), :, :].rearrange("p o h n -> p (o h) n")

        @block.sync
        def _(sp):
            x_v = x.rearrange("(t p) c -> p t c", p=TP)
            for c in range(CHUNKS):
                sp.dma_start(x_tm[0:TP, chunk(c), :], x_v[:, chunk(c), :]).then_inc(x_loaded[c], 16)
            for dst, src in small_loads:
                sp.dma_start(dst, src).then_inc(w_loaded, 16)
            for dst, src in moe_small:
                sp.dma_start(dst, src).then_inc(moe_small_loaded, 16)

            def load_t(b, par):
                if not is_int(b) or b >= 2:
                    sp.wait_ge(tlo_done, (b - 1) * NCH)
                sp.dma_start(t32[par][:], ctx_t[b] if is_int(b) else ctx_t[bass.ds(b, 1), :, :].rearrange("o p n -> (o p) n")).then_inc(t_loaded[par], 16)

            def load_n(b, par):
                if not is_int(b) or b >= 2:
                    sp.wait_ge(nlo_done, b - 1)
                else:
                    sp.wait_ge(z_tr, CHUNKS)
                sp.dma_start(n32[par][0:KP, :], ctx_n[b] if is_int(b) else ctx_n[bass.ds(b, 1), :, :].rearrange("o p n -> (o p) n")).then_inc(n_loaded[par], 16)
            load_t(0, 0)
            load_t(1, 1)
            sp.dma_start(w1_raw[:], w1[0]).then_inc(w1_loaded, 16)
            sp.dma_start(w2_raw[:], w2[0]).then_inc(w2_loaded, 16)
            load_n(0, 0)
            load_n(1, 1)
            with sp.Fori(1, B // 2) as i:
                for par in range(2):
                    load_t(i * 2 + par, par)
                    load_n(i * 2 + par, par)
            sp.wait_ge(b2_cleared, LAYERS)
            for l in range(LAYERS):
                for row in (0, BR):
                    sp.dma_start(b2_raw[l][row:row + 1, :], b2[l:l + 1, :]).then_inc(b2_loaded, 16)
            for l in range(1, LAYERS):
                sp.wait_ge(w_split, 2 * EXPERTS * l)
                sp.dma_start(w1_raw[:], w1[l]).then_inc(w1_loaded, 16)
                sp.dma_start(w2_raw[:], w2[l]).then_inc(w2_loaded, 16)
            out_v = out.rearrange("(t p) c -> p t c", p=TP)
            for g in range(CHUNKS):
                sp.wait_ge(out_ready, g + 1)
                sp.dma_start(out_v[:, chunk(g), :], x_tm[0:TP, chunk(g), :]).then_inc(out_stored, 16)
            sp.wait_ge(out_stored, 16 * CHUNKS)

        @block.gpsimd
        def _(pool):
            steps = [0]

            def step(ins):
                steps[0] += 1
                ins.then_inc(pool_step, 1)
                pool.wait_ge(pool_step, steps[0])

            step(nc.gpsimd.memset(ident[:], 0.0))
            step(nc.gpsimd.affine_select(out=ident[:], in_=ident[:], compare_op=ALU.not_equal, fill=1.0, base=0,
                                         pattern=[[-1, P]], channel_multiplier=1))
            nc.gpsimd.tensor_copy(ident_b[:], ident[:]).then_inc(consts_made, 1)
            nc.gpsimd.memset(ones32[:], 1.0).then_inc(consts_made, 1)
            nc.gpsimd.memset(ones_b[:], 1.0).then_inc(consts_made, 1)
            nc.gpsimd.memset(ones_h[:], 1.0).then_inc(consts_made, 1)
            step(nc.gpsimd.memset(lower[:], 0.0))
            for e in range(1, EXPERTS):
                nc.gpsimd.memset(lower[:, e, 0:e], 1.0)
            step(nc.gpsimd.memset(neghalf[:], -0.5))
            for i in range(2):
                nc.gpsimd.memset(t_hi[i][:, NKEY:TPAD], 0.0).then_inc(consts_made, 1)
                nc.gpsimd.memset(t_lo[i][:, NKEY:TPAD], 0.0).then_inc(consts_made, 1)

            T = nc.gpsimd.tensor_tensor

            def scale(k, c):
                at = LN_SLOT[k], slice(CT * c, CT * (c + 1))
                pool.wait_ge(var_ready[k], c + 1)
                step(T(ln_scale[0:TP, *at], ln_var[0:TP, *at], neghalf[0:TP, :], ALU.pow))
                T(ln_shift[0:TP, *at], ln_neg[0:TP, *at], ln_scale[0:TP, *at], mul).then_inc(scale_ready[k], 1)

            for c in range(CHUNKS):
                scale(LN_IN, c)
            for c in range(CHUNKS):
                scale(LN_ONE, c)
            pool.wait_ge(rows_gated, 1)
            pool.wait_ge(normed[LN_IN], CHUNKS)
            T(x_tm[0:TP], x_tm[0:TP], b3_row[0:TP, None, :].to_broadcast([TP, TILES, P]), add).then_inc(x_biased, 1)

            def split_piece(l, k):
                s, e = l % 2, k % EXPERTS
                first = k < EXPERTS
                raw = w1_raw[:, e, :] if first else w2_raw[:, e * FT:(e + 1) * FT, :].rearrange("p q c -> p (q c)")
                hi, lo = (w1_hi[s], w1_lo[s]) if first else (w2_hi[s], w2_lo[s])
                cols = slice(e * FF, (e + 1) * FF)
                gain = moe_g_s[:, EXPERTS * l + e:EXPERTS * l + e + 1] if first else 1.0
                nc.gpsimd.tensor_scalar(hi[:, cols], raw, gain, WS, mul, mul)
                step(nc.gpsimd.tensor_scalar(raw, raw, gain, WS, mul, mul))
                last = nc.gpsimd.tensor_tensor(lo[:, cols], raw, hi[:, cols], sub)
                last.then_inc(w_split, 1)

            def split_share(l, g):
                for k in (2 * g, 2 * g + 1):
                    split_piece(l, k)

            def split_ready(l):
                pool.wait_ge(w1_loaded, 16 * (l + 1))
                pool.wait_ge(w2_loaded, 16 * (l + 1))
                pool.wait_ge(b1_mm, l + 1)
                if l == 0:
                    pool.wait_ge(plo_done, B * NCH)
                elif l == 1:
                    pool.wait_ge(ff2_mm, CHUNKS)
                else:
                    pool.wait_ge(y_mm, CHUNKS * EXPERTS * (l - 1))

            def split_n(b, par):
                pool.wait_ge(nhi_done, b + 1)
                nc.gpsimd.tensor_tensor(n_lo[par][0:KP, :, :].rearrange("p t c -> p (t c)"), n32[par][0:KP, :],
                                        n_hi[par][0:KP, :, :].rearrange("p t c -> p (t c)"), sub).then_inc(nlo_done, 1)

            def sequence(b, par):
                total = p_sum[par][0:KP, :]
                for j in range(NCH):
                    for i in range(TPS):
                        t = TPS * j + i
                        if t == 0:
                            continue
                        pool.wait_ge(phi_done, b * KT + (t + 1))
                        tile = p32[j % 2][0:KP, i, :]
                        if t == 1:
                            if not (is_int(b) and b < 2):
                                pool.wait_ge(p_sum_mm, b - 1)
                            nc.gpsimd.tensor_tensor(total, p32[0][0:KP, 0, :], tile, add).then_inc(p_added, 1)
                        else:
                            pool.wait_ge(p_added, b * ADDS + (t - 1))
                            nc.gpsimd.tensor_tensor(total, total, tile, add).then_inc(p_added, 1)
                    if j == 1 and not is_int(b, B - 1):
                        split_n(b + 1, 1 - par)

            split_n(0, 0)
            seq_pairs(pool, sequence)

            pool.wait_ge(pv_mm, B * NCH)
            for l in range(LAYERS):
                nc.gpsimd.memset(b2_raw[l][0:BR + 1, :], 0.0).then_inc(b2_cleared, 1)

            TS = nc.gpsimd.tensor_scalar
            E_LINKS = 5

            def e_scale_of(m, l):
                link = chained(pool, e_step, m * E_LINKS)
                a = slice(0, TP)
                pool.wait_ge(e_stats, m + 1)
                T(m_sum[a], e_stats_s[a, :, 1], e_stats_s[a, :, 4], add)
                T(m_diff[a], e_stats_s[a, :, 1], e_stats_s[a, :, 4], sub)
                link(T(v_sum[a], e_stats_s[a, :, 2], e_stats_s[a, :, 5], add))
                TS(m_diff[a], m_diff[a], 0.5, None, mul)
                TS(e_neg[a], m_sum[a], -0.5, None, mul)
                TS(e_mean[a], m_sum[a], 0.5, None, mul)
                link(TS(v_sum[a], v_sum[a], 1.0 / P, EPS, mul, add))
                T(lg_bias[a], e_mean[a, :, None].to_broadcast(te), rw_sum[a, l:l + 1, :].to_broadcast(te), mul)
                link(T(m_diff[a], m_diff[a], m_diff[a], mul))
                T(lg_bias[a], lg_bias[a], rb_s[a, l:l + 1, :].to_broadcast(te), add)
                link(T(e_var[a], m_diff[a], v_sum[a], add))
                link(T(e_scale[a], e_var[a], neghalf[a], ALU.pow))
                T(e_std[a], e_var[a], e_scale[a], mul)
                T(e_shift[a], e_neg[a], e_scale[a], mul).then_inc(e_normable, 1)

            pool.wait_ge(moe_small_loaded, 16 * len(moe_small))
            pool.wait_ge(w_loaded, 16 * len(small_loads))
            split_ready(0)
            PIECES = ((0, 1), (2, 3), (4,), (5,), (6, 7))
            for s in range(CHUNKS + 1):
                if s >= 2:
                    scale(LN_THREE, s - 2)
                    scale(LN_OUTER, s - 2)
                if s >= 2:
                    e_scale_of(s - 2, 0)
                for k in PIECES[s]:
                    split_piece(0, k)
                if s < CHUNKS:
                    scale(LN_TWO, s)
            scale(LN_THREE, CHUNKS - 1)
            scale(LN_OUTER, CHUNKS - 1)

            def group(l, g):
                f = follower(l, g)
                if f is None:
                    return
                e_scale_of(f[0], f[1])
                if l < LAYERS - 1:
                    if is_int(g, 0):
                        split_ready(l + 1)
                    split_share(l + 1, g)

            for l in range(LAYERS):
                group(l, 0)
                if l < LAYERS - 1:
                    for g in range(1, CHUNKS):
                        group(l, g)

        @block.scalar
        def _(act):
            for dst, src in fold_loads:
                act.dma_start(dst, src).then_inc(fold_loaded, 16)

            def normalise(k, c, src, dst):
                act.wait_ge(scale_ready[k], c + 1)
                for i in range(CT):
                    t = CT * c + i
                    last = nc.scalar.activation(dst[0:TP, t, :], src(t, i), ACT.Identity, bias=ln_shift[0:TP, LN_SLOT[k], t:t + 1],
                                                scale=ln_scale[0:TP, LN_SLOT[k], t:t + 1])
                last.then_inc(normed[k], 1)

            def gained(c, bank_i, gain, s):
                a = {} if gain is None else {"scale": gain[:, 0:1], "bias": gain[:, 1:2]}
                nc.scalar.activation(f_t[:, c * CW:(c + 1) * CW], bank[bank_i][:, 0:CW], ACT.Identity, **a).then_inc(s, 1)

            def high_queries(c, h0, h1):
                for h in range(h0, h1):
                    k = c * HEADS + h
                    act.wait_ge(q_mm, k + 1)
                    nc.scalar.activation(q_parts[:, c * CB:(c + 1) * CB, 0, h * NQ:(h + 1) * NQ],
                                         bank[4 + k % 4][:, 0:CW].rearrange("p (b n) -> p b n", b=CB), ACT.Identity,
                                         bias=q_bias[:, h:h + 1]).then_inc(q_hi_done, 1)

            def split_t(b, par, j):
                if j == 0:
                    act.wait_ge(t_loaded[par], 16 * (b // 2 + 1) if is_int(b) else (b - par) * 8 + 16)
                nc.scalar.copy(t_hi[par][:, j * SW:(j + 1) * SW], t32[par][:, j * SW:(j + 1) * SW]).then_inc(thi_done, 1)

            def copy_sums(b):
                act.wait_ge(pv_mm, b * NCH + NCH)
                nc.scalar.copy(context_sums(b), bank[6][:, 0:QW].rearrange("p (h n) -> p h n", h=HEADS)).then_inc(ctx_copied, 1)

            def split_n(b, par):
                act.wait_ge(n_loaded[par], 16 * (b // 2 + 1) if is_int(b) else (b - par) * 8 + 16)
                nc.scalar.copy(n_hi[par][0:KP, :, :].rearrange("p t c -> p (t c)"), n32[par][0:KP, :]).then_inc(nhi_done, 1)

            for c in range(CHUNKS):
                normalise(LN_IN, c, lambda t, i: x_tm[0:TP, t, :], y_tm)
            act.wait_ge(fold_loaded, 16 * len(fold_loads))
            nc.scalar.activation(gates[:], gates[:], ACT.Tanh).then_inc(gates_done, 1)
            act.wait_ge(w_loaded, 16 * len(small_loads))
            act.wait_ge(folds_done, 1)
            for s in range(CHUNKS + 2):
                if s < CHUNKS:
                    act.wait_ge(y_tr, s + 1)
                    gained(s, 0, None, y_tr_evac)
                if s < 2:
                    for j in range(NCH):
                        split_t(s, s, j)
                if s >= 2:
                    high_queries(s - 2, 0, HEADS // 2)
                if 1 <= s <= CHUNKS:
                    normalise(LN_ONE, s - 1, lambda t, i: z_tm[0:TP, t, :], z_tm)
                if s >= 2:
                    high_queries(s - 2, HEADS // 2, HEADS)
                if 1 <= s <= CHUNKS:
                    act.wait_ge(z_tr, s)
                    gained(s - 1, 2, ln1_s, z_tr_evac)
            split_n(0, 0)

            def sequence(b, par):
                for j in range(NCH):
                    ring = j % 2
                    if j == 1 and not is_int(b, 0):
                        copy_sums(b - 1)
                    if not (is_int(b, 0) and j < 2):
                        act.wait_ge(pv_mm, b * NCH + (j - 1))
                        act.wait_ge(p_added, adds(b, j - 2) if j >= 2 else adds(b - 1, j + 2))
                    for i in range(TPS):
                        t = TPS * j + i
                        act.wait_ge(score_mm, b * KT + (t + 1))
                        nc.scalar.activation(p32[ring][0:KP, i, :], bank[3 + i][0:KP, 0:QW], ACT.Exp)
                        nc.scalar.activation(p_hi[ring][0:KP, i, :], bank[3 + i][0:KP, 0:QW], ACT.Exp).then_inc(phi_done, 1)
                    if not (is_int(b) and b >= B - 2):
                        split_t(b + 2, par, j)
                    if j == 1 and not is_int(b, B - 1):
                        split_n(b + 1, 1 - par)

            seq_pairs(act, sequence)
            copy_sums(B - 1)

            def split_xt(m, g):
                act.wait_ge(xt_mm, m + 1)
                nc.scalar.copy(xt_hi[:, bass.ds(g * CW, CW)], bank[6][:, 0:CW]).then_inc(xthi_done, 1)

            def normalise_e(m, src):
                act.wait_ge(e_normable, m + 1)
                if not is_int(m, 0):
                    act.wait_ge(xt_mm, m)
                for i in range(CT):
                    last = nc.scalar.activation(z_grp[0:TP, i, :], src(i), ACT.Identity, bias=e_shift[0:TP, i:i + 1],
                                                scale=e_scale[0:TP, i:i + 1])
                last.then_inc(e_normed, 1)

            def gate(m):
                act.wait_ge(gap_ready, m + 1)
                nc.scalar.activation(gap[0:TP], gap[0:TP], ACT.Tanh, scale=0.5).then_inc(gate_tanh, 1)

            def bank_tiles(i_bank):
                return lambda t, i: bank[i_bank][0:TP, i * P:(i + 1) * P]

            for s in range(CHUNKS + 1):
                if s >= 2:
                    normalise(LN_THREE, s - 2, bank_tiles(5), z_tm)
                if s >= 3:
                    split_xt(s - 3, s - 3)
                if s >= 1:
                    act.wait_ge(x2_tr, s)
                    gained(s - 1, 2, ln2_s, x2_tr_evac)
                    for q in range(FT):
                        k = (s - 1) * FT + q
                        act.wait_ge(ff1_mm, k + 1)
                        nc.scalar.activation(ffh[s - 1][:, q, :], bank[3 + k % 2][:, 0:CW], ACT.Relu, bias=l1b_s[:, q:q + 1]).then_inc(ff1_act, 1)
                if s >= 2:
                    normalise(LN_OUTER, s - 2, lambda t, i: x_tm[0:TP, t, :], y_tm)
                if s >= 3:
                    gate(s - 3)
                if s < CHUNKS:
                    normalise(LN_TWO, s, bank_tiles(1), z_tm)
                if s >= 2:
                    normalise_e(s - 2, lambda i: y_tm[0:TP, CT * (s - 2) + i, :])
            normalise(LN_THREE, CHUNKS - 1, bank_tiles(5), z_tm)
            act.wait_ge(ff2_mm, CHUNKS)

            def unit(l, g, e):
                u, par = last_count(l, g, e), e % 2
                first_use = is_int(u) and u < 2
                if e == 0 and is_int(g, 0):
                    act.wait_ge(b1_done, l + 1)
                if not first_use:
                    act.wait_ge(hlo_done, u - 1)
                for q in range(FT):
                    k = e * FT + q
                    act.wait_ge(hid_mm, u * FT + (q + 1))
                    nc.scalar.activation(h32[par][:, q, :], bank[q][:, 0:CW], ACT.Gelu, scale=1.0 / WS,
                                         bias=b1_fold[l % 2][:, k:k + 1]).then_inc(gelu_done, 1)
                act.wait_ge(gelu_done, u * FT + FT)
                if not first_use:
                    act.wait_ge(y_mm, u - 1)
                nc.scalar.copy(h_hi[par], h32[par]).then_inc(hhi_done, 1)

            def group(l, g):
                f = follower(l, g)
                start = l == 0 and is_int(g, 0)
                for e in range(EXPERTS):
                    if start and e == 1:
                        split_xt(CHUNKS - 2, CHUNKS - 2)
                    if e == 3 and f is not None:
                        split_xt(f[0], f[2])
                    unit(l, g, e)
                    if start:
                        if e == 0:
                            normalise(LN_OUTER, CHUNKS - 1, lambda t, i: x_tm[0:TP, t, :], y_tm)
                        if e == 1:
                            gate(CHUNKS - 2)
                        if e == 2:
                            normalise_e(CHUNKS - 1, lambda i: y_tm[0:TP, CT * (CHUNKS - 1) + i, :])
                    if e == 3 and f is not None:
                        gate(f[0])
                    if start:
                        continue
                    if e == 1 and f is not None:
                        act.wait_ge(acc_done, last_count(l, g, 0))
                        nc.scalar.copy(y_tm[0:TP, chunk(f[2]), :], y_grp[0:TP]).then_inc(y_saved, 1)
                    if e == 2 and f is not None:
                        normalise_e(f[0], lambda i: y_grp[0:TP, i, :])

            expert_groups(act, group)

        @block.vector
        def _(dve):
            steps = [0]

            def step(ins):
                steps[0] += 1
                ins.then_inc(vec_step, 1)
                dve.wait_ge(vec_step, steps[0])

            V = nc.vector

            def variances(k, c, src):
                for i in range(CT):
                    last = V.bn_stats(stats[0:TP, i, :], src(CT * c + i, i))
                step(last)
                for i in range(CT):
                    last = V.bn_aggr(mv[0:TP, i, :], stats[0:TP, i, :])
                step(last)
                at = LN_SLOT[k], slice(CT * c, CT * (c + 1))
                V.tensor_scalar(ln_neg[0:TP, *at], mv[0:TP, :, 0], -1.0, None, mul)
                V.tensor_scalar(ln_var[0:TP, *at], mv[0:TP, :, 1], EPS, None, add).then_inc(var_ready[k], 1)

            for c in range(CHUNKS):
                dve.wait_ge(x_loaded[c], 16)
                variances(LN_IN, c, lambda t, i: x_tm[0:TP, t, :])

            dve.wait_ge(fold_loaded, 16 * len(fold_loads))
            dve.wait_ge(folds_mm, 1)
            V.tensor_copy(m_sa[:], bank[0][:, 0:128])
            V.tensor_tensor(sa_bias[:], bank[0][:, 128:256], sa_bias[:], add)
            V.tensor_tensor(ca_bias[:], bank[0][:, 256:257], ca_bias[:], add)
            V.tensor_copy(rw_sum[:].rearrange("p l e -> p (l e)"), bank[0][:, 260:276])
            V.tensor_scalar(q_bias[:], bank[0][:, 280:288], HD ** -0.5, None, mul)
            for i in range(2):
                V.tensor_scalar(a_qk[:, 4 * i:4 * i + 4, :], bank[1 + i][:, :].rearrange("p (h c) -> p h c", h=4), HD ** -0.5, None, mul)
                V.tensor_copy(a_vo[:, 4 * i:4 * i + 4, :], bank[3 + i][:, :].rearrange("p (h c) -> p h c", h=4))
            dve.wait_ge(gates_done, 1)
            V.tensor_scalar(g3_row[:], g3_row[:], gates[:, 0:1], None, mul)
            V.tensor_scalar(b3_row[:], b3_row[:], gates[:, 0:1], None, mul).then_inc(rows_gated, 1)
            step(V.tensor_scalar(rw_s[:], rw_s[:], WS, None, mul))
            step(V.tensor_copy(rw_hi[:], rw_s[:]))
            V.tensor_tensor(rw_lo[:], rw_s[:], rw_hi[:], sub).then_inc(folds_done, 1)
            dve.wait_ge(folds_done, 1)

            def low_queries(c, h0, h1):
                for h in range(h0, h1):
                    k = c * HEADS + h
                    dve.wait_ge(q_hi_done, k + 1)
                    V.scalar_tensor_tensor(out=q_parts[:, c * CB:(c + 1) * CB, 1, h * NQ:(h + 1) * NQ],
                                           in0=bank[4 + k % 4][:, 0:CW].rearrange("p (b n) -> p b n", b=CB), scalar=q_bias[:, h:h + 1],
                                           in1=q_parts[:, c * CB:(c + 1) * CB, 0, h * NQ:(h + 1) * NQ],
                                           op0=add, op1=sub).then_inc(q_lo_done, 1)

            def split_t(b, par, j):
                dve.wait_ge(thi_done, b * NCH + (j + 1))
                V.tensor_tensor(t_lo[par][:, j * SW:(j + 1) * SW], t32[par][:, j * SW:(j + 1) * SW],
                                t_hi[par][:, j * SW:(j + 1) * SW], sub).then_inc(tlo_done, 1)

            dve.wait_ge(consts_made, 8)
            for s in range(CHUNKS + 2):
                if s < CHUNKS:
                    dve.wait_ge(normed[LN_IN], s + 1)
                    step(V.tensor_tensor(z_tm[0:TP, chunk(s), :], y_tm[0:TP, chunk(s), :],
                                         sa_bias[0:TP, None, :].to_broadcast([TP, CT, P]), add))
                if s >= 2:
                    low_queries(s - 2, 0, HEADS // 2)
                if s < CHUNKS:
                    dve.wait_ge(sa_mm, s + 1)
                    V.tensor_tensor(z_tm[0:TP, chunk(s), :], tiles_of(1), z_tm[0:TP, chunk(s), :], add).then_inc(sa_added, 1)
                    dve.wait_ge(sa_added, s + 1)
                if s >= 2:
                    low_queries(s - 2, HEADS // 2, HEADS)
                if s < CHUNKS:
                    variances(LN_ONE, s, lambda t, i: z_tm[0:TP, t, :])
                if s < 2:
                    for j in range(NCH):
                        split_t(s, s, j)

            def fold_b1(l):
                dve.wait_ge(b1_mm, l + 1)
                V.tensor_tensor(b1_fold[l % 2][:], bank[7][:, 256:256 + EXPERTS * FT], b1_s[:, l, :], add).then_inc(b1_done, 1)

            fold_b1(0)

            def maximum(b, par, j):
                dve.wait_ge(max_mm, b * NCH + (j + 1))
                V.tensor_reduce(out=nmax[0:PAIR, j:j + 1],
                                in_=max_scores, axis=AX.XY, op=ALU.max).then_inc(max_read, 1)
                dve.wait_ge(max_read, b * NCH + (j + 1))
                if j == 0 and not (is_int(b) and b < 2):
                    dve.wait_ge(score_mm, (b - 1) * KT)
                V.tensor_scalar(shift_d[par][0:PAIR, j * PAIR:(j + 1) * PAIR], ident_b[0:PAIR, 0:PAIR],
                                nmax[0:PAIR, j:j + 1], -1.0, mul, mul).then_inc(shift_ready, 1)

            def low_probs(b, j):
                ring = j % 2
                dve.wait_ge(phi_done, b * KT + TPS * (j + 1))
                V.tensor_tensor(p_lo[ring][0:KP, :, :].rearrange("p t w -> p (t w)"),
                                p32[ring][0:KP, :, :].rearrange("p t w -> p (t w)"),
                                p_hi[ring][0:KP, :, :].rearrange("p t w -> p (t w)"), sub).then_inc(plo_done, 1)

            def invert(b):
                dve.wait_ge(p_sum_mm, b + 1)
                V.reciprocal(inv_sum[0:PAIR, :], bank[7][0:PAIR, QW:QW + NCH]).then_inc(inv_ready, 1)
                dve.wait_ge(inv_ready, b + 1)
                blocks = [PAIR, NCH, PAIR]
                V.tensor_tensor(inv_diag[0:PAIR, :].rearrange("p (j w) -> p j w", j=NCH), ident[0:PAIR, None, 0:PAIR].to_broadcast(blocks),
                                inv_sum[0:PAIR, :, None].to_broadcast(blocks), mul).then_inc(inv_diag_ready, 1)

            def divide(b):
                dve.wait_ge(inv_mm, b + 1)
                dve.wait_ge(ctx_copied, b + 1)
                o = context_sums(b)
                V.tensor_tensor(o, bank[7][:, 0:QW].rearrange("p (h n) -> p h n", h=HEADS), o, mul).then_inc(sum_done, 1)

            for j in range(NCH):
                maximum(0, 0, j)

            def sequence(b, par):
                for j in range(NCH):
                    first = is_int(b, 0) and j == 0
                    pb, ppar, pj = before(b, par, j)
                    if not first:
                        low_probs(pb, pj)
                    if not is_int(b, B - 1):
                        maximum(b + 1, 1 - par, j)
                    if not first and not (is_int(pb) and pb >= B - 2):
                        split_t(pb + 2, ppar, pj)
                    if not is_int(b, 0):
                        if j == 1:
                            invert(b - 1)
                        if j == 3:
                            divide(b - 1)

            seq_pairs(dve, sequence)
            low_probs(B - 1, NCH - 1)
            invert(B - 1)
            divide(B - 1)

            def to_residual(c, bank_i, bias, s):
                V.scalar_tensor_tensor(out=f_t[:, c * CW:(c + 1) * CW], in0=bank[bank_i][:, 0:CW], scalar=bias[:, 0:1],
                                       in1=f_t[:, c * CW:(c + 1) * CW], op0=add, op1=add).then_inc(s, 1)

            def bank_tiles(i_bank):
                return lambda t, i: bank[i_bank][0:TP, i * P:(i + 1) * P]

            def outer_residual(c):
                dve.wait_ge(normed[LN_THREE], c + 1)
                z, xc = z_tm[0:TP, chunk(c), :], x_tm[0:TP, chunk(c), :]
                step(V.tensor_tensor(z, z, g3_row[0:TP, None, :].to_broadcast([TP, CT, P]), mul))
                if c == 0:
                    dve.wait_ge(x_biased, 1)
                step(V.tensor_tensor(xc, xc, z, add))
                variances(LN_OUTER, c, lambda t, i: x_tm[0:TP, t, :])

            def e_statistics(m, src):
                if not is_int(m, 0):
                    dve.wait_ge(e_normable, m)
                for i in range(CT):
                    last = V.bn_stats(e_stats_s[0:TP, i, :], src(i))
                last.then_inc(e_stats, 1)

            def split_xt(m, g):
                dve.wait_ge(xthi_done, m + 1)
                V.tensor_tensor(xt_lo[:, bass.ds(g * CW, CW)], bank[6][:, 0:CW], xt_hi[:, bass.ds(g * CW, CW)], sub).then_inc(xtlo_done, 1)

            RANK_LINKS, WEIGH_LINKS = 9, 2
            a = slice(0, TP)

            def rank_experts(m):
                link = chained(dve, route_step, m * (RANK_LINKS + WEIGH_LINKS))
                dve.wait_ge(logit_mm, m + 1)
                link(V.scalar_tensor_tensor(out=lg[a], in0=bank[7][a, 0:CT * EXPERTS].rearrange("p (t e) -> p t e", t=CT),
                                            scalar=1.0 / WS, in1=e_std[a, :, None].to_broadcast(te), op0=mul, op1=mul))
                last = V.tensor_tensor(lg[a], lg[a], lg_bias[a], add)
                last.then_inc(lg_ready, 1)
                dve.wait_ge(lg_ready, m + 1)
                other, own = lg[a, :, None, :].to_broadcast(pairs), lg[a, :, :, None].to_broadcast(pairs)
                V.tensor_tensor(larger[a], other, own, ALU.is_gt)
                link(V.tensor_tensor(equal[a], other, own, ALU.is_equal))
                link(V.tensor_tensor(equal[a], equal[a], lower[a, None, :, :].to_broadcast(pairs), mul))
                link(V.tensor_tensor(larger[a], larger[a], equal[a], add))
                link(V.tensor_reduce(out=rank[a], in_=larger[a], axis=AX.X, op=add))
                V.tensor_scalar(best[a], rank[a], 0.0, None, ALU.is_equal)
                link(V.tensor_scalar(second[a], rank[a], 1.0, None, ALU.is_equal))
                V.tensor_tensor(picked[a], best[a], second[a], add)
                link(V.tensor_tensor(best[a], best[a], second[a], sub))
                link(V.tensor_tensor(halves[a], best[a], lg[a], mul))
                link(V.tensor_tensor(halves[a, :, 0:2], halves[a, :, 0:2], halves[a, :, 2:4], add))
                V.tensor_tensor(gap[a], halves[a, :, 0], halves[a, :, 1], add).then_inc(gap_ready, 1)

            def weigh_experts(m, g):
                link = chained(dve, route_step, m * (RANK_LINKS + WEIGH_LINKS) + RANK_LINKS)
                dve.wait_ge(gate_tanh, m + 1)
                link(V.tensor_tensor(best[a], best[a], gap[a, :, None].to_broadcast(te), mul))
                link(V.tensor_tensor(best[a], best[a], picked[a], add))
                d = comb_s[a, g, :, :] if is_int(g) else comb_s[a, bass.ds(g, 1), :, :].rearrange("p o t e -> p (o t) e")
                V.tensor_scalar(d, best[a], 0.5 / WS, None, mul).then_inc(comb_ready, 1)

            def output_bias(l):
                if l == 0:
                    dve.wait_ge(b2_loaded, 16 * 2 * LAYERS)
                rows = slice(0, BR + 1)
                step(V.tensor_scalar(b2_raw[l][rows, :], b2_raw[l][rows, :], WS, None, mul))
                step(V.tensor_copy(b2_parts[l][rows, :], b2_raw[l][rows, :]))
                V.tensor_tensor(b2_parts[l][BR:BR + 1, :], b2_raw[l][BR:BR + 1, :], b2_parts[l][BR:BR + 1, :], sub).then_inc(b2_ready, 1)

            for s in range(CHUNKS + 1):
                if s >= 2:
                    outer_residual(s - 2)
                if s >= 3:
                    split_xt(s - 3, s - 3)
                if s < CHUNKS:
                    dve.wait_ge(ca_mm, s + 1)
                    to_residual(s, 0, ca_bias, ca_added)
                if s >= 3:
                    rank_experts(s - 3)
                if s >= 2:
                    dve.wait_ge(normed[LN_OUTER], s - 1)
                    e_statistics(s - 2, lambda i: y_tm[0:TP, CT * (s - 2) + i, :])
                if s < CHUNKS:
                    dve.wait_ge(ca_back, s + 1)
                    variances(LN_TWO, s, bank_tiles(1))
                if s >= 1:
                    dve.wait_ge(ff2_mm, s)
                    to_residual(s - 1, 2, l2b_s, ff2_added)
                    dve.wait_ge(ff_back, s)
                    variances(LN_THREE, s - 1, bank_tiles(5))
                if s < LAYERS:
                    output_bias(s)
                if s >= 3:
                    weigh_experts(s - 3, s - 3)
            outer_residual(CHUNKS - 1)

            def low_parts(l, g, e):
                u, par = last_count(l, g, e), e % 2
                dve.wait_ge(hhi_done, u + 1)
                V.tensor_tensor(h_lo[par], h32[par], h_hi[par], sub).then_inc(hlo_done, 1)

            def accumulate(l, g, e):
                u = last_count(l, g, e)
                dve.wait_ge(y_mm, u + 1)
                if e == 0:
                    dve.wait_ge(comb_ready, g + (CHUNKS * l + 1))
                    if l:
                        dve.wait_ge(y_saved, g + (CHUNKS * (l - 1) + 1))
                if e == EXPERTS - 1 and not (l == 0 and is_int(g, 0)):
                    dve.wait_ge(e_normed, CHUNKS * LAYERS if l == LAYERS - 1 else g + CHUNKS * (l + 1))
                for i in range(CT):
                    if is_int(g):
                        yt, cs = y_tm[0:TP, CT * g + i, :], comb_s[0:TP, g, i, e:e + 1]
                    else:
                        yt = y_tm[0:TP, bass.ds(g * CT + i, 1), :].rearrange("p o c -> p (o c)")
                        cs = comb_s[0:TP, bass.ds(g, 1), i, e:e + 1].rearrange("p o c -> p (o c)")
                    last = V.scalar_tensor_tensor(out=yt if e < EXPERTS - 1 else y_grp[0:TP, i, :], in0=bank[4 + e % 2][0:TP, i * P:(i + 1) * P],
                                                  scalar=cs, in1=yt, op0=mul, op1=add)
                last.then_inc(acc_done, 1)
                dve.wait_ge(acc_done, u + 1)

            def finish(g):
                V.scalar_tensor_tensor(out=x_tm[0:TP, chunk(g), :], in0=y_grp[0:TP],
                                       scalar=gates[0:TP, 1:2], in1=x_tm[0:TP, chunk(g), :], op0=mul, op1=add).then_inc(out_ready, 1)

            def group(l, g):
                f = follower(l, g)
                start = l == 0 and is_int(g, 0)
                for e in range(EXPERTS):
                    if start and e == 1:
                        split_xt(CHUNKS - 2, CHUNKS - 2)
                        rank_experts(CHUNKS - 2)
                    if e == 3 and f is not None:
                        split_xt(f[0], f[2])
                        rank_experts(f[0])
                    low_parts(l, g, e)
                    if e:
                        accumulate(l, g, e - 1)
                    elif not start:
                        accumulate(l - 1 if is_int(g, 0) else l, CHUNKS - 1 if is_int(g, 0) else g - 1, EXPERTS - 1)
                        if f is None:
                            finish(g - 1)
                        else:
                            e_statistics(f[0], lambda i: y_grp[0:TP, i, :])
                    if start and e == 1:
                        weigh_experts(CHUNKS - 2, CHUNKS - 2)
                    if e == 3 and f is not None:
                        weigh_experts(f[0], f[2])
                    if start and e == 1:
                        dve.wait_ge(normed[LN_OUTER], CHUNKS)
                        e_statistics(CHUNKS - 1, lambda i: y_tm[0:TP, CT * (CHUNKS - 1) + i, :])
                    if e == 1 and is_int(g, 0) and l < LAYERS - 1:
                        fold_b1(l + 1)

            expert_groups(dve, group)
            accumulate(LAYERS - 1, CHUNKS - 1, EXPERTS - 1)
            finish(CHUNKS - 1)

        @block.tensor
        def _(pe):
            def mm(dst, lhs, rhs, start=True, stop=True):
                return nc.tensor.matmul(dst, lhs, rhs, start=start, stop=stop)

            pe.wait_ge(fold_loaded, 16 * len(fold_loads))
            pe.wait_ge(consts_made, 8)
            mm(bank[0][:, 0:128], sa_wv_s[:], sa_wot_s[:])
            mm(bank[0][:, 128:256], sa_bv_s[:, 0:1].to_broadcast([P, P]), sa_wot_s[:])
            mm(bank[0][:, 256:257], wot_s[:], bv_s[:])
            mm(bank[0][:, 260:276], ones32[:], rw_s[:])
            for h in range(HEADS):
                mm(bank[0][:, 280 + h:281 + h], wk_s[:, h, :], bq_s[:, h:h + 1])
                mm(bank[1 + h // 4][:, (h % 4) * P:(h % 4 + 1) * P], wq_s[:, h, :], wk_s[:, h, :])
                last = mm(bank[3 + h // 4][:, (h % 4) * P:(h % 4 + 1) * P], wv_s[:, h, :], wo_s[:, h, :])
            last.then_inc(folds_mm, 1)

            def to_features(c, src, bank_i, s):
                for i in range(CT):
                    last = nc.tensor.transpose(bank[bank_i][:, i * TP:(i + 1) * TP], src[0:TP, CT * c + i, :], ident[0:TP, 0:TP])
                last.then_inc(s, 1)

            def to_tokens(c, bank_i, s):
                for i in range(CT):
                    t = CT * c + i
                    last = nc.tensor.transpose(bank[bank_i][0:TP, i * P:(i + 1) * P], f_t[:, t * TP:(t + 1) * TP], ident[:])
                last.then_inc(s, 1)

            def fold_queries(c, h0, h1):
                for h in range(h0, h1):
                    k = c * HEADS + h
                    if k >= 4:
                        pe.wait_ge(q_lo_done, k - 3)
                    mm(bank[4 + k % 4][:, 0:CW], a_qk[:, h, :], f_t[:, c * CW:(c + 1) * CW]).then_inc(q_mm, 1)

            pe.wait_ge(folds_done, 1)
            for s in range(CHUNKS + 2):
                if s < CHUNKS:
                    pe.wait_ge(normed[LN_IN], s + 1)
                    if s:
                        pe.wait_ge(y_tr_evac, s)
                    to_features(s, y_tm, 0, y_tr)
                if s >= 2:
                    pe.wait_ge(z_tr_evac, s - 1)
                    fold_queries(s - 2, 0, HEADS // 2)
                if s < CHUNKS:
                    pe.wait_ge(y_tr_evac, s + 1)
                    if s:
                        pe.wait_ge(sa_added, s)
                    for i in range(CT):
                        t = CT * s + i
                        last = mm(bank[1][0:TP, i * P:(i + 1) * P], f_t[:, t * TP:(t + 1) * TP], m_sa[:])
                    last.then_inc(sa_mm, 1)
                if s >= 2:
                    fold_queries(s - 2, HEADS // 2, HEADS)
                if 1 <= s <= CHUNKS:
                    pe.wait_ge(normed[LN_ONE], s)
                    if s > 1:
                        pe.wait_ge(z_tr_evac, s - 1)
                    to_features(s - 1, z_tm, 2, z_tr)

            def fold_b1(l):
                pe.wait_ge(w1_loaded, 16 * (l + 1))
                if l == 0:
                    pe.wait_ge(moe_small_loaded, 16 * len(moe_small))
                for k in range(EXPERTS * FT):
                    e, q = divmod(k, FT)
                    last = mm(bank[7][:, 256 + k:257 + k], w1_raw[:, e, q * P:(q + 1) * P],
                              moe_b_s[:, EXPERTS * l + e:EXPERTS * l + e + 1])
                last.then_inc(b1_mm, 1)

            pe.wait_ge(q_lo_done, CHUNKS * HEADS)
            fold_b1(0)
            pe.wait_ge(b1_done, 1)

            def queries(b, s, w0, w):
                if is_int(b):
                    return q_parts[:, b, s, w0:w0 + w]
                return q_parts[:, bass.ds(b, 1), s, w0:w0 + w].rearrange("p o w -> p (o w)")

            def maximum(b, par, j):
                if j == 0:
                    pe.wait_ge(thi_done, (b + 1) * NCH)
                if not (is_int(b, 0) and j == 0):
                    pe.wait_ge(max_read, b * NCH + j)
                for r in range(TPS):
                    last = mm(psum[0:PAIR, r, 0:RW], queries(b, 0, j * PAIR, PAIR), t_hi[par][:, r * RW:(r + 1) * RW])
                last.then_inc(max_mm, 1)

            def scores(b, par, j):
                if j == 0:
                    pe.wait_ge(tlo_done, (b + 1) * NCH)
                    pe.wait_ge(shift_ready, (b + 1) * NCH)
                for i in range(TPS):
                    t = TPS * j + i
                    dst = bank[3 + i][:, 0:QW]
                    keys = slice(t * KP, t * KP + P)
                    if not (is_int(b, 0) and j == 0):
                        pe.wait_ge(phi_done, b * KT + (t - TPS + 1))
                    mm(dst, t_hi[par][:, keys], queries(b, 0, 0, QW), True, False)
                    mm(dst, t_hi[par][:, keys], queries(b, 1, 0, QW), False, False)
                    mm(dst, t_lo[par][:, keys], queries(b, 0, 0, QW), False, False)
                    mm(dst, ones_b[0:PAIR, :], shift_d[par][0:PAIR, :], False, True).then_inc(score_mm, 1)

            def weighted(b, par, j):
                ring = j % 2
                pe.wait_ge(plo_done, b * NCH + (j + 1))
                if j == 0:
                    pe.wait_ge(nlo_done, b + 1)
                    if not is_int(b, 0):
                        pe.wait_ge(ctx_copied, b)
                for i in range(TPS):
                    t = TPS * j + i
                    hi, lo = p_hi[ring][0:KP, i, :], p_lo[ring][0:KP, i, :]
                    first, end = t == 0, t == KT - 1
                    mm(bank[6][:, 0:QW], n_hi[par][0:KP, t, :], hi, first, False)
                    mm(bank[6][:, 0:QW], n_hi[par][0:KP, t, :], lo, False, False)
                    last = mm(bank[6][:, 0:QW], n_lo[par][0:KP, t, :], hi, False, end)
                last.then_inc(pv_mm, 1)

            def probability_sums(b, par):
                pe.wait_ge(p_added, b * ADDS + ADDS)
                if not (is_int(b) and b < 1):
                    pe.wait_ge(sum_done, b)
                for j in range(NCH):
                    last = mm(bank[7][0:PAIR, QW + j:QW + j + 1], p_sum[par][0:KP, j * PAIR:(j + 1) * PAIR], ones32[0:KP, 0:1])
                last.then_inc(p_sum_mm, 1)

            def spread_inverses(b):
                pe.wait_ge(inv_diag_ready, b + 1)
                mm(bank[7][:, 0:QW], ones32[0:PAIR, :], inv_diag[0:PAIR, :]).then_inc(inv_mm, 1)

            for j in range(NCH):
                maximum(0, 0, j)

            def sequence(b, par):
                for j in range(NCH):
                    if not is_int(b, B - 1):
                        maximum(b + 1, 1 - par, j)
                    if j == 2 and not is_int(b, 0):
                        spread_inverses(b - 1)
                    scores(b, par, j)
                    if not (is_int(b, 0) and j == 0):
                        weighted(*before(b, par, j))
                    if j == 0 and not is_int(b, 0):
                        probability_sums(b - 1, 1 - par)

            seq_pairs(pe, sequence)
            weighted(B - 1, 1, NCH - 1)
            probability_sums(B - 1, 1)
            spread_inverses(B - 1)

            def project(c, h0, h1):
                for h in range(h0, h1):
                    last = mm(bank[0][:, 0:CW], a_vo[:, h, :], ctx_sum[:, c * CB:(c + 1) * CB, h, :], h == 0, h == HEADS - 1)
                return last

            def transposes_e(m, g):
                pe.wait_ge(e_normed, m + 1)
                if not is_int(m, 0):
                    pe.wait_ge(xtlo_done, m)
                for i in range(CT):
                    last = nc.tensor.transpose(bank[6][:, i * TP:(i + 1) * TP], z_grp[0:TP, i, :], ident[0:TP, 0:TP])
                last.then_inc(xt_mm, 1)

            def logits(m, l, g):
                pe.wait_ge(xtlo_done, m + 1)
                if not is_int(m, 0):
                    pe.wait_ge(lg_ready, m)
                cols = slice(EXPERTS * l, EXPERTS * (l + 1))
                for i in range(CT):
                    dst = bank[7][0:TP, i * EXPERTS:(i + 1) * EXPERTS]
                    hi, lo = (v[:, bass.ds(g * CW + i * TP, TP)] for v in (xt_hi, xt_lo))
                    mm(dst, hi, rw_hi[:, cols], True, False)
                    mm(dst, hi, rw_lo[:, cols], False, False)
                    last = mm(dst, lo, rw_hi[:, cols], False, True)
                last.then_inc(logit_mm, 1)

            pe.wait_ge(max_read, B * NCH)
            for s in range(CHUNKS + 1):
                if s < CHUNKS:
                    pe.wait_ge(sum_done, (s + 1) * CB)
                    if s:
                        pe.wait_ge(ca_added, s)
                    project(s, 0, HEADS // 2)
                if s >= 3:
                    transposes_e(s - 3, s - 3)
                if s >= 1:
                    pe.wait_ge(normed[LN_TWO], s)
                    if s > 1:
                        pe.wait_ge(ff2_added, s - 1)
                    to_features(s - 1, z_tm, 2, x2_tr)
                if s < CHUNKS:
                    project(s, HEADS // 2, HEADS).then_inc(ca_mm, 1)
                if s >= 3:
                    logits(s - 3, 0, s - 3)
                if s >= 1:
                    pe.wait_ge(x2_tr_evac, s)
                    for q in range(FT):
                        k = (s - 1) * FT + q
                        if k >= 2:
                            pe.wait_ge(ff1_act, k - 1)
                        mm(bank[3 + k % 2][:, 0:CW], l1_s[:, q * P:(q + 1) * P], f_t[:, (s - 1) * CW:s * CW]).then_inc(ff1_mm, 1)
                if s < CHUNKS:
                    pe.wait_ge(ca_added, s + 1)
                    if s:
                        pe.wait_ge(normed[LN_TWO], s)
                    to_tokens(s, 1, ca_back)
                if s >= 1:
                    pe.wait_ge(ff1_act, s * FT)
                    for q in range(FT):
                        last = mm(bank[2][:, 0:CW], l2_s[:, q, :], ffh[s - 1][:, q, :], q == 0, q == FT - 1)
                    last.then_inc(ff2_mm, 1)
                    pe.wait_ge(ff2_added, s)
                    if s > 1:
                        pe.wait_ge(normed[LN_THREE], s - 1)
                    to_tokens(s - 1, 5, ff_back)

            def hidden(l, g, e):
                u, s = last_count(l, g, e), l % 2
                toks = bass.ds(g * CW, CW)
                for q in range(FT):
                    if not (is_int(u, 0)):
                        pe.wait_ge(gelu_done, u * FT + (q - FT + 1))
                    dst, w = bank[q][:, 0:CW], slice(e * FF + q * P, e * FF + (q + 1) * P)
                    mm(dst, w1_hi[s][:, w], xt_hi[:, toks], True, False)
                    mm(dst, w1_hi[s][:, w], xt_lo[:, toks], False, False)
                    mm(dst, w1_lo[s][:, w], xt_hi[:, toks], False, True).then_inc(hid_mm, 1)

            def output(l, g, e):
                u, s, par = last_count(l, g, e), l % 2, e % 2
                pe.wait_ge(hlo_done, u + 1)
                if not (is_int(u) and u < 2):
                    pe.wait_ge(acc_done, u - 1)
                for i in range(CT):
                    dst, toks = bank[4 + par][0:TP, i * P:(i + 1) * P], slice(i * TP, (i + 1) * TP)
                    mm(dst, ones_h[0:BR + 1, :], b2_parts[l][0:BR + 1, e * P:(e + 1) * P], True, False)
                    for q in range(FT):
                        w = slice((e * FT + q) * P, (e * FT + q + 1) * P)
                        mm(dst, h_hi[par][:, q, toks], w2_hi[s][:, w], False, False)
                        mm(dst, h_hi[par][:, q, toks], w2_lo[s][:, w], False, False)
                        last = mm(dst, h_lo[par][:, q, toks], w2_hi[s][:, w], False, q == FT - 1)
                last.then_inc(y_mm, 1)

            pe.wait_ge(normed[LN_THREE], CHUNKS)
            pe.wait_ge(b2_ready, LAYERS)

            def group(l, g):
                f = follower(l, g)
                start = l == 0 and is_int(g, 0)
                if is_int(g, 0):
                    pe.wait_ge(w_split, 2 * EXPERTS * (l + 1))
                for e in range(EXPERTS):
                    if start and e == 1:
                        transposes_e(CHUNKS - 2, CHUNKS - 2)
                    if e == 3 and f is not None:
                        transposes_e(f[0], f[2])
                    hidden(l, g, e)
                    if start and e == 1:
                        logits(CHUNKS - 2, 0, CHUNKS - 2)
                    if e == 3 and f is not None:
                        logits(*f)
                    if e:
                        output(l, g, e - 1)
                    elif not start:
                        output(l - 1 if is_int(g, 0) else l, CHUNKS - 1 if is_int(g, 0) else g - 1, EXPERTS - 1)
                    if e == 1 and is_int(g, 0) and l < LAYERS - 1:
                        pe.wait_ge(lg_ready, CHUNKS * l + CHUNKS - 1)
                        fold_b1(l + 1)
                        pe.wait_ge(b1_done, l + 2)

            expert_groups(pe, group)
            output(LAYERS - 1, CHUNKS - 1, EXPERTS - 1)


_OUT = (B, NQ, C)


def kernel(**inputs):
    import numpy as _np
    import concourse.bacc as _bacc
    from concourse import mybir as _mybir
    from concourse.bass_utils import run_bass_kernel_spmd as _run

    a = {k: _np.asarray(v) for k, v in inputs.items()}
    qkv_w, qkv_b = a["L0_xattn_qkv_w"], a["L0_xattn_qkv_b"]
    in_w, in_b = a["L0_xattn_in_proj_w"], a["L0_xattn_in_proj_b"]
    ctx, out_w = a["ctx_1024"], a["L0_xattn_mha_out_w"]

    def heads_first(w):
        return w.reshape(HEADS, HD, P).transpose(1, 0, 2)

    layout = {
        "x": a["x"].reshape(TOK, C),
        "ctx_n": ctx.reshape(B, KP, KT * C),
        "ctx_t": ctx.reshape(B, KP, KT, C).transpose(0, 3, 2, 1).reshape(B, C, NKEY),
        "g_xattn": a["g_xattn"].reshape(1, 1),
        "g_ffn": a["g_ffn"].reshape(1, 1),
        "sa_wv": qkv_w[2 * C:3 * C],
        "sa_bv": qkv_b[2 * C:3 * C].reshape(C, 1),
        "sa_wot": a["L0_xattn_sa_out_w"].T,
        "sa_bo": a["L0_xattn_sa_out_b"].reshape(1, C),
        "wq": heads_first(in_w[0:C]),
        "wk": heads_first(in_w[C:2 * C]),
        "wv": heads_first(in_w[2 * C:3 * C]),
        "bq": in_b[0:C].reshape(HEADS, HD).T,
        "bv": in_b[2 * C:3 * C].reshape(C, 1),
        "wot": out_w.T,
        "wot_h": heads_first(out_w.T),
        "bo": a["L0_xattn_mha_out_b"].reshape(C, 1),
        "l1t": a["L0_xattn_lin1_w"].T,
        "l1b": a["L0_xattn_lin1_b"].reshape(FT, P).T,
        "l2t": a["L0_xattn_lin2_w"].T,
        "l2b": a["L0_xattn_lin2_b"].reshape(C, 1),
        "ln1": _np.stack([a["L0_xattn_ln1_g"], a["L0_xattn_ln1_b"]], 1),
        "ln2": _np.stack([a["L0_xattn_ln2_g"], a["L0_xattn_ln2_b"]], 1),
        "ln3_g": a["L0_xattn_ln3_g"].reshape(1, C),
        "ln3_b": a["L0_xattn_ln3_b"].reshape(1, C),
        "rw": a["L0_ffn_router_w"].transpose(1, 0, 2).reshape(C, LAYERS * EXPERTS),
        "rb": a["L0_ffn_router_b"].reshape(1, LAYERS * EXPERTS),
        "moe_g": a["L0_ffn_ln_g"].reshape(LAYERS * EXPERTS, C).T,
        "moe_b": a["L0_ffn_ln_b"].reshape(LAYERS * EXPERTS, C).T,
        "w1": a["L0_ffn_w1"].transpose(0, 2, 1, 3),
        "b1": a["L0_ffn_b1"].reshape(LAYERS, EXPERTS * FT, P).transpose(2, 0, 1),
        "w2": a["L0_ffn_w2"].reshape(LAYERS, EXPERTS * FT, P, C).transpose(0, 2, 1, 3),
        "b2": a["L0_ffn_b2"].reshape(LAYERS, EXPERTS * C),
    }
    nc = _bacc.Bacc("TRN2", target_bir_lowering=False, num_devices=1)
    arrays, args = {}, []
    for name, v in layout.items():
        v = _np.ascontiguousarray(v)
        arrays[f"in_{name}"] = v
        args.append(nc.dram_tensor(f"in_{name}", v.shape, _mybir.dt.from_np(v.dtype), kind="ExternalInput").ap())
    args.append(nc.dram_tensor("out", (TOK, C), _mybir.dt.float32, kind="ExternalOutput").ap())
    flamingo_block(nc, *args)
    r = _run(nc, [arrays], core_ids=[0])
    return _np.asarray(r.results[0]["out"]).reshape(_OUT)
```

```python
import concourse.bass as bass
from concourse import mybir
from contextlib import ExitStack

B, NQ, NKEY, C = 32, 56, 1500, 128
HEADS, HD = 8, 16
FF = 512
LAYERS, EXPERTS = 4, 4
TOK = B * NQ
P = 128
TP = PAIR = 2 * NQ
TILES = TOK // TP
KT, KP = 12, 125
QW = HEADS * NQ
NCH = 4
TPS = KT // NCH
SW = TPS * KP
RW = NKEY // TPS
CB = 8
CW = CB * NQ
CHUNKS = TOK // CW
CT = CW // TP
FT = FF // P
MS = 64.0
IS = 1024.0
COLUMNS = 8 + FT + LAYERS * EXPERTS
ROWS = 3 * P + LAYERS * EXPERTS + 2
EPS = 1e-5
WS = 64.0


def flamingo_block(nc, x, ctx_n, ctx_t, squares, columns, per_head, rows, dense, moe_columns, w1, w2, b2, out):
    f32, f16 = mybir.dt.float32, mybir.dt.float16
    ALU, ACT, AX = mybir.AluOpType, mybir.ActivationFunctionType, mybir.AxisListType
    add, sub, mul = ALU.add, ALU.subtract, ALU.mult
    es = ExitStack()
    with es:
        def sb(name, shape, dt=f32):
            return es.enter_context(nc.sbuf_tensor(name, shape, dt))

        def sem(name):
            return es.enter_context(nc.semaphore(name))

        ident = sb("ident", [P, P])
        ident_h = sb("ident_h", [P, P], f16)
        ones32 = sb("ones32", [P, P])
        scale_h = sb("scale_h", [P, P], f16)
        ones_w = sb("ones_w", [P, P], f16)
        ones_h = ones_w[:, 0:TP]
        neghalf = sb("neghalf", [P, CT])
        squares_s = sb("squares_s", [P, 3, P])
        sa_wv_s, sa_wot_s, wot_s = (squares_s[:, i, :] for i in range(3))
        columns_s = sb("columns_s", [P, COLUMNS])
        sa_bv_s, bv_s, ca_bias, l2b_s = (columns_s[:, i:i + 1] for i in range(4))
        ln1_s, ln2_s, l1b_s, rw_s = columns_s[:, 4:6], columns_s[:, 6:8], columns_s[:, 8:8 + FT], columns_s[:, 8 + FT:COLUMNS]
        per_head_s = sb("per_head_s", [HD, 4 * HEADS * P + HEADS])
        wq_s, wk_s, wv_s, wo_s = (per_head_s[:, i * HEADS * P:(i + 1) * HEADS * P].rearrange("p (h c) -> p h c", h=HEADS) for i in range(4))
        bq_s = per_head_s[:, 4 * HEADS * P:]
        rows_s = sb("rows_s", [P, ROWS])
        sa_bias, g3_row, b3_row = (rows_s[:, i * P:(i + 1) * P] for i in range(3))
        rb_s = rows_s[:, 3 * P:3 * P + LAYERS * EXPERTS].rearrange("p (l e) -> p l e", l=LAYERS)
        gates = rows_s[:, ROWS - 2:ROWS]
        dense_s = sb("dense_s", [P, 2 * FF])
        l1_s, l2_s = dense_s[:, 0:FF], dense_s[:, FF:].rearrange("p (q o) -> p q o", q=FT)
        moe_columns_s = sb("moe_columns_s", [P, 2 * LAYERS * EXPERTS + LAYERS * EXPERTS * FT])
        moe_g_s, moe_b_s = (moe_columns_s[:, i * LAYERS * EXPERTS:(i + 1) * LAYERS * EXPERTS] for i in range(2))
        b1_s = moe_columns_s[:, 2 * LAYERS * EXPERTS:].rearrange("p (l k) -> p l k", l=LAYERS)
        rw_hi = sb("rw_hi", [P, LAYERS * EXPERTS], f16)
        rw_lo = sb("rw_lo", [P, LAYERS * EXPERTS], f16)
        rw_sum = sb("rw_sum", [P, LAYERS, EXPERTS])
        m_sa = sb("m_sa", [P, P])
        a_qk = sb("a_qk", [P, HEADS, P])
        a_vo = sb("a_vo", [P, HEADS, P])
        q_bias = sb("q_bias", [P, HEADS])

        x_tm = sb("x_tm", [P, TILES, P])
        y_tm = sb("y_tm", [P, TILES, P])
        z_tm = sb("z_tm", [P, TILES, P])
        f_t = sb("f_t", [P, TOK])
        stats = sb("stats", [P, CT, 6])
        mv = sb("mv", [P, CT, 2])
        ln_var, ln_neg, ln_scale, ln_shift = (sb(n, [P, 3, TILES]) for n in ("ln_var", "ln_neg", "ln_scale", "ln_shift"))

        q_region = sb("q_region", [P, B * QW])
        q_parts = q_region[:, :].bitcast(f16).rearrange("p (b s w) -> p b s w", b=B, s=2)
        ctx_sum = q_region[:, :].rearrange("p (b h n) -> p b h n", b=B, h=HEADS)

        n32 = [v[:].rearrange("p t c -> p (t c)")[:, 0:KT * P] for v in (y_tm, z_tm)]
        t32 = [sb(f"t32_{i}", [P, NKEY]) for i in range(2)]
        n_hi = [sb(f"n_hi{i}", [P, KT, P], f16) for i in range(2)]
        n_lo = [sb(f"n_lo{i}", [P, KT, P], f16) for i in range(2)]
        TPAD = NKEY + 4
        t_hi = [sb(f"t_hi{i}", [P, TPAD], f16) for i in range(2)]
        t_lo = [sb(f"t_lo{i}", [P, TPAD], f16) for i in range(2)]
        p32 = [sb(f"p32_{i}", [P, TPS, QW]) for i in range(2)]
        p_hi = [sb(f"p_hi{i}", [P, TPS, QW], f16) for i in range(2)]
        p_lo = [sb(f"p_lo{i}", [P, TPS, QW], f16) for i in range(2)]
        nmax = sb("nmax", [P, NCH])
        shift_d = [sb(f"shift_d{i}", [P, QW], f16) for i in range(2)]
        p_sum = [sb(f"p_sum{i}", [P, QW]) for i in range(2)]
        inv_sum = sb("inv_sum", [P, NCH])
        inv_parts = sb("inv_parts", [P, 2, NCH], f16)
        inv_diag = sb("inv_diag", [P, 2, QW], f16)

        w1_raw = sb("w1_raw", [P, EXPERTS, FF])
        w2_raw = sb("w2_raw", [P, EXPERTS * FT, P])

        def part(buf, words, dt=f32):
            v = buf[:].rearrange("p a b -> p (a b)") if len(buf.shape) == 3 else buf[:]
            v = v[:, 0:words] if v.dtype is f32 else v[:, 0:2 * words].bitcast(f32)
            return v if dt is f32 else v.bitcast(dt)

        def region(chunk, words, dt=f32, at=0):
            v = q_region[:, chunk * CB * QW + at:chunk * CB * QW + at + words]
            return v if dt is f32 else v.bitcast(dt)

        EW, HW = EXPERTS * FF // 2, FT * CW
        ffh = [region(c, HW).rearrange("p (q n) -> p q n", q=FT) for c in range(CHUNKS)]
        xt_hi, xt_lo = region(0, TOK // 2, f16, HW), region(0, TOK // 2, f16, HW + TOK // 2)
        h32 = [region(1 + i, HW, at=HW).rearrange("p (q n) -> p q n", q=FT) for i in range(2)]
        h_hi = [region(0, HW // 2, f16, i * HW // 2).rearrange("p (q n) -> p q n", q=FT) for i in range(2)]
        h_lo = [region(1, HW // 2, f16, i * HW // 2).rearrange("p (q n) -> p q n", q=FT) for i in range(2)]
        w1_hi = [part(p32[0], EW, f16), region(2, EW, f16)]
        w1_lo = [part(p32[1], EW, f16), region(3, EW, f16)]
        w2_hi = [part(t32[0], EW, f16), region(3, EW, f16, EW)]
        w2_lo = [part(t32[1], EW, f16), region(3, EW, f16, 2 * EW)]
        y_grp, z_grp = (part(p_hi[i], CT * P).rearrange("p (t c) -> p t c", t=CT) for i in (1, 0))
        b2_raw = [part(v, EXPERTS * P) for v in (n_lo[0], n_lo[1], t_lo[0], t_lo[1])]
        b2_parts = [part(v, EXPERTS * P, f16)[:, k * EXPERTS * P:(k + 1) * EXPERTS * P] for v in n_hi for k in range(2)]
        b1_fold = [sb(f"b1_fold{i}", [P, EXPERTS * FT]) for i in range(2)]
        te = [TP, CT, EXPERTS]
        pairs = [TP, CT, EXPERTS, EXPERTS]
        e_stats_s = sb("e_stats_s", [P, CT, 6])
        (m_sum, m_diff, v_sum, e_neg, e_mean, e_var, e_scale, e_shift, gap) = (
            sb(n, [P, CT]) for n in ("m_sum", "m_diff", "v_sum", "e_neg", "e_mean", "e_var", "e_scale", "e_shift", "gap"))
        lg, rank, best, second, picked, halves = (
            sb(n, [P, CT, EXPERTS]) for n in ("lg", "rank", "best", "second", "picked", "halves"))
        e_stds, lg_biases = sb("e_stds", [P, 2, CT]), sb("lg_biases", [P, 2, CT, EXPERTS])
        larger, equal = sb("larger", [P, CT, EXPERTS, EXPERTS]), sb("equal", [P, CT, EXPERTS, EXPERTS])
        lower = sb("lower", [P, EXPERTS, EXPERTS])
        comb_s = sb("comb_s", [P, CHUNKS, CT, EXPERTS])

        psum = es.enter_context(nc.psum_tensor("psum", [P, 8, 512], f32))
        bank = [psum[:, i, :] for i in range(8)]

        def max_scores(b, j):
            k = TPS * (j % 2) if is_int(b, 0) else 0
            return psum[0:PAIR, k:k + TPS, 0:RW]

        x_loaded = [sem(f"x_loaded{c}") for c in range(CHUNKS)]
        fold_loaded, w_loaded, moe_loaded = (sem(n) for n in ("fold_loaded", "w_loaded", "moe_loaded"))
        t_loaded = [sem(f"t_loaded{i}") for i in range(2)]
        n_loaded = [sem(f"n_loaded{i}") for i in range(2)]
        w1_loaded, w2_loaded = sem("w1_loaded"), sem("w2_loaded")
        consts_made, pool_step = sem("consts_made"), sem("pool_step")
        vec_step = sem("vec_step")
        heads_folded = sem("heads_folded")
        folds_mm, folds_done, gates_done, rows_gated = (sem(n) for n in ("folds_mm", "folds_done", "gates_done", "rows_gated"))
        var_ready, scale_ready, normed = ([sem(f"{n}{k}") for k in range(5)] for n in ("var_ready", "scale_ready", "normed"))
        y_tr, y_tr_evac, sa_mm, sa_added, z_tr, z_tr_evac = (sem(n) for n in ("y_tr", "y_tr_evac", "sa_mm", "sa_added", "z_tr", "z_tr_evac"))
        q_mm, q_hi_done, q_lo_done = sem("q_mm"), sem("q_hi_done"), sem("q_lo_done")
        max_mm, max_read, shift_ready = sem("max_mm"), sem("max_read"), sem("shift_ready")
        score_mm, phi_done, plo_done, p_added = sem("score_mm"), sem("phi_done"), sem("plo_done"), sem("p_added")
        pv_mm, ctx_copied, p_sum_mm, inv_ready, inv_diag_ready = (sem(n) for n in ("pv_mm", "ctx_copied", "p_sum_mm", "inv_ready", "inv_diag_ready"))
        inv_mm, sum_done = sem("inv_mm"), sem("sum_done")
        thi_done, tlo_done, nhi_done, nlo_done = sem("thi_done"), sem("tlo_done"), sem("nhi_done"), sem("nlo_done")
        x_biased = sem("x_biased")
        ca_mm, ca_added, ca_back, x2_tr, x2_tr_evac = (sem(n) for n in ("ca_mm", "ca_added", "ca_back", "x2_tr", "x2_tr_evac"))
        ff_back = sem("ff_back")
        ff1_mm, ff1_act, ff2_mm, ff2_added = sem("ff1_mm"), sem("ff1_act"), sem("ff2_mm"), sem("ff2_added")
        w_split, b1_mm, b1_done = sem("w_split"), sem("b1_mm"), sem("b1_done")
        b2_cleared, b2_loaded, b2_ready = sem("b2_cleared"), sem("b2_loaded"), sem("b2_ready")
        hid_mm, gelu_done, hhi_done, hlo_done = sem("hid_mm"), sem("gelu_done"), sem("hhi_done"), sem("hlo_done")
        y_mm, acc_done, y_saved = sem("y_mm"), sem("acc_done"), sem("y_saved")
        e_stats, e_normed, e_step, route_step = (sem(n) for n in ("e_stats", "e_normed", "e_step", "route_step"))
        xt_mm, xthi_done, xtlo_done, logit_mm = (sem(n) for n in ("xt_mm", "xthi_done", "xtlo_done", "logit_mm"))
        lg_ready, gap_ready, gate_tanh, comb_ready = (sem(n) for n in ("lg_ready", "gap_ready", "gate_tanh", "comb_ready"))
        out_ready, out_stored = sem("out_ready"), sem("out_stored")

        fold_loads = [(per_head_s[:], per_head), (squares_s[:], squares), (columns_s[:], columns),
                      (rows_s[:], rows.to_broadcast([P, ROWS]))]
        LN_IN, LN_ONE, LN_TWO, LN_THREE, LN_OUTER = range(5)
        LN_SLOT = (0, 1, 0, 1, 2)
        BR = 32

        def chunk(c):
            return slice(CT * c, CT * (c + 1)) if is_int(c) else bass.ds(c * CT, CT)

        def tiles_of(bank_i):
            return bank[bank_i][0:TP, :].rearrange("p (t c) -> p t c", t=CT)

        def units_before(l, g, e):
            return g * EXPERTS + (CHUNKS * EXPERTS * l + e)

        def expert_groups(engine, body):
            for l in range(LAYERS):
                peeled = 2 if l == LAYERS - 1 else 1
                for g in range(peeled):
                    body(l, g)
                with engine.Fori(peeled, CHUNKS) as g:
                    body(l, g)

        def chained(engine, s, base):
            done = [0]

            def link(ins):
                done[0] += 1
                ins.then_inc(s, 1)
                engine.wait_ge(s, base + done[0])
            return link

        def router_terms(m):
            slot = m % 2 if is_int(m) and m < CHUNKS else 0
            return e_stds[0:TP, slot, :], lg_biases[0:TP, slot, :, :]

        def follower(l, g):
            if is_int(g, 0):
                return CHUNKS * l + CHUNKS - 1, l, CHUNKS - 1
            if l == LAYERS - 1:
                return None
            return g + (CHUNKS * (l + 1) - 1), l + 1, g - 1

        block = es.enter_context(nc.Block())

        def seq_pairs(engine, step):
            step(0, 0)
            step(1, 1)
            with engine.Fori(1, B // 2 - 1) as i:
                for par in range(2):
                    step(i * 2 + par, par)
            step(B - 2, 0)
            step(B - 1, 1)

        def is_int(b, v=None):
            return type(b) is int and (v is None or b == v)

        def before(b, par, j):
            return (b, par, j - 1) if j else (b - 1, 1 - par, NCH - 1)

        ADDS = KT - 1

        def adds(b, j):
            return b * ADDS + (TPS * (j + 1) - 1)

        def context_sums(b):
            return ctx_sum[:, b, :, :] if is_int(b) else ctx_sum[:, bass.ds(b, 1), :, :].rearrange("p o h n -> p (o h) n")

        @block.sync
        def _(sp):
            x_v = x.rearrange("(t p) c -> p t c", p=TP)
            for c in range(CHUNKS):
                sp.dma_start(x_tm[0:TP, chunk(c), :], x_v[:, chunk(c), :]).then_inc(x_loaded[c], 16)
            sp.dma_start(dense_s[:], dense).then_inc(w_loaded, 16)
            sp.dma_start(moe_columns_s[:], moe_columns).then_inc(moe_loaded, 16)

            def load_t(b, par):
                if not is_int(b) or b >= 2:
                    sp.wait_ge(tlo_done, (b - 1) * NCH)
                sp.dma_start(t32[par][:], ctx_t[b] if is_int(b) else ctx_t[bass.ds(b, 1), :, :].rearrange("o p n -> (o p) n")).then_inc(t_loaded[par], 16)

            def load_n(b, par):
                if not is_int(b) or b >= 2:
                    sp.wait_ge(nlo_done, b - 1)
                else:
                    sp.wait_ge(z_tr, CHUNKS)
                sp.dma_start(n32[par][0:KP, :], ctx_n[b] if is_int(b) else ctx_n[bass.ds(b, 1), :, :].rearrange("o p n -> (o p) n")).then_inc(n_loaded[par], 16)
            load_t(0, 0)
            load_t(1, 1)
            sp.dma_start(w1_raw[:], w1[0]).then_inc(w1_loaded, 16)
            sp.dma_start(w2_raw[:], w2[0]).then_inc(w2_loaded, 16)
            load_n(0, 0)
            load_n(1, 1)
            with sp.Fori(1, B // 2) as i:
                for par in range(2):
                    load_t(i * 2 + par, par)
                    load_n(i * 2 + par, par)
            sp.wait_ge(b2_cleared, LAYERS)
            for l in range(LAYERS):
                for row in (0, BR):
                    sp.dma_start(b2_raw[l][row:row + 1, :], b2[l:l + 1, :]).then_inc(b2_loaded, 16)
            for l in range(1, LAYERS):
                sp.wait_ge(w_split, 2 * EXPERTS * l - (EXPERTS if l > 1 else 0))
                sp.dma_start(w1_raw[:], w1[l]).then_inc(w1_loaded, 16)
                sp.wait_ge(w_split, 2 * EXPERTS * l)
                sp.dma_start(w2_raw[:], w2[l]).then_inc(w2_loaded, 16)
            out_v = out.rearrange("(t p) c -> p t c", p=TP)
            for g in range(CHUNKS):
                sp.wait_ge(out_ready, g + 1)
                sp.dma_start(out_v[:, chunk(g), :], x_tm[0:TP, chunk(g), :]).then_inc(out_stored, 16)
            sp.wait_ge(out_stored, 16 * CHUNKS)

        @block.gpsimd
        def _(pool):
            steps = [0]

            def step(ins):
                steps[0] += 1
                ins.then_inc(pool_step, 1)
                pool.wait_ge(pool_step, steps[0])

            step(nc.gpsimd.memset(ident[:], 0.0))
            step(nc.gpsimd.affine_select(out=ident[:], in_=ident[:], compare_op=ALU.not_equal, fill=1.0, base=0,
                                         pattern=[[-1, P]], channel_multiplier=1))
            nc.gpsimd.tensor_copy(ident_h[:], ident[:]).then_inc(consts_made, 1)
            nc.gpsimd.memset(ones32[:], 1.0).then_inc(consts_made, 1)
            nc.gpsimd.memset(scale_h[:], MS).then_inc(consts_made, 1)
            nc.gpsimd.memset(ones_w[:], 1.0).then_inc(consts_made, 1)
            step(nc.gpsimd.memset(lower[:], 0.0))
            for e in range(1, EXPERTS):
                nc.gpsimd.memset(lower[:, e, 0:e], 1.0)
            nc.gpsimd.memset(gap[:], 0.0).then_inc(y_saved, 1)
            step(nc.gpsimd.memset(neghalf[:], -0.5))
            for i in range(2):
                nc.gpsimd.memset(t_hi[i][:, NKEY:TPAD], 0.0).then_inc(consts_made, 1)
                nc.gpsimd.memset(t_lo[i][:, NKEY:TPAD], 0.0).then_inc(consts_made, 1)

            T = nc.gpsimd.tensor_tensor

            def scale(k, c):
                at = LN_SLOT[k], slice(CT * c, CT * (c + 1))
                pool.wait_ge(var_ready[k], c + 1)
                step(T(ln_scale[0:TP, *at], ln_var[0:TP, *at], neghalf[0:TP, :], ALU.pow))
                T(ln_shift[0:TP, *at], ln_neg[0:TP, *at], ln_scale[0:TP, *at], mul).then_inc(scale_ready[k], 1)

            for c in range(CHUNKS):
                scale(LN_IN, c)
            for c in range(CHUNKS):
                scale(LN_ONE, c)
            pool.wait_ge(rows_gated, 1)
            pool.wait_ge(normed[LN_IN], CHUNKS)
            T(x_tm[0:TP], x_tm[0:TP], b3_row[0:TP, None, :].to_broadcast([TP, TILES, P]), add).then_inc(x_biased, 1)

            def split_piece(l, k):
                s, e = l % 2, k % EXPERTS
                first = k < EXPERTS
                raw = w1_raw[:, e, :] if first else w2_raw[:, e * FT:(e + 1) * FT, :].rearrange("p q c -> p (q c)")
                hi, lo = (w1_hi[s], w1_lo[s]) if first else (w2_hi[s], w2_lo[s])
                cols = slice(e * FF, (e + 1) * FF)
                gain = moe_g_s[:, EXPERTS * l + e:EXPERTS * l + e + 1] if first else 1.0
                nc.gpsimd.tensor_scalar(hi[:, cols], raw, gain, WS, mul, mul)
                step(nc.gpsimd.tensor_scalar(raw, raw, gain, WS, mul, mul))
                last = nc.gpsimd.tensor_tensor(lo[:, cols], raw, hi[:, cols], sub)
                last.then_inc(w_split, 1)

            def split_share(l, g):
                for k in (2 * g, 2 * g + 1):
                    split_piece(l, k)

            def split_ready(l):
                if l == 0:
                    pool.wait_ge(moe_loaded, 16)
                pool.wait_ge(w1_loaded, 16 * (l + 1))
                pool.wait_ge(w2_loaded, 16 * (l + 1))
                pool.wait_ge(b1_mm, l + 1)
                if l == 0:
                    pool.wait_ge(tlo_done, B * NCH)
                elif l == 1:
                    pool.wait_ge(ff2_mm, CHUNKS)
                else:
                    pool.wait_ge(y_mm, CHUNKS * EXPERTS * (l - 1))

            def split_n(b, par):
                pool.wait_ge(nhi_done, b + 1)
                nc.gpsimd.tensor_tensor(n_lo[par][0:KP, :, :].rearrange("p t c -> p (t c)"), n32[par][0:KP, :],
                                        n_hi[par][0:KP, :, :].rearrange("p t c -> p (t c)"), sub).then_inc(nlo_done, 1)

            def sequence(b, par):
                total = p_sum[par][0:KP, :]
                for j in range(NCH):
                    for i in range(TPS):
                        t = TPS * j + i
                        if t == 0:
                            continue
                        pool.wait_ge(phi_done, b * KT + (t + 1))
                        tile = p32[j % 2][0:KP, i, :]
                        if t == 1:
                            if not (is_int(b) and b < 2):
                                pool.wait_ge(p_sum_mm, b - 1)
                            nc.gpsimd.tensor_tensor(total, p32[0][0:KP, 0, :], tile, add).then_inc(p_added, 1)
                        else:
                            pool.wait_ge(p_added, b * ADDS + (t - 1))
                            nc.gpsimd.tensor_tensor(total, total, tile, add).then_inc(p_added, 1)
                    if j == 1 and not is_int(b, B - 1):
                        split_n(b + 1, 1 - par)
                    if is_int(b, B - 1):
                        if j == 0:
                            split_ready(0)
                        for k in ((0,), (1,), (), (2, 3))[j]:
                            split_piece(0, EXPERTS + k)

            split_n(0, 0)
            seq_pairs(pool, sequence)

            pool.wait_ge(pv_mm, B * NCH)
            for l in range(LAYERS):
                nc.gpsimd.memset(b2_raw[l][0:BR + 1, :], 0.0).then_inc(b2_cleared, 1)

            TS = nc.gpsimd.tensor_scalar
            E_LINKS = 6

            def normalise_e(m, l, src):
                link = chained(pool, e_step, m * E_LINKS)
                a = slice(0, TP)
                e_std, lg_bias = router_terms(m)
                pool.wait_ge(e_stats, m + 1)
                T(m_sum[a], e_stats_s[a, :, 1], e_stats_s[a, :, 4], add)
                T(m_diff[a], e_stats_s[a, :, 1], e_stats_s[a, :, 4], sub)
                link(T(v_sum[a], e_stats_s[a, :, 2], e_stats_s[a, :, 5], add))
                TS(m_diff[a], m_diff[a], 0.5, None, mul)
                TS(e_neg[a], m_sum[a], -0.5, None, mul)
                TS(e_mean[a], m_sum[a], 0.5, None, mul)
                link(TS(v_sum[a], v_sum[a], 1.0 / P, EPS, mul, add))
                T(lg_bias, e_mean[a, :, None].to_broadcast(te), rw_sum[a, l:l + 1, :].to_broadcast(te), mul)
                link(T(m_diff[a], m_diff[a], m_diff[a], mul))
                T(lg_bias, lg_bias, rb_s[a, l:l + 1, :].to_broadcast(te), add)
                link(T(e_var[a], m_diff[a], v_sum[a], add))
                link(T(e_scale[a], e_var[a], neghalf[a], ALU.pow))
                T(e_std, e_var[a], e_scale[a], mul)
                link(T(e_shift[a], e_neg[a], e_scale[a], mul))
                if not is_int(m, 0):
                    pool.wait_ge(xt_mm, m)
                for i in range(CT):
                    last = TS(z_grp[a, i, :], src(i), e_scale[a, i:i + 1], e_shift[a, i:i + 1], mul, add)
                last.then_inc(e_normed, 1)

            pool.wait_ge(w_loaded, 16)
            pool.wait_ge(plo_done, B * NCH)
            PIECES = ((0, 1), (2, 3), (), (), ())
            for s in range(CHUNKS + 1):
                if s >= 2:
                    scale(LN_OUTER, s - 2)
                if s < CHUNKS:
                    scale(LN_TWO, s)
                if s >= 1:
                    scale(LN_THREE, s - 1)
                if s >= 2:
                    normalise_e(s - 2, 0, lambda i: y_tm[0:TP, CT * (s - 2) + i, :])
                for k in PIECES[s]:
                    split_piece(0, k)
            scale(LN_OUTER, CHUNKS - 1)

            def group(l, g):
                f = follower(l, g)
                if f is None:
                    return
                if l == 0 and g == 0:
                    normalise_e(f[0], f[1], lambda i: y_tm[0:TP, CT * f[2] + i, :])
                else:
                    normalise_e(f[0], f[1], lambda i: y_grp[0:TP, i, :])
                    TS(y_tm[0:TP, chunk(f[2]), :], y_grp[0:TP], 1.0, None, mul).then_inc(y_saved, 1)
                if l < LAYERS - 1:
                    if is_int(g, 0):
                        split_ready(l + 1)
                    split_share(l + 1, g)

            for l in range(LAYERS):
                group(l, 0)
                if l < LAYERS - 1:
                    for g in range(1, CHUNKS):
                        group(l, g)

        @block.scalar
        def _(act):
            for dst, src in fold_loads:
                act.dma_start(dst, src).then_inc(fold_loaded, 16)

            def normalise(k, c, src, dst):
                act.wait_ge(scale_ready[k], c + 1)
                for i in range(CT):
                    t = CT * c + i
                    last = nc.scalar.activation(dst[0:TP, t, :], src(t, i), ACT.Identity, bias=ln_shift[0:TP, LN_SLOT[k], t:t + 1],
                                                scale=ln_scale[0:TP, LN_SLOT[k], t:t + 1])
                last.then_inc(normed[k], 1)

            def gained(c, bank_i, gain, s):
                a = {} if gain is None else {"scale": gain[:, 0:1], "bias": gain[:, 1:2]}
                nc.scalar.activation(f_t[:, c * CW:(c + 1) * CW], bank[bank_i][:, 0:CW], ACT.Identity, **a).then_inc(s, 1)

            def high_queries(c, h0, h1):
                for h in range(h0, h1):
                    k = c * HEADS + h
                    act.wait_ge(q_mm, k + 1)
                    nc.scalar.activation(q_parts[:, c * CB:(c + 1) * CB, 0, h * NQ:(h + 1) * NQ],
                                         bank[4 + k % 4][:, 0:CW].rearrange("p (b n) -> p b n", b=CB), ACT.Identity,
                                         bias=q_bias[:, h:h + 1]).then_inc(q_hi_done, 1)

            def split_t(b, par, j):
                if j == 0:
                    act.wait_ge(t_loaded[par], 16 * (b // 2 + 1) if is_int(b) else (b - par) * 8 + 16)
                nc.scalar.copy(t_hi[par][:, j * SW:(j + 1) * SW], t32[par][:, j * SW:(j + 1) * SW]).then_inc(thi_done, 1)

            def copy_sums(b):
                act.wait_ge(pv_mm, b * NCH + NCH)
                nc.scalar.copy(context_sums(b), bank[6][:, 0:QW].rearrange("p (h n) -> p h n", h=HEADS)).then_inc(ctx_copied, 1)

            def split_n(b, par):
                act.wait_ge(n_loaded[par], 16 * (b // 2 + 1) if is_int(b) else (b - par) * 8 + 16)
                nc.scalar.copy(n_hi[par][0:KP, :, :].rearrange("p t c -> p (t c)"), n32[par][0:KP, :]).then_inc(nhi_done, 1)

            for c in range(CHUNKS):
                normalise(LN_IN, c, lambda t, i: x_tm[0:TP, t, :], y_tm)
            act.wait_ge(fold_loaded, 16 * len(fold_loads))
            nc.scalar.activation(gates, gates, ACT.Tanh).then_inc(gates_done, 1)
            act.wait_ge(w_loaded, 16)

            def heads_out(k, dst, first_bank, factor):
                act.wait_ge(folds_mm, k + 1)
                for i in range(2):
                    last = nc.scalar.activation(dst[:, 4 * i:4 * i + 4, :], bank[first_bank + i][:, :].rearrange("p (h c) -> p h c", h=4),
                                                ACT.Copy, scale=factor)
                last.then_inc(heads_folded, 1)

            for s in range(CHUNKS + 2):
                if s < CHUNKS:
                    act.wait_ge(y_tr, s + 1)
                    gained(s, 0, None, y_tr_evac)
                if s == 0:
                    heads_out(1, a_qk, 4, HD ** -0.5)
                if s == 1:
                    heads_out(2, a_vo, 6, 1.0)
                    act.wait_ge(folds_done, 2)
                if s < 2:
                    for j in range(NCH):
                        split_t(s, s, j)
                if s >= 2:
                    high_queries(s - 2, 0, HEADS // 2)
                if 1 <= s <= CHUNKS:
                    normalise(LN_ONE, s - 1, lambda t, i: z_tm[0:TP, t, :], z_tm)
                if s >= 2:
                    high_queries(s - 2, HEADS // 2, HEADS - 1)
                if 1 <= s <= CHUNKS:
                    act.wait_ge(z_tr, s)
                    gained(s - 1, 2, ln1_s, z_tr_evac)
                if s >= 2:
                    high_queries(s - 2, HEADS - 1, HEADS)
            split_n(0, 0)

            def sequence(b, par):
                for j in range(NCH):
                    ring = j % 2
                    if j == 1 and not is_int(b, 0):
                        copy_sums(b - 1)
                    if not (is_int(b, 0) and j < 2):
                        act.wait_ge(pv_mm, b * NCH + (j - 1))
                        act.wait_ge(p_added, adds(b, j - 2) if j >= 2 else adds(b - 1, j + 2))
                    for i in range(TPS):
                        t = TPS * j + i
                        act.wait_ge(score_mm, b * KT + (t + 1))
                        nc.scalar.activation(p32[ring][0:KP, i, :], bank[3 + i][0:KP, 0:QW], ACT.Exp)
                        nc.scalar.activation(p_hi[ring][0:KP, i, :], bank[3 + i][0:KP, 0:QW], ACT.Exp).then_inc(phi_done, 1)
                    if not (is_int(b) and b >= B - 2):
                        split_t(b + 2, par, j)
                    if j == 1 and not is_int(b, B - 1):
                        split_n(b + 1, 1 - par)

            seq_pairs(act, sequence)
            copy_sums(B - 1)

            def split_xt(m, g):
                act.wait_ge(xt_mm, m + 1)
                nc.scalar.copy(xt_hi[:, bass.ds(g * CW, CW)], bank[6][:, 0:CW]).then_inc(xthi_done, 1)

            def gate(m):
                act.wait_ge(gap_ready, m + 1)
                nc.scalar.activation(gap[0:TP], gap[0:TP], ACT.Tanh, scale=0.5).then_inc(gate_tanh, 1)

            def bank_tiles(i_bank):
                return lambda t, i: bank[i_bank][0:TP, i * P:(i + 1) * P]

            for s in range(CHUNKS + 1):
                if s >= 1:
                    act.wait_ge(x2_tr, s)
                    gained(s - 1, 2, ln2_s, x2_tr_evac)
                if s >= 2:
                    normalise(LN_THREE, s - 2, bank_tiles(5), z_tm)
                if s >= 1:
                    for q in range(FT):
                        k = (s - 1) * FT + q
                        act.wait_ge(ff1_mm, k + 1)
                        nc.scalar.activation(ffh[s - 1][:, q, :], bank[3 + k % 2][:, 0:CW], ACT.Relu, bias=l1b_s[:, q:q + 1]).then_inc(ff1_act, 1)
                if s >= 3:
                    split_xt(s - 3, s - 3)
                if s >= 2:
                    normalise(LN_OUTER, s - 2, lambda t, i: x_tm[0:TP, t, :], y_tm)
                if s < CHUNKS:
                    normalise(LN_TWO, s, bank_tiles(1), z_tm)
                if s >= 4:
                    gate(s - 4)
            act.wait_ge(ff2_mm, CHUNKS)

            def unit(l, g, e):
                u, par = units_before(l, g, e), e % 2
                first_use = is_int(u) and u < 2
                if e == 0 and is_int(g, 0):
                    act.wait_ge(b1_done, l + 1)
                if not first_use:
                    act.wait_ge(hlo_done, u - 1)
                for q in range(FT):
                    k = e * FT + q
                    act.wait_ge(hid_mm, u * FT + (q + 1))
                    nc.scalar.activation(h32[par][:, q, :], bank[q][:, 0:CW], ACT.Gelu, scale=1.0 / WS,
                                         bias=b1_fold[l % 2][:, k:k + 1]).then_inc(gelu_done, 1)
                act.wait_ge(gelu_done, u * FT + FT)
                if not first_use:
                    act.wait_ge(y_mm, u - 1)
                nc.scalar.copy(h_hi[par], h32[par]).then_inc(hhi_done, 1)

            def group(l, g):
                f = follower(l, g)
                start = l == 0 and is_int(g, 0)
                for e in range(EXPERTS):
                    if e == 3 and f is not None and not start:
                        split_xt(f[0], f[2])
                    unit(l, g, e)
                    if start:
                        if e == 0:
                            normalise(LN_THREE, CHUNKS - 1, bank_tiles(5), z_tm)
                            gate(CHUNKS - 3)
                        if e == 1:
                            split_xt(CHUNKS - 2, CHUNKS - 2)
                            normalise(LN_OUTER, CHUNKS - 1, lambda t, i: x_tm[0:TP, t, :], y_tm)
                        if e == 2:
                            gate(CHUNKS - 2)
                        if e == 3:
                            split_xt(f[0], f[2])
                    if e == 3 and f is not None:
                        gate(f[0])

            expert_groups(act, group)

        @block.vector
        def _(dve):
            steps = [0]

            def step(ins):
                steps[0] += 1
                ins.then_inc(vec_step, 1)
                dve.wait_ge(vec_step, steps[0])

            V = nc.vector

            def variances(k, c, src):
                for i in range(CT):
                    last = V.bn_stats(stats[0:TP, i, :], src(CT * c + i, i))
                step(last)
                for i in range(CT):
                    last = V.bn_aggr(mv[0:TP, i, :], stats[0:TP, i, :])
                step(last)
                at = LN_SLOT[k], slice(CT * c, CT * (c + 1))
                V.tensor_scalar(ln_neg[0:TP, *at], mv[0:TP, :, 0], -1.0, None, mul)
                V.tensor_scalar(ln_var[0:TP, *at], mv[0:TP, :, 1], EPS, None, add).then_inc(var_ready[k], 1)

            for c in range(CHUNKS):
                dve.wait_ge(x_loaded[c], 16)
                variances(LN_IN, c, lambda t, i: x_tm[0:TP, t, :])

            dve.wait_ge(fold_loaded, 16 * len(fold_loads))
            dve.wait_ge(folds_mm, 1)
            V.tensor_tensor(sa_bias, bank[3][:, 128:256], sa_bias, add)
            V.tensor_copy(m_sa[:], bank[3][:, 0:128]).then_inc(folds_done, 1)
            V.tensor_tensor(ca_bias, bank[3][:, 256:257], ca_bias, add)
            V.tensor_copy(rw_sum[:].rearrange("p l e -> p (l e)"), bank[3][:, 260:276])
            V.tensor_scalar(q_bias[:], bank[3][:, 280:288], HD ** -0.5, None, mul)
            step(V.tensor_scalar(rw_s, rw_s, WS, None, mul))
            step(V.tensor_copy(rw_hi[:], rw_s))
            V.tensor_tensor(rw_lo[:], rw_s, rw_hi[:], sub).then_inc(folds_done, 1)
            dve.wait_ge(folds_done, 2)

            def low_queries(c, h0, h1):
                for h in range(h0, h1):
                    k = c * HEADS + h
                    dve.wait_ge(q_hi_done, k + 1)
                    V.scalar_tensor_tensor(out=q_parts[:, c * CB:(c + 1) * CB, 1, h * NQ:(h + 1) * NQ],
                                           in0=bank[4 + k % 4][:, 0:CW].rearrange("p (b n) -> p b n", b=CB), scalar=q_bias[:, h:h + 1],
                                           in1=q_parts[:, c * CB:(c + 1) * CB, 0, h * NQ:(h + 1) * NQ],
                                           op0=add, op1=sub).then_inc(q_lo_done, 1)

            def split_t(b, par, j):
                dve.wait_ge(thi_done, b * NCH + (j + 1))
                V.tensor_tensor(t_lo[par][:, j * SW:(j + 1) * SW], t32[par][:, j * SW:(j + 1) * SW],
                                t_hi[par][:, j * SW:(j + 1) * SW], sub).then_inc(tlo_done, 1)

            def maximum(b, par, j):
                dve.wait_ge(max_mm, b * NCH + (j + 1))
                V.tensor_reduce(out=nmax[0:PAIR, j:j + 1],
                                in_=max_scores(b, j), axis=AX.XY, op=ALU.max).then_inc(max_read, 1)
                dve.wait_ge(max_read, b * NCH + (j + 1))
                if j == 0 and not (is_int(b) and b < 2):
                    dve.wait_ge(score_mm, (b - 1) * KT)
                V.tensor_scalar(shift_d[par][0:PAIR, j * PAIR:(j + 1) * PAIR], ident_h[0:PAIR, 0:PAIR],
                                nmax[0:PAIR, j:j + 1], -1.0 / MS, mul, mul).then_inc(shift_ready, 1)

            def fold_b1(l, bank_i):
                dve.wait_ge(b1_mm, l + 1)
                V.tensor_tensor(b1_fold[l % 2][:], bank[bank_i][:, 256:256 + EXPERTS * FT], b1_s[:, l, :], add).then_inc(b1_done, 1)

            dve.wait_ge(consts_made, 8)
            for s in range(CHUNKS + 2):
                if s < CHUNKS:
                    dve.wait_ge(normed[LN_IN], s + 1)
                    step(V.tensor_tensor(z_tm[0:TP, chunk(s), :], y_tm[0:TP, chunk(s), :],
                                         sa_bias[0:TP, None, :].to_broadcast([TP, CT, P]), add))
                if s >= 2:
                    low_queries(s - 2, 0, HEADS // 2)
                if s < CHUNKS:
                    dve.wait_ge(sa_mm, s + 1)
                    V.tensor_tensor(z_tm[0:TP, chunk(s), :], tiles_of(1), z_tm[0:TP, chunk(s), :], add).then_inc(sa_added, 1)
                    dve.wait_ge(sa_added, s + 1)
                if s == CHUNKS + 1:
                    maximum(0, 0, 0)
                if s >= 2:
                    low_queries(s - 2, HEADS // 2, HEADS)
                if s == CHUNKS + 1:
                    maximum(0, 0, 1)
                if s < CHUNKS:
                    variances(LN_ONE, s, lambda t, i: z_tm[0:TP, t, :])
                if s < 2:
                    for j in range(NCH):
                        split_t(s, s, j)
                if s == 1:
                    dve.wait_ge(gates_done, 1)
                    V.tensor_scalar(g3_row, g3_row, gates[:, 0:1], None, mul)
                    V.tensor_scalar(b3_row, b3_row, gates[:, 0:1], None, mul).then_inc(rows_gated, 1)


            def low_probs(b, j):
                ring = j % 2
                dve.wait_ge(phi_done, b * KT + TPS * (j + 1))
                V.tensor_tensor(p_lo[ring][0:KP, :, :].rearrange("p t w -> p (t w)"),
                                p32[ring][0:KP, :, :].rearrange("p t w -> p (t w)"),
                                p_hi[ring][0:KP, :, :].rearrange("p t w -> p (t w)"), sub).then_inc(plo_done, 1)

            def invert(b):
                dve.wait_ge(p_sum_mm, b + 1)
                link = chained(dve, inv_ready, b * 4)
                link(V.reciprocal(inv_sum[0:PAIR, :], bank[7][0:PAIR, QW:QW + NCH]))
                link(V.tensor_scalar(inv_sum[0:PAIR, :], inv_sum[0:PAIR, :], IS, None, mul))
                link(V.tensor_scalar(inv_parts[0:PAIR, 0, :], inv_sum[0:PAIR, :], 1.0, None, mul))
                link(V.tensor_tensor(inv_parts[0:PAIR, 1, :], inv_sum[0:PAIR, :], inv_parts[0:PAIR, 0, :], sub))
                blocks = [PAIR, 2 * NCH, PAIR]
                V.tensor_tensor(inv_diag[0:PAIR, :, :].rearrange("p s (j w) -> p (s j) w", j=NCH),
                                ident_h[0:PAIR, None, 0:PAIR].to_broadcast(blocks),
                                inv_parts[0:PAIR, :, :].rearrange("p s j -> p (s j)")[:, :, None].to_broadcast(blocks),
                                mul).then_inc(inv_diag_ready, 1)

            def divide(b):
                dve.wait_ge(inv_mm, b + 1)
                dve.wait_ge(ctx_copied, b + 1)
                o = context_sums(b)
                V.scalar_tensor_tensor(out=o, in0=bank[7][:, 0:QW].rearrange("p (h n) -> p h n", h=HEADS), scalar=1.0 / IS, in1=o,
                                       op0=mul, op1=mul).then_inc(sum_done, 1)

            maximum(0, 0, 2)
            maximum(0, 0, 3)
            fold_b1(0, 6)

            def sequence(b, par):
                for j in range(NCH):
                    first = is_int(b, 0) and j == 0
                    pb, ppar, pj = before(b, par, j)
                    if not first:
                        low_probs(pb, pj)
                    if not is_int(b, B - 1):
                        maximum(b + 1, 1 - par, j)
                    if not first and not (is_int(pb) and pb >= B - 2):
                        split_t(pb + 2, ppar, pj)
                    if not is_int(b, 0):
                        if j == 1:
                            invert(b - 1)
                        if j == 3:
                            divide(b - 1)

            seq_pairs(dve, sequence)
            low_probs(B - 1, NCH - 1)
            invert(B - 1)
            divide(B - 1)

            def to_residual(c, bank_i, bias, s):
                V.scalar_tensor_tensor(out=f_t[:, c * CW:(c + 1) * CW], in0=bank[bank_i][:, 0:CW], scalar=bias[:, 0:1],
                                       in1=f_t[:, c * CW:(c + 1) * CW], op0=add, op1=add).then_inc(s, 1)

            def bank_tiles(i_bank):
                return lambda t, i: bank[i_bank][0:TP, i * P:(i + 1) * P]

            def outer_residual(c):
                dve.wait_ge(normed[LN_THREE], c + 1)
                z, xc = z_tm[0:TP, chunk(c), :], x_tm[0:TP, chunk(c), :]
                step(V.tensor_tensor(z, z, g3_row[0:TP, None, :].to_broadcast([TP, CT, P]), mul))
                if c == 0:
                    dve.wait_ge(x_biased, 1)
                step(V.tensor_tensor(xc, xc, z, add))
                variances(LN_OUTER, c, lambda t, i: x_tm[0:TP, t, :])

            def e_statistics(m, src):
                if not is_int(m, 0):
                    dve.wait_ge(e_normed, m)
                for i in range(CT):
                    last = V.bn_stats(e_stats_s[0:TP, i, :], src(i))
                last.then_inc(e_stats, 1)

            def split_xt(m, g):
                dve.wait_ge(xthi_done, m + 1)
                V.tensor_tensor(xt_lo[:, bass.ds(g * CW, CW)], bank[6][:, 0:CW], xt_hi[:, bass.ds(g * CW, CW)], sub).then_inc(xtlo_done, 1)

            RANK_LINKS, WEIGH_LINKS = 9, 2
            a = slice(0, TP)

            def rank_experts(m):
                link = chained(dve, route_step, m * (RANK_LINKS + WEIGH_LINKS))
                e_std, lg_bias = router_terms(m)
                dve.wait_ge(logit_mm, m + 1)
                link(V.scalar_tensor_tensor(out=lg[a], in0=bank[7][a, 0:CT * EXPERTS].rearrange("p (t e) -> p t e", t=CT),
                                            scalar=1.0 / WS, in1=e_std[:, :, None].to_broadcast(te), op0=mul, op1=mul))
                last = V.tensor_tensor(lg[a], lg[a], lg_bias, add)
                last.then_inc(lg_ready, 1)
                dve.wait_ge(lg_ready, m + 1)
                other, own = lg[a, :, None, :].to_broadcast(pairs), lg[a, :, :, None].to_broadcast(pairs)
                V.tensor_tensor(larger[a], other, own, ALU.is_gt)
                link(V.tensor_tensor(equal[a], other, own, ALU.is_equal))
                link(V.tensor_tensor(equal[a], equal[a], lower[a, None, :, :].to_broadcast(pairs), mul))
                link(V.tensor_tensor(larger[a], larger[a], equal[a], add))
                link(V.tensor_reduce(out=rank[a], in_=larger[a], axis=AX.X, op=add))
                V.tensor_scalar(best[a], rank[a], 0.0, None, ALU.is_equal)
                link(V.tensor_scalar(second[a], rank[a], 1.0, None, ALU.is_equal))
                V.tensor_tensor(picked[a], best[a], second[a], add)
                link(V.tensor_tensor(best[a], best[a], second[a], sub))
                link(V.tensor_tensor(halves[a], best[a], lg[a], mul))
                link(V.tensor_tensor(halves[a, :, 0:2], halves[a, :, 0:2], halves[a, :, 2:4], add))
                V.tensor_tensor(gap[a], halves[a, :, 0], halves[a, :, 1], add).then_inc(gap_ready, 1)

            def weigh_experts(m, g):
                link = chained(dve, route_step, m * (RANK_LINKS + WEIGH_LINKS) + RANK_LINKS)
                dve.wait_ge(gate_tanh, m + 1)
                link(V.tensor_tensor(best[a], best[a], gap[a, :, None].to_broadcast(te), mul))
                link(V.tensor_tensor(best[a], best[a], picked[a], add))
                d = comb_s[a, g, :, :] if is_int(g) else comb_s[a, bass.ds(g, 1), :, :].rearrange("p o t e -> p (o t) e")
                V.tensor_scalar(d, best[a], 0.5 / WS, None, mul).then_inc(comb_ready, 1)

            def output_bias(l):
                if l == 0:
                    dve.wait_ge(b2_loaded, 16 * 2 * LAYERS)
                rows = slice(0, BR + 1)
                step(V.tensor_scalar(b2_raw[l][rows, :], b2_raw[l][rows, :], WS, None, mul))
                step(V.tensor_copy(b2_parts[l][rows, :], b2_raw[l][rows, :]))
                V.tensor_tensor(b2_parts[l][BR:BR + 1, :], b2_raw[l][BR:BR + 1, :], b2_parts[l][BR:BR + 1, :], sub).then_inc(b2_ready, 1)

            def dense_residual(c):
                dve.wait_ge(ff2_mm, c + 1)
                to_residual(c, 2, l2b_s, ff2_added)
                dve.wait_ge(ff_back, c + 1)
                variances(LN_THREE, c, bank_tiles(5))

            for s in range(CHUNKS + 1):
                if s < CHUNKS:
                    dve.wait_ge(ca_mm, s + 1)
                    to_residual(s, 0, ca_bias, ca_added)
                if s >= 2:
                    outer_residual(s - 2)
                if s < CHUNKS:
                    dve.wait_ge(ca_back, s + 1)
                    variances(LN_TWO, s, bank_tiles(1))
                if s >= 3:
                    split_xt(s - 3, s - 3)
                if s >= CHUNKS - 1:
                    dense_residual(s - 1)
                if s >= 2:
                    dve.wait_ge(normed[LN_OUTER], s - 1)
                    e_statistics(s - 2, lambda i: y_tm[0:TP, CT * (s - 2) + i, :])
                if 1 <= s < CHUNKS - 1:
                    dense_residual(s - 1)
                if s >= 4:
                    weigh_experts(s - 4, s - 4)
                if s >= 3:
                    rank_experts(s - 3)
                if s < LAYERS:
                    output_bias(s)

            def low_parts(l, g, e):
                u, par = units_before(l, g, e), e % 2
                dve.wait_ge(hhi_done, u + 1)
                V.tensor_tensor(h_lo[par], h32[par], h_hi[par], sub).then_inc(hlo_done, 1)

            def accumulate(l, g, e):
                u = units_before(l, g, e)
                dve.wait_ge(y_mm, u + 1)
                if e == 0:
                    dve.wait_ge(comb_ready, g + (CHUNKS * l + 1))
                    if l:
                        dve.wait_ge(y_saved, g + (CHUNKS * (l - 1) + 2))
                if e == EXPERTS - 1 and not (l == 0 and is_int(g, 0)):
                    dve.wait_ge(y_saved, CHUNKS * (LAYERS - 1) + 1 if l == LAYERS - 1 else g + (CHUNKS * l + 1))
                for i in range(CT):
                    if is_int(g):
                        yt, cs = y_tm[0:TP, CT * g + i, :], comb_s[0:TP, g, i, e:e + 1]
                    else:
                        yt = y_tm[0:TP, bass.ds(g * CT + i, 1), :].rearrange("p o c -> p (o c)")
                        cs = comb_s[0:TP, bass.ds(g, 1), i, e:e + 1].rearrange("p o c -> p (o c)")
                    last = V.scalar_tensor_tensor(out=yt if e < EXPERTS - 1 else y_grp[0:TP, i, :], in0=bank[4 + e % 2][0:TP, i * P:(i + 1) * P],
                                                  scalar=cs, in1=yt, op0=mul, op1=add)
                last.then_inc(acc_done, 1)
                dve.wait_ge(acc_done, u + 1)

            def finish(g):
                V.scalar_tensor_tensor(out=x_tm[0:TP, chunk(g), :], in0=y_grp[0:TP],
                                       scalar=gates[0:TP, 1:2], in1=x_tm[0:TP, chunk(g), :], op0=mul, op1=add).then_inc(out_ready, 1)

            def group(l, g):
                f = follower(l, g)
                start = l == 0 and is_int(g, 0)
                for e in range(EXPERTS):
                    if is_int(g, 0) and 0 < l < LAYERS - 1 and e == 3:
                        fold_b1(l + 1, 7)
                    if start and e == 2:
                        rank_experts(CHUNKS - 2)
                    if e == 3 and f is not None and not start:
                        rank_experts(f[0])
                    low_parts(l, g, e)
                    if start and e == 0:
                        outer_residual(CHUNKS - 1)
                        weigh_experts(CHUNKS - 3, CHUNKS - 3)
                    if start and e == 1:
                        split_xt(CHUNKS - 2, CHUNKS - 2)
                    if e == 2 and f is not None and not start or e == 3 and start:
                        split_xt(f[0], f[2])
                    if e:
                        accumulate(l, g, e - 1)
                    elif not start:
                        accumulate(l - 1 if is_int(g, 0) else l, CHUNKS - 1 if is_int(g, 0) else g - 1, EXPERTS - 1)
                        if f is None:
                            finish(g - 1)
                        else:
                            e_statistics(f[0], lambda i: y_grp[0:TP, i, :])
                    if start and e == 1:
                        fold_b1(1, 7)
                        dve.wait_ge(normed[LN_OUTER], CHUNKS)
                        e_statistics(CHUNKS - 1, lambda i: y_tm[0:TP, CT * (CHUNKS - 1) + i, :])
                    if start and e == 2:
                        weigh_experts(CHUNKS - 2, CHUNKS - 2)
                    if start and e == 3:
                        rank_experts(f[0])
                    if e == 3 and f is not None:
                        weigh_experts(f[0], f[2])

            expert_groups(dve, group)
            accumulate(LAYERS - 1, CHUNKS - 1, EXPERTS - 1)
            finish(CHUNKS - 1)

        @block.tensor
        def _(pe):
            def mm(dst, lhs, rhs, start=True, stop=True):
                return nc.tensor.matmul(dst, lhs, rhs, start=start, stop=stop)

            pe.wait_ge(fold_loaded, 16 * len(fold_loads))
            pe.wait_ge(consts_made, 8)
            mm(bank[3][:, 0:128], sa_wv_s, sa_wot_s)
            mm(bank[3][:, 128:256], sa_bv_s[:, 0:1].to_broadcast([P, P]), sa_wot_s)
            mm(bank[3][:, 256:257], wot_s, bv_s[:])
            mm(bank[3][:, 260:276], ones32[:], rw_s)
            for h in range(HEADS):
                last = mm(bank[3][:, 280 + h:281 + h], wk_s[:, h, :], bq_s[:, h:h + 1])
            last.then_inc(folds_mm, 1)

            def fold_heads(first_bank, a, b):
                for h in range(HEADS):
                    last = mm(bank[first_bank + h // 4][:, (h % 4) * P:(h % 4 + 1) * P], a[:, h, :], b[:, h, :])
                last.then_inc(folds_mm, 1)

            def to_features(c, src, bank_i, s):
                for i in range(CT):
                    last = nc.tensor.transpose(bank[bank_i][:, i * TP:(i + 1) * TP], src[0:TP, CT * c + i, :], ident[0:TP, 0:TP])
                last.then_inc(s, 1)

            def to_tokens(c, bank_i, s):
                for i in range(CT):
                    t = CT * c + i
                    last = nc.tensor.transpose(bank[bank_i][0:TP, i * P:(i + 1) * P], f_t[:, t * TP:(t + 1) * TP], ident[:])
                last.then_inc(s, 1)

            def fold_queries(c, h0, h1):
                for h in range(h0, h1):
                    k = c * HEADS + h
                    if k >= 4:
                        pe.wait_ge(q_lo_done, k - 3)
                    mm(bank[4 + k % 4][:, 0:CW], a_qk[:, h, :], f_t[:, c * CW:(c + 1) * CW]).then_inc(q_mm, 1)

            def queries(b, s, w0, w):
                if is_int(b):
                    return q_parts[:, b, s, w0:w0 + w]
                return q_parts[:, bass.ds(b, 1), s, w0:w0 + w].rearrange("p o w -> p (o w)")

            def maximum(b, par, j):
                if j == 0:
                    pe.wait_ge(thi_done, (b + 1) * NCH)
                if is_int(b, 0):
                    if j >= 2:
                        pe.wait_ge(max_read, j - 1)
                else:
                    pe.wait_ge(max_read, b * NCH + j)
                for r in range(TPS):
                    last = mm(max_scores(b, j)[:, r, :], queries(b, 0, j * PAIR, PAIR), t_hi[par][:, r * RW:(r + 1) * RW])
                last.then_inc(max_mm, 1)

            def fold_b1(l, bank_i, k0=0, k1=EXPERTS * FT):
                if k0 == 0:
                    pe.wait_ge(w1_loaded, 16 * (l + 1))
                    if l == 0:
                        pe.wait_ge(moe_loaded, 16)
                for k in range(k0, k1):
                    e, q = divmod(k, FT)
                    last = mm(bank[bank_i][:, 256 + k:257 + k], w1_raw[:, e, q * P:(q + 1) * P],
                              moe_b_s[:, EXPERTS * l + e:EXPERTS * l + e + 1])
                if k1 == EXPERTS * FT:
                    last.then_inc(b1_mm, 1)

            for s in range(CHUNKS + 2):
                if s < CHUNKS:
                    pe.wait_ge(normed[LN_IN], s + 1)
                    if s:
                        pe.wait_ge(y_tr_evac, s)
                    to_features(s, y_tm, 0, y_tr)
                if s == 0:
                    fold_heads(4, wq_s, wk_s)
                    pe.wait_ge(folds_done, 1)
                if s == 1:
                    fold_heads(6, wv_s, wo_s)
                if s >= 2:
                    if s == 2:
                        pe.wait_ge(heads_folded, 2)
                    pe.wait_ge(z_tr_evac, s - 1)
                    fold_queries(s - 2, 0, HEADS // 2)
                if s < CHUNKS:
                    pe.wait_ge(y_tr_evac, s + 1)
                    if s:
                        pe.wait_ge(sa_added, s)
                    for i in range(CT):
                        t = CT * s + i
                        last = mm(bank[1][0:TP, i * P:(i + 1) * P], f_t[:, t * TP:(t + 1) * TP], m_sa[:])
                    last.then_inc(sa_mm, 1)
                if s == CHUNKS + 1:
                    pe.wait_ge(z_tr_evac, CHUNKS)
                    maximum(0, 0, 0)
                if s >= 2:
                    fold_queries(s - 2, HEADS // 2, HEADS - 1)
                if 1 <= s <= CHUNKS:
                    pe.wait_ge(normed[LN_ONE], s)
                    if s > 1:
                        pe.wait_ge(z_tr_evac, s - 1)
                    to_features(s - 1, z_tm, 2, z_tr)
                if s >= 2:
                    fold_queries(s - 2, HEADS - 1, HEADS)

            pe.wait_ge(q_lo_done, CHUNKS * HEADS)
            for j, part in ((1, (0, 5)), (2, (5, 10)), (3, (10, 16))):
                maximum(0, 0, j)
                fold_b1(0, 6, *part)
            pe.wait_ge(b1_done, 1)

            def scores(b, par, j):
                if j == 0:
                    pe.wait_ge(tlo_done, (b + 1) * NCH)
                    pe.wait_ge(shift_ready, (b + 1) * NCH)
                for i in range(TPS):
                    t = TPS * j + i
                    dst = bank[3 + i][:, 0:QW]
                    keys = slice(t * KP, t * KP + P)
                    if not (is_int(b, 0) and j == 0):
                        pe.wait_ge(phi_done, b * KT + (t - TPS + 1))
                    mm(dst, t_hi[par][:, keys], queries(b, 0, 0, QW), True, False)
                    mm(dst, t_hi[par][:, keys], queries(b, 1, 0, QW), False, False)
                    mm(dst, t_lo[par][:, keys], queries(b, 0, 0, QW), False, False)
                    mm(dst, scale_h[0:PAIR, :], shift_d[par][0:PAIR, :], False, True).then_inc(score_mm, 1)

            def weighted(b, par, j):
                ring = j % 2
                pe.wait_ge(plo_done, b * NCH + (j + 1))
                if j == 0:
                    pe.wait_ge(nlo_done, b + 1)
                    if not is_int(b, 0):
                        pe.wait_ge(ctx_copied, b)
                for i in range(TPS):
                    t = TPS * j + i
                    hi, lo = p_hi[ring][0:KP, i, :], p_lo[ring][0:KP, i, :]
                    first, end = t == 0, t == KT - 1
                    mm(bank[6][:, 0:QW], n_hi[par][0:KP, t, :], hi, first, False)
                    mm(bank[6][:, 0:QW], n_hi[par][0:KP, t, :], lo, False, False)
                    last = mm(bank[6][:, 0:QW], n_lo[par][0:KP, t, :], hi, False, end)
                last.then_inc(pv_mm, 1)

            def probability_sums(b, par):
                pe.wait_ge(p_added, b * ADDS + ADDS)
                if not (is_int(b) and b < 1):
                    pe.wait_ge(sum_done, b)
                for j in range(NCH):
                    last = mm(bank[7][0:PAIR, QW + j:QW + j + 1], p_sum[par][0:KP, j * PAIR:(j + 1) * PAIR], ones32[0:KP, 0:1])
                last.then_inc(p_sum_mm, 1)

            def spread_inverses(b):
                pe.wait_ge(inv_diag_ready, b + 1)
                mm(bank[7][:, 0:QW], ones_w[0:PAIR, :], inv_diag[0:PAIR, 0, :], True, False)
                mm(bank[7][:, 0:QW], ones_w[0:PAIR, :], inv_diag[0:PAIR, 1, :], False, True).then_inc(inv_mm, 1)


            def sequence(b, par):
                for j in range(NCH):
                    if not is_int(b, B - 1):
                        maximum(b + 1, 1 - par, j)
                    if j == 2 and not is_int(b, 0):
                        spread_inverses(b - 1)
                    scores(b, par, j)
                    if not (is_int(b, 0) and j == 0):
                        weighted(*before(b, par, j))
                    if j == 0 and not is_int(b, 0):
                        probability_sums(b - 1, 1 - par)

            seq_pairs(pe, sequence)
            def project(c, h0, h1):
                if h0 == 0:
                    pe.wait_ge(sum_done, (c + 1) * CB)
                    if c:
                        pe.wait_ge(ca_added, c)
                for h in range(h0, h1):
                    last = mm(bank[0][:, 0:CW], a_vo[:, h, :], ctx_sum[:, c * CB:(c + 1) * CB, h, :], h == 0, h == HEADS - 1)
                if h1 == HEADS:
                    last.then_inc(ca_mm, 1)

            pe.wait_ge(max_read, B * NCH)
            project(0, 0, HEADS // 2)
            weighted(B - 1, 1, NCH - 1)
            probability_sums(B - 1, 1)
            project(0, HEADS // 2, HEADS)
            spread_inverses(B - 1)

            def transposes_e(m, g):
                pe.wait_ge(e_normed, m + 1)
                if not is_int(m, 0):
                    pe.wait_ge(xtlo_done, m)
                for i in range(CT):
                    last = nc.tensor.transpose(bank[6][:, i * TP:(i + 1) * TP], z_grp[0:TP, i, :], ident[0:TP, 0:TP])
                last.then_inc(xt_mm, 1)

            def logits(m, l, g):
                pe.wait_ge(xtlo_done, m + 1)
                if not is_int(m, 0):
                    pe.wait_ge(lg_ready, m)
                cols = slice(EXPERTS * l, EXPERTS * (l + 1))
                for i in range(CT):
                    dst = bank[7][0:TP, i * EXPERTS:(i + 1) * EXPERTS]
                    hi, lo = (v[:, bass.ds(g * CW + i * TP, TP)] for v in (xt_hi, xt_lo))
                    mm(dst, hi, rw_hi[:, cols], True, False)
                    mm(dst, hi, rw_lo[:, cols], False, False)
                    last = mm(dst, lo, rw_hi[:, cols], False, True)
                last.then_inc(logit_mm, 1)

            for s in range(CHUNKS + 1):
                if s >= 1:
                    pe.wait_ge(normed[LN_TWO], s)
                    if s > 1:
                        pe.wait_ge(ff2_added, s - 1)
                    to_features(s - 1, z_tm, 2, x2_tr)
                if 1 <= s < CHUNKS:
                    project(s, HEADS // 2, HEADS)
                if s >= 1:
                    pe.wait_ge(x2_tr_evac, s)
                    for q in range(FT):
                        k = (s - 1) * FT + q
                        if k >= 2:
                            pe.wait_ge(ff1_act, k - 1)
                        mm(bank[3 + k % 2][:, 0:CW], l1_s[:, q * P:(q + 1) * P], f_t[:, (s - 1) * CW:s * CW]).then_inc(ff1_mm, 1)
                if s < CHUNKS:
                    pe.wait_ge(ca_added, s + 1)
                    if s:
                        pe.wait_ge(normed[LN_TWO], s)
                    to_tokens(s, 1, ca_back)
                if s >= 3:
                    transposes_e(s - 3, s - 3)
                if s >= 1:
                    pe.wait_ge(ff1_act, s * FT)
                    for q in range(FT):
                        last = mm(bank[2][:, 0:CW], l2_s[:, q, :], ffh[s - 1][:, q, :], q == 0, q == FT - 1)
                    last.then_inc(ff2_mm, 1)
                if s < CHUNKS - 1:
                    project(s + 1, 0, HEADS // 2)
                if s >= 1:
                    pe.wait_ge(ff2_added, s)
                    if s > 1:
                        pe.wait_ge(normed[LN_THREE], s - 1)
                    to_tokens(s - 1, 5, ff_back)
                if s >= 3:
                    logits(s - 3, 0, s - 3)

            def hidden(l, g, e):
                u, s = units_before(l, g, e), l % 2
                if is_int(g, 0):
                    pe.wait_ge(w_split, 2 * EXPERTS * l + (e + 1 if l else EXPERTS + e + 1))
                toks = bass.ds(g * CW, CW)
                for q in range(FT):
                    if not (is_int(u, 0)):
                        pe.wait_ge(gelu_done, u * FT + (q - FT + 1))
                    dst, w = bank[q][:, 0:CW], slice(e * FF + q * P, e * FF + (q + 1) * P)
                    mm(dst, w1_hi[s][:, w], xt_hi[:, toks], True, False)
                    mm(dst, w1_hi[s][:, w], xt_lo[:, toks], False, False)
                    mm(dst, w1_lo[s][:, w], xt_hi[:, toks], False, True).then_inc(hid_mm, 1)

            def output(l, g, e):
                u, s, par = units_before(l, g, e), l % 2, e % 2
                if is_int(g, 0) and l:
                    pe.wait_ge(w_split, 2 * EXPERTS * l + (EXPERTS + e + 1))
                pe.wait_ge(hlo_done, u + 1)
                if not (is_int(u) and u < 2):
                    pe.wait_ge(acc_done, u - 1)
                for i in range(CT):
                    dst, toks = bank[4 + par][0:TP, i * P:(i + 1) * P], slice(i * TP, (i + 1) * TP)
                    mm(dst, ones_h[0:BR + 1, :], b2_parts[l][0:BR + 1, e * P:(e + 1) * P], True, False)
                    for q in range(FT):
                        w = slice((e * FT + q) * P, (e * FT + q + 1) * P)
                        mm(dst, h_hi[par][:, q, toks], w2_hi[s][:, w], False, False)
                        mm(dst, h_hi[par][:, q, toks], w2_lo[s][:, w], False, False)
                        last = mm(dst, h_lo[par][:, q, toks], w2_hi[s][:, w], False, q == FT - 1)
                last.then_inc(y_mm, 1)

            B1_PARTS = ({0: (0, 8), 1: (8, 16)}, {0: (0, 5), 1: (5, 10), 2: (10, 16)})

            def group(l, g):
                f = follower(l, g)
                start = l == 0 and is_int(g, 0)
                for e in range(EXPERTS):
                    if e == 3 and f is not None and not start:
                        transposes_e(f[0], f[2])
                    hidden(l, g, e)
                    if start and e == 1:
                        transposes_e(CHUNKS - 2, CHUNKS - 2)
                    if is_int(g, 0) and l < LAYERS - 1 and e == (3 if l else 2):
                        pe.wait_ge(b1_done, l + 2)
                    if start and e == 2:
                        logits(CHUNKS - 2, 0, CHUNKS - 2)
                    if start and e == 3:
                        transposes_e(f[0], f[2])
                    if e == 3 and f is not None and not start:
                        logits(*f)
                    if start and e == 1:
                        pe.wait_ge(b2_ready, LAYERS)
                    if start and e == 2:
                        pe.wait_ge(normed[LN_THREE], CHUNKS)
                    if e:
                        output(l, g, e - 1)
                    elif not start:
                        output(l - 1 if is_int(g, 0) else l, CHUNKS - 1 if is_int(g, 0) else g - 1, EXPERTS - 1)
                    if start and e == 3:
                        logits(*f)
                    if is_int(g, 0) and l < LAYERS - 1 and e in B1_PARTS[l > 0]:
                        if e == 0:
                            pe.wait_ge(lg_ready, CHUNKS * l + CHUNKS - 1 if l else CHUNKS - 2)
                        fold_b1(l + 1, 7, *B1_PARTS[l > 0][e])

            expert_groups(pe, group)
            output(LAYERS - 1, CHUNKS - 1, EXPERTS - 1)


_OUT = (B, NQ, C)


def kernel(**inputs):
    import numpy as _np
    import concourse.bacc as _bacc
    from concourse import mybir as _mybir
    from concourse.bass_utils import run_bass_kernel_spmd as _run

    a = {k: _np.asarray(v) for k, v in inputs.items()}
    qkv_w, qkv_b = a["L0_xattn_qkv_w"], a["L0_xattn_qkv_b"]
    in_w, in_b = a["L0_xattn_in_proj_w"], a["L0_xattn_in_proj_b"]
    ctx, out_w = a["ctx_1024"], a["L0_xattn_mha_out_w"]

    def heads_first(w):
        return w.reshape(HEADS, HD, P).transpose(1, 0, 2)

    layout = {
        "x": a["x"].reshape(TOK, C),
        "ctx_n": ctx.reshape(B, KP, KT * C),
        "ctx_t": ctx.reshape(B, KP, KT, C).transpose(0, 3, 2, 1).reshape(B, C, NKEY),
        "squares": _np.stack([qkv_w[2 * C:3 * C], a["L0_xattn_sa_out_w"].T, out_w.T], 1),
        "columns": _np.concatenate([_np.stack([
            qkv_b[2 * C:3 * C], in_b[2 * C:3 * C], a["L0_xattn_mha_out_b"], a["L0_xattn_lin2_b"],
            a["L0_xattn_ln1_g"], a["L0_xattn_ln1_b"], a["L0_xattn_ln2_g"], a["L0_xattn_ln2_b"]], 1),
            a["L0_xattn_lin1_b"].reshape(FT, P).T,
            a["L0_ffn_router_w"].transpose(1, 0, 2).reshape(C, LAYERS * EXPERTS)], 1),
        "per_head": _np.concatenate(
            [heads_first(w).reshape(HD, HEADS * P) for w in (in_w[0:C], in_w[C:2 * C], in_w[2 * C:3 * C], out_w.T)]
            + [in_b[0:C].reshape(HEADS, HD).T], 1),
        "rows": _np.concatenate([a["L0_xattn_sa_out_b"], a["L0_xattn_ln3_g"], a["L0_xattn_ln3_b"],
                                 a["L0_ffn_router_b"].reshape(-1), a["g_xattn"], a["g_ffn"]]).reshape(1, ROWS),
        "dense": _np.concatenate([a["L0_xattn_lin1_w"].T, a["L0_xattn_lin2_w"].T.reshape(FT, P, C).transpose(1, 0, 2).reshape(P, FF)], 1),
        "moe_columns": _np.concatenate([
            a["L0_ffn_ln_g"].reshape(LAYERS * EXPERTS, C).T, a["L0_ffn_ln_b"].reshape(LAYERS * EXPERTS, C).T,
            a["L0_ffn_b1"].reshape(LAYERS * EXPERTS * FT, P).T], 1),
        "w1": a["L0_ffn_w1"].transpose(0, 2, 1, 3),
        "w2": a["L0_ffn_w2"].reshape(LAYERS, EXPERTS * FT, P, C).transpose(0, 2, 1, 3),
        "b2": a["L0_ffn_b2"].reshape(LAYERS, EXPERTS * C),
    }
    nc = _bacc.Bacc("TRN2", target_bir_lowering=False, num_devices=1)
    arrays, args = {}, []
    for name, v in layout.items():
        v = _np.ascontiguousarray(v)
        arrays[f"in_{name}"] = v
        args.append(nc.dram_tensor(f"in_{name}", v.shape, _mybir.dt.from_np(v.dtype), kind="ExternalInput").ap())
    args.append(nc.dram_tensor("out", (TOK, C), _mybir.dt.float32, kind="ExternalOutput").ap())
    flamingo_block(nc, *args)
    r = _run(nc, [arrays], core_ids=[0])
    return _np.asarray(r.results[0]["out"]).reshape(_OUT)
```
